# Optimizing a Trainium2 kernel written in Bass

```python
import numpy as np
import jax
import jax.numpy as jnp

def _softmax(x, axis=-1):
    return jax.nn.softmax(x, axis=axis)

def _gelu(x):
    return jax.nn.gelu(x, approximate=True)

def _silu(x):
    return jax.nn.silu(x)

def _sigmoid(x):
    return jax.nn.sigmoid(x)

def _layernorm(x, axis=-1, eps=1e-05):
    m = jnp.mean(x, axis=axis, keepdims=True)
    v = jnp.var(x, axis=axis, keepdims=True)
    return (x - m) / jnp.sqrt(v + eps)

def _scatter_add(tgt, idx, src, axis=0):
    return tgt.at[idx].add(src)

def _segment_sum(src, seg, n):
    return jax.ops.segment_sum(src, seg, n)
kernel_name = 'mk_seq_postln_d1_jaxref_r8_b1ae79'

def setup_inputs(seed: int=0):
    np.random.seed(seed)
    _w = jnp.asarray

    def _L0_attn_setup():
        import jax, jax.numpy as jnp
        import numpy as np
        D_MODEL = 256
        N_HEAD = 16
        HEAD_DIM = D_MODEL // N_HEAD
        SCALE = 1.0 / HEAD_DIM ** 0.5
        key = jax.random.key(seed)
        kx, kq, kk, kv, ko = jax.random.split(key, 5)
        std = 1.0 / np.sqrt(D_MODEL)
        return {'x': jax.random.normal(kx, (2, 256, D_MODEL), dtype=jnp.float32), 'w_q': jax.random.normal(kq, (D_MODEL, D_MODEL), dtype=jnp.float32) * std, 'w_k': jax.random.normal(kk, (D_MODEL, D_MODEL), dtype=jnp.float32) * std, 'w_v': jax.random.normal(kv, (D_MODEL, D_MODEL), dtype=jnp.float32) * std, 'w_o': jax.random.normal(ko, (D_MODEL, D_MODEL), dtype=jnp.float32) * std}
    _L0_attn_in = _L0_attn_setup()

    def _L0_ffn_setup():
        import math
        import jax, jax.numpy as jnp
        import numpy as np
        NUM_EXPERTS = 8
        TOP_K = 2
        CAP_FACTOR = 1.25
        D_MODEL = 256
        D_HIDDEN = 1024
        B, S = (4, 256)
        key = jax.random.key(seed)
        ks = jax.random.split(key, 6)
        x = jax.random.normal(ks[0], (B, S, D_MODEL), dtype=jnp.float32)
        gating_w = jax.random.normal(ks[1], (D_MODEL, NUM_EXPERTS), dtype=jnp.float32) * (1.0 / math.sqrt(D_MODEL))
        w1 = jax.random.normal(ks[2], (NUM_EXPERTS, D_MODEL, D_HIDDEN), dtype=jnp.float32) * (1.0 / math.sqrt(D_MODEL))
        b1 = jnp.zeros((NUM_EXPERTS, D_HIDDEN), dtype=jnp.float32)
        w2 = jax.random.normal(ks[3], (NUM_EXPERTS, D_HIDDEN, D_MODEL), dtype=jnp.float32) * (1.0 / math.sqrt(D_HIDDEN))
        b2 = jnp.zeros((NUM_EXPERTS, D_MODEL), dtype=jnp.float32)
        return {'x': x, 'gating_w': gating_w, 'w1': w1, 'b1': b1, 'w2': w2, 'b2': b2}
    _L0_ffn_in = _L0_ffn_setup()
    _d = {'L0_attn_x': _L0_attn_in['x'], 'L0_attn_w_q': _L0_attn_in['w_q'], 'L0_attn_w_k': _L0_attn_in['w_k'], 'L0_attn_w_v': _L0_attn_in['w_v'], 'L0_attn_w_o': _L0_attn_in['w_o'], 'L0_ffn_gating_w': _L0_ffn_in['gating_w'], 'L0_ffn_w1': _L0_ffn_in['w1'], 'L0_ffn_b1': _L0_ffn_in['b1'], 'L0_ffn_w2': _L0_ffn_in['w2'], 'L0_ffn_b2': _L0_ffn_in['b2']}
    _x0 = _d['L0_attn_x']
    _d['L0_attn_x'] = jax.random.normal(jax.random.fold_in(jax.random.key(seed), 1), (16, 256, 256), dtype=_x0.dtype)
    del _x0
    return _d

def reference(L0_attn_x, L0_attn_w_q, L0_attn_w_k, L0_attn_w_v, L0_attn_w_o, L0_ffn_gating_w, L0_ffn_w1, L0_ffn_b1, L0_ffn_w2, L0_ffn_b2):

    def _L0_attn_ref(x, w_q, w_k, w_v, w_o):
        import jax, jax.numpy as jnp
        import numpy as np
        D_MODEL = 256
        N_HEAD = 16
        HEAD_DIM = D_MODEL // N_HEAD
        SCALE = 1.0 / HEAD_DIM ** 0.5
        b, s, d = x.shape

        def proj(w):
            y = jnp.einsum('bsd,ed->bse', x, w)
            return y.reshape(b, s, N_HEAD, HEAD_DIM).transpose(0, 2, 1, 3)
        q, k, v = (proj(w_q), proj(w_k), proj(w_v))
        scores = jnp.einsum('bhqd,bhkd->bhqk', q, k) * SCALE
        probs = jax.nn.softmax(scores, axis=-1)
        attn = jnp.einsum('bhqk,bhkd->bhqd', probs, v)
        attn = attn.transpose(0, 2, 1, 3).reshape(b, s, d)
        return jnp.einsum('bsd,ed->bse', attn, w_o)

    def _L0_ffn_ref(x, gating_w, w1, b1, w2, b2):
        import math
        import jax, jax.numpy as jnp
        import numpy as np
        NUM_EXPERTS = 8
        TOP_K = 2
        CAP_FACTOR = 1.25
        D_MODEL = 256
        D_HIDDEN = 1024
        B, S = (4, 256)
        b, s, d = x.shape
        x_flat = x.reshape(-1, d)
        T = x_flat.shape[0]
        num_items = T * TOP_K
        capacity = int(math.ceil(num_items / NUM_EXPERTS * CAP_FACTOR))
        gates = jax.nn.softmax(x_flat @ gating_w, axis=-1)
        topk_w, topk_idx = jax.lax.top_k(gates, TOP_K)
        norm_w = topk_w / (jnp.sum(topk_w, axis=-1, keepdims=True) + 1e-08)
        flat_e = topk_idx.reshape(-1)
        flat_t = jnp.repeat(jnp.arange(T, dtype=jnp.int32), TOP_K)
        flat_w = norm_w.reshape(-1)
        onehot = (flat_e[:, None] == jnp.arange(NUM_EXPERTS)[None, :]).astype(jnp.int32)
        pos_all = jnp.cumsum(onehot, axis=0) - 1
        position = jnp.take_along_axis(pos_all, flat_e[:, None].astype(jnp.int32), axis=1)[:, 0]
        valid = position < capacity
        pos_scatter = jnp.where(valid, position, capacity)
        buf = jnp.zeros((NUM_EXPERTS, capacity, d), dtype=x.dtype)
        buf = buf.at[flat_e, pos_scatter].set(x_flat[flat_t], mode='drop')
        h = jnp.maximum(jnp.einsum('ecd,edh->ech', buf, w1) + b1[:, None, :], 0.0)
        out_e = jnp.einsum('ech,ehd->ecd', h, w2) + b2[:, None, :]
        pos_gather = jnp.minimum(position, capacity - 1)
        gathered = out_e[flat_e, pos_gather]
        w_eff = jnp.where(valid, flat_w, 0.0)
        out_flat = jnp.zeros_like(x_flat).at[flat_t].add(gathered * w_eff[:, None])
        return out_flat.reshape(b, s, d)
    x = L0_attn_x
    x = _layernorm(x + _L0_attn_ref(x, L0_attn_w_q, L0_attn_w_k, L0_attn_w_v, L0_attn_w_o), axis=-1)
    x = _layernorm(x + _L0_ffn_ref(x, L0_ffn_gating_w, L0_ffn_w1, L0_ffn_b1, L0_ffn_w2, L0_ffn_b2), axis=-1)
    return x

_drawn_inputs = setup_inputs


def setup_inputs(seed=0):
    import zlib

    import numpy as np

    out = dict(_drawn_inputs(seed))
    spreads = {'L0_ffn_b1': (0.0, 0.1), 'L0_ffn_b2': (0.0, 0.1)}
    factors = {}
    for name, (base, spread) in spreads.items():
        noise = np.random.default_rng([zlib.crc32(name.encode()), seed]).standard_normal(out[name].shape)
        drawn = base * np.exp(spread * noise) if base else spread * noise
        out[name] = jnp.asarray(drawn.astype(out[name].dtype))
    for name, factor in factors.items():
        out[name] = (out[name] * factor).astype(out[name].dtype)
    return out
```

```python
from contextlib import ExitStack

import concourse.bass as bass
from concourse import mybir

F32 = mybir.dt.float32
F32R = mybir.dt.float32r
BF16 = mybir.dt.bfloat16
I32 = mybir.dt.int32
U32 = mybir.dt.uint32
ALU = mybir.AluOpType
ACT = mybir.ActivationFunctionType
X = mybir.AxisListType.X

P = 128
EPS = 1e-5
ROW_B, ROW_C, ROW_M, STACK = 16, 64, 96, 98
RING = 8
HBUF = (0, 1, 0, 1, 2)


def wait_apart(engine, passed, *waits):
    for semaphore, value in waits:
        engine.wait_ge(semaphore, value)
    engine.sem_inc(passed, 1)


class Seq:

    def __init__(self, i, off):
        self.n = 2 * i + off
        self.parity = off % 2
        self.half = i + off // 2


def build(nc, x_d, wq_d, wk_d, wv_d, wo_d, gw_d, w1_d, b1_d, w2_d, b2_d, out_d):
    NB, S, D = x_d.shape
    T = NB * S
    R = 16
    H = D // R
    NE, _, FF = w1_d.shape
    TOPK = 2
    CAP = -(-(T * TOPK * 5) // (NE * 4))
    SCALE = R ** -0.5
    QC = S // P
    DK = D // P
    HH = P // R
    FT = FF // P
    BLK = CAP // P
    NC = BLK // QC
    C = QC * P
    TRASH = P

    x1_d = nc.dram_tensor("x1_rows", (T + TRASH, D), F32, kind="Internal").ap()
    acc_d = nc.dram_tensor("acc_rows", (T + TRASH, D), F32, kind="Internal").ap()
    list_d = nc.dram_tensor("slot_list", (NE * CAP, 2), I32, kind="Internal").ap()

    x_v = x_d.rearrange("b (c p) d -> b p c d", p=P)
    x1_v = x1_d[0:T, :].rearrange("(b c p) d -> b p c d", p=P, c=QC)
    acc_v = acc_d[0:T, :].rearrange("(b c p) d -> b p c d", p=P, c=QC)
    list_v = list_d.rearrange("(e p j) w -> p e (j w)", e=NE, p=P)

    top = ExitStack()

    def sem(name, ctx=top):
        return ctx.enter_context(nc.semaphore(name))

    def sb(name, shape, dt=F32, ctx=top):
        return ctx.enter_context(nc.sbuf_tensor(name, shape, dt))

    with top:
        banks = [top.enter_context(nc.psum_tensor(f"bank{i}", [P, 512], F32)) for i in range(8)]
        ident = sb("ident", [P, P])
        b1T = sb("b1T", [P, NE * FT])
        w1_raw = sb("w1_raw", [P, DK, FF])
        w2_raw = sb("w2_raw", [P, FT, D])
        expo = sb("expo", [P, QC])
        w1_loaded, w2_loaded, b2_loaded = sem("w1_loaded"), sem("w2_loaded"), sem("b2_loaded")

        attention(nc, locals())
        experts(nc, locals())
        last_norm(nc, locals())


def attention(nc, g):
    (x_v, x1_v, acc_v, list_v, x1_d, acc_d, list_d) = (
        g["x_v"], g["x1_v"], g["acc_v"], g["list_v"], g["x1_d"], g["acc_d"], g["list_d"])
    NB, S, D, T, R, H = g["NB"], g["S"], g["D"], g["T"], g["R"], g["H"]
    QC, DK, HH, NE, FT, CAP, BLK = g["QC"], g["DK"], g["HH"], g["NE"], g["FT"], g["CAP"], g["BLK"]
    SCALE, TRASH, TOPK = g["SCALE"], g["TRASH"], g["TOPK"]
    banks, ident, b1T, expo = g["banks"], g["ident"], g["b1T"], g["expo"]
    G = H // HH
    QUADS = H // 4
    ctx = ExitStack()
    with ctx:
        def sem(name):
            return ctx.enter_context(nc.semaphore(name))

        def sb(name, shape, dt=F32):
            return ctx.enter_context(nc.sbuf_tensor(name, shape, dt))

        tri = sb("tri", [P, P], BF16)
        ones = sb("ones", [P, P], BF16)
        w_raw = sb("w_raw", [P, 4, DK, D])
        wT_hi = sb("wT_hi", [P, 4, DK, D], F32R)
        wT_lo = sb("wT_lo", [P, 4, DK, D], F32R)
        b1_raw = sb("b1_raw", [NE * FT, P])
        gate_w = sb("gate_w", [P, DK, NE])
        iota_e = sb("iota_e", [P, NE])
        slot0 = sb("slot0", [P, NE])
        fill = sb("fill", [P, NE, BLK, 2], I32)
        zrow = sb("zrow", [P, D])
        tok = sb("tok", [P, QC])
        x_sb = [sb(f"x_sb{i}", [P, QC, D]) for i in range(2)]
        xres = [sb(f"xres{i}", [P, QC, D]) for i in range(2)]
        xT_hi = sb("xT_hi", [P, DK, S], F32R)
        xT_lo = sb("xT_lo", [P, DK, S], F32R)
        qk = [sb(f"qk{i}", [P, 2, G, 2, S], F32R) for i in range(2)]
        stack = [sb(f"stack{i}", [STACK, H, 2, S], F32R) for i in range(2)]
        v_aug = [sb(f"v_aug{i}", [P, QC, H, 32]) for i in range(2)]
        negm = sb("negm", [P, QC, H])
        mT_hi = [sb(f"mT_hi{i}", [HH, S], F32R) for i in range(2)]
        mT_lo = [sb(f"mT_lo{i}", [HH, S], F32R) for i in range(2)]
        probs = sb("probs", [P, RING, QC, S])
        u_sb = sb("u_sb", [P, QUADS, S])
        rec = sb("rec", [P, QC, H])
        attn = sb("attn", [P, QC, D])
        aT_hi = sb("aT_hi", [P, DK, S], F32R)
        aT_lo = sb("aT_lo", [P, DK, S], F32R)
        y = sb("y", [P, QC, D])
        stats = sb("stats", [P, QC, 6])
        mv = sb("mv", [P, QC, 2])
        veps = sb("veps", [P, QC])
        rstd = sb("rstd", [P, QC])
        x1 = sb("x1", [P, QC, D])
        x1T = sb("x1T", [P, DK, S])
        lg = sb("lg", [P, QC, NE])
        mx = sb("mx", [P, QC, NE])
        ix = sb("ix", [P, QC, NE], U32)
        ixf = sb("ixf", [P, QC, TOPK])
        hot = sb("hot", [P, QC, TOPK, NE])
        mask = sb("mask", [P, QC, NE], BF16)
        seen = [sb(f"seen{i}", [P, NE], BF16) for i in range(2)]
        seen_t = sb("seen_t", [P, NE], BF16)
        dmx = sb("dmx", [P, QC, NE])
        ex = sb("ex", [P, QC, NE])
        zsum = sb("zsum", [P, QC])
        den = sb("den", [P, QC])
        den2 = sb("den2", [P, QC])
        over = sb("over", [P, QC, NE])
        slot = sb("slot", [P, QC, NE])
        slot_b = sb("slot_b", [P, QC, NE])
        pick = sb("pick", [P, QC, TOPK, NE])
        dest_f = sb("dest_f", [P, QC, TOPK])
        dest = [sb(f"dest{i}", [P, QC * TOPK], I32) for i in range(2)]
        item = [sb(f"item{i}", [P, QC * TOPK, 2], I32) for i in range(2)]

        consts_ready, zeros_ready, filled = sem("consts_ready"), sem("zeros_ready"), sem("filled")
        ident0, w_loaded, wT_ready, wT_hi_done = sem("ident0"), sem("w_loaded"), sem("wT_ready"), sem("wT_hi_done")
        wT_lo_done, small_loaded, b1T_ready, b1T_done = sem("wT_lo_done"), sem("small_loaded"), sem("b1T_ready"), sem("b1T_done")
        x_loaded = [sem(f"x_loaded{i}") for i in range(2)]
        xres_loaded = [sem(f"xres_loaded{i}") for i in range(2)]
        xT_ready, xT_hi_done, xT_lo_done = sem("xT_ready"), sem("xT_hi_done"), sem("xT_lo_done")
        q_ready, k_ready, v_ready, v_done = sem("q_ready"), sem("k_ready"), sem("v_ready"), sem("v_done")
        qk_ready = (q_ready, k_ready)
        qk_hi_done = (sem("q_hi_done"), sem("k_hi_done"))
        qk_lo_done = (sem("q_lo_done"), sem("k_lo_done"))
        stacked = [sem(f"stacked{i}") for i in range(2)]
        s_ready, max_done = sem("s_ready"), sem("max_done")
        mT_ready, mT_hi_done, mT_lo_done = ([sem(f"{n}{i}") for i in range(2)] for n in ("mT_ready", "mT_hi_done", "mT_lo_done"))
        shift_in = [sem(f"shift_in{i}") for i in range(2)]
        st_ready, exp_done = sem("st_ready"), sem("exp_done")
        pv_ready, u_done = sem("pv_ready"), sem("u_done")
        uT_ready, rec_done, attn_done = sem("uT_ready"), sem("rec_done"), sem("attn_done")
        aT_ready, aT_hi_done, aT_lo_done = sem("aT_ready"), sem("aT_hi_done"), sem("aT_lo_done")
        o_ready, y_done, stats_done, mv_done = sem("o_ready"), sem("y_done"), sem("stats_done"), sem("mv_done")
        veps_done, rstd_done, x1_done = sem("veps_done"), sem("rstd_done"), sem("x1_done")
        x1_stored = [sem(f"x1_stored{i}") for i in range(2)]
        x1T_ready, x1T_done, lg_ready, lg_done = sem("x1T_ready"), sem("x1T_done"), sem("lg_ready"), sem("lg_done")
        mx_done, ix_done, ixf_done, hot_done = sem("mx_done"), sem("ix_done"), sem("ixf_done"), sem("hot_done")
        mask_done, seen_mid, seen_done, pos_ready = sem("mask_done"), sem("seen_mid"), sem("seen_done"), sem("pos_ready")
        dmx_done, ex_done, zsum_done, den_done = sem("dmx_done"), sem("ex_done"), sem("zsum_done"), sem("den_done")
        den2_done, w0_done, item_done, tok_done = sem("den2_done"), sem("w0_done"), sem("item_done"), sem("tok_done")
        over_done, slot_done, slotb_done, pick_done = sem("over_done"), sem("slot_done"), sem("slotb_done"), sem("pick_done")
        destf_done, dest_done = sem("destf_done"), sem("dest_done")
        keys_cleared, keys_ready = sem("keys_cleared"), sem("keys_ready")
        sp_passed, pool_passed, dve_passed = sem("sp_passed"), sem("pool_passed"), sem("dve_passed")
        listed = [sem(f"listed{i}") for i in range(2)]

        BQ, BD, BU, BA, BB, BC = (0, 1), (2, 3), 4, 5, 6, 7

        def bank(i, **kw):
            return banks[i][:, :].rearrange("p (a b) -> p a b", **kw)

        def from_bank(w, c):
            t = banks[4 + w][:, c * D:c * D + D]
            return t.rearrange("p (x h r) -> p x h r", h=HH // 2, r=R) if w < 2 else t

        def by_feature(t, w, c):
            return t[:, w, c].rearrange("p (x r h) -> p x h r", h=HH // 2, r=R) if w < 2 else t[:, w, c]

        block = ctx.enter_context(nc.Block())

        first, last = -1, NB + 1

        def pipeline(engine, step):
            lo, hi = 2, (NB - 2) // 2
            for s in range(first, 2 * lo):
                step(Seq(0, s), s)
            with engine.Fori(lo, hi) as i:
                for j in range(2):
                    step(Seq(i, j), None)
            for s in range(2 * hi, last + 1):
                step(Seq(s // 2, s % 2), s)

        def stage(s, num, lag):
            if num is not None:
                n = num - lag
                return Seq(n // 2, n % 2) if 0 <= n < NB else None
            return Seq(s.half, s.parity - lag)

        @block.sync
        def _(sp):
            for w, name in enumerate(("wq_d", "wk_d", "wv_d", "wo_d")):
                sp.dma_start(w_raw[:, w], g[name].rearrange("(c p) d -> p c d", p=P)).then_inc(w_loaded, 16)
            sp.dma_start(x_sb[0][:, :, :], x_v[0]).then_inc(x_loaded[0], 16)
            sp.dma_start(b1_raw[:, :], g["b1_d"].rearrange("e (f p) -> (e f) p", p=P)).then_inc(small_loaded, 16)
            sp.dma_start(gate_w[:, :, :], g["gw_d"].rearrange("(c p) e -> p c e", p=P)).then_inc(small_loaded, 16)
            sp.wait_ge(zeros_ready, 2)
            sp.dma_start(list_v, fill[:, :, :, :].rearrange("p e j w -> p e (j w)")).then_inc(filled, 16)
            sp.dma_start(x1_d[T:T + TRASH, :], zrow[:, :]).then_inc(filled, 16)
            sp.dma_start(acc_d[T:T + TRASH, :], zrow[:, :]).then_inc(filled, 16)
            sp.dma_start(g["w1_raw"][:, :, :], g["w1_d"][0].rearrange("(c p) f -> p c f", p=P)).then_inc(g["w1_loaded"], 16)
            sp.dma_start(g["w2_raw"][:, :, :], g["w2_d"][0].rearrange("(f p) d -> p f d", p=P)).then_inc(g["w2_loaded"], 16)

            def shift_rows(b, half):
                sp.wait_ge(mT_hi_done[half], b.n + 1)
                sp.wait_ge(mT_lo_done[half], b.n + 1)
                heads = slice(HH * half, HH * (half + 1))
                for row, src in ((ROW_M, mT_hi[half]), (ROW_M + 1, mT_lo[half])):
                    sp.dma_start(stack[b.parity][row:row + 1, heads, 0, :].bitcast(F32), src[:, :].bitcast(F32)).then_inc(shift_in[half], 16)

            def stack_rows(a, half):
                src = qk[a.parity][P // 2 * half:P // 2 * (half + 1)].bitcast(F32)
                dst = stack[a.parity][:, HH * half:HH * (half + 1)].bitcast(F32)
                pair = src.rearrange("p c g w t -> p c (g w t)")
                both = dst.rearrange("r h w t -> r (h w t)")
                for out, in_ in ((dst[0:R, :, 0, :], src[:, 1, :, 0, :]), (dst[0:R, :, 1, :], src[:, 0, :, 1, :]),
                                 (both[ROW_B:ROW_B + R], pair[:, 0, :]), (both[ROW_C:ROW_C + R], pair[:, 1, :])):
                    sp.dma_start(out, in_).then_inc(stacked[half], 16)

            def step(s, num):
                a, b, d, e = (stage(s, num, lag) for lag in (-1, 0, 1, 2))
                nxt = stage(s, num, -2)
                if nxt:
                    if num is None or num >= 0:
                        sp.wait_ge(xT_ready, nxt.n - 1)
                    sp.dma_start(x_sb[nxt.parity][:, :, :], x_v[nxt.n]).then_inc(x_loaded[nxt.parity], 16)
                if e:
                    if num is None or num >= 4:
                        sp.wait_ge(y_done, e.n - 1)
                    sp.dma_start(xres[e.parity][:, :, :], x_v[e.n]).then_inc(xres_loaded[e.parity], 16)
                if d:
                    shift_rows(d, 1)
                if a:
                    if num == -1:
                        sp.wait_ge(keys_ready, 2)
                        sp.wait_ge(consts_ready, POOL_CONSTS)
                    for w in range(2):
                        sp.wait_ge(qk_hi_done[w], a.n + 1)
                        sp.wait_ge(qk_lo_done[w], a.n + 1)
                for half in range(2):
                    if a:
                        if b:
                            wait_apart(sp, sp_passed, (s_ready, H * b.n + HH * half + 1))
                        if num is None or num >= 1:
                            wait_apart(sp, sp_passed, (st_ready, H * (a.n - 2) + HH * (half + 1)))
                        stack_rows(a, half)
                    if half == 0 and b:
                        shift_rows(b, 0)
                    if half == 0 and e:
                        sp.wait_ge(x1_done, e.n + 1)
                        sp.dma_start(x1_v[e.n], x1[:, :, :]).then_inc(x1_stored[e.parity], 16)
                        sp.dma_start(acc_v[e.n], x1[:, :, :]).then_inc(x1_stored[e.parity], 16)

            pipeline(sp, step)
            for i in range(2):
                sp.wait_ge(x1_stored[i], 32 * (NB // 2))
                sp.wait_ge(listed[i], 16 * QC * TOPK * (NB // 2))
            sp.wait_ge(filled, 48)

        @block.gpsimd
        def _(pool):
            nc.gpsimd.memset(ident[:, :], 0.0).then_inc(ident0, 1)
            nc.gpsimd.memset(tri[:, :], 1.0).then_inc(ident0, 1)
            nc.gpsimd.memset(ones[:, :], 1.0).then_inc(consts_ready, 1)
            nc.gpsimd.memset(fill[:, :, :, :], 0).then_inc(ident0, 1)
            nc.gpsimd.memset(zrow[:, :], 0.0).then_inc(zeros_ready, 1)
            pool.wait_ge(ident0, 3)
            nc.gpsimd.affine_select(out=ident[:, :], in_=ident[:, :], compare_op=ALU.not_equal, fill=1.0,
                                    base=0, pattern=[[-1, P]], channel_multiplier=1).then_inc(consts_ready, 1)
            nc.gpsimd.affine_select(out=tri[:, :], in_=tri[:, :], compare_op=ALU.is_gt, fill=0.0,
                                    base=0, pattern=[[1, P]], channel_multiplier=-1).then_inc(consts_ready, 1)
            nc.gpsimd.iota(fill[:, :, :, 0], pattern=[[0, NE], [0, BLK]], base=T, channel_multiplier=1).then_inc(zeros_ready, 1)
            for i in range(2):
                nc.gpsimd.memset(stack[i][:, :, 0, :].bitcast(F32), 0.0).then_inc(consts_ready, 1)
            nc.gpsimd.iota(iota_e[:, :], pattern=[[1, NE]], base=0, channel_multiplier=0,
                           allow_small_or_imprecise_dtypes=True).then_inc(consts_ready, 1)
            nc.gpsimd.iota(slot0[:, :], pattern=[[CAP, NE]], base=0, channel_multiplier=0,
                           allow_small_or_imprecise_dtypes=True).then_inc(consts_ready, 1)
            nc.gpsimd.iota(tok[:, :], pattern=[[P, QC]], base=0, channel_multiplier=1,
                           allow_small_or_imprecise_dtypes=True).then_inc(tok_done, 1)
            nc.gpsimd.memset(expo[:, :], -0.5).then_inc(consts_ready, 1)
            nc.gpsimd.memset(seen[0][:, :], 0.0).then_inc(consts_ready, 1)
            pool.wait_ge(consts_ready, POOL_CONSTS)

            def step(s, num):
                e = stage(s, num, 2)
                if not e:
                    return
                wait_apart(pool, pool_passed, (mv_done, e.n + 1), (rstd_done, e.n))
                nc.gpsimd.tensor_scalar(veps[:, :], mv[:, :, 1], EPS, None, ALU.add).then_inc(veps_done, 1)
                pool.wait_ge(veps_done, e.n + 1)
                if num is None or num >= 3:
                    pool.wait_ge(x1_done, e.n)
                nc.gpsimd.tensor_tensor(rstd[:, :], veps[:, :], expo[:, :], ALU.pow).then_inc(rstd_done, 1)
                if num == 2:
                    pool.wait_ge(filled, 48)
                wait_apart(pool, pool_passed, (dest_done, e.n + 1), (item_done, e.n + 1))
                for n in range(QC * TOPK):
                    nc.gpsimd.indirect_dma_start(
                        out=list_d, out_offset=bass.IndirectOffsetOnAxis(ap=dest[e.parity][:, n:n + 1], axis=0),
                        in_=item[e.parity][:, n, :], in_offset=None, bounds_check=NE * CAP - 1,
                        oob_is_err=False).then_inc(listed[e.parity], 16)

            pipeline(pool, step)

        @block.scalar
        def _(act):
            act.wait_ge(keys_ready, 2)
            for w in range(4):
                act.wait_ge(wT_ready, w + 1)
                for c in range(DK):
                    ins = nc.scalar.activation(by_feature(wT_hi, w, c), from_bank(w, c), ACT.Copy)
                ins.then_inc(wT_hi_done, 1)
            act.wait_ge(b1T_ready, 1)
            nc.scalar.activation(b1T[:, :], banks[0][:, 0:NE * FT], ACT.Copy).then_inc(b1T_done, 1)

            def u_copy(b, half):
                act.wait_ge(pv_ready, QUADS * b.n + 2 * half + 2)
                act.wait_ge(uT_ready, b.n)
                nc.scalar.activation(u_sb[:, 2 * half:2 * half + 2, :], bank(BU, a=2), ACT.Copy).then_inc(u_done, 1)

            def mT_copy(b, half):
                act.wait_ge(mT_ready[half], b.n + 1)
                act.wait_ge(shift_in[half], 32 * b.n)
                act.wait_ge(mT_lo_done[half], b.n)
                nc.scalar.activation(mT_hi[half][:, :], banks[BB][0:HH, 0:S], ACT.Copy).then_inc(mT_hi_done[half], 1)

            def step(s, num):
                a, b, d, e = (stage(s, num, lag) for lag in (-1, 0, 1, 2))
                if e:
                    u_copy(e, 1)
                for k in range(H):
                    if k == 0 and b:
                        act.wait_ge(v_ready, b.n + 1)
                        if num is None or num >= 2:
                            act.wait_ge(pv_ready, QUADS * (b.n - 1))
                        for c in range(QC):
                            dst = v_aug[b.parity][:, c, :, 0:R].rearrange("p (h g) r -> p g h r", g=G)
                            src = banks[BA][:, c * D:c * D + D].rearrange("p (g h r) -> p g h r", g=G, r=R)
                            ins = nc.scalar.activation(dst, src, ACT.Copy)
                        ins.then_inc(v_done, 1)
                    if k == 1 and a:
                        act.wait_ge(xT_ready, a.n + 1)
                        if num is None or num >= 0:
                            act.wait_ge(v_ready, a.n)
                            act.wait_ge(xT_lo_done, a.n)
                        nc.scalar.activation(xT_hi[:, :, :], bank(BC, a=DK), ACT.Copy).then_inc(xT_hi_done, 1)
                    if k == 1 and d:
                        mT_copy(d, 1)
                    if k in (3, 4) and a:
                        w = k - 3
                        act.wait_ge(qk_ready[w], a.n + 1)
                        if num is None or num >= 1:
                            act.wait_ge(s_ready, H * (a.n - 1))
                            act.wait_ge(qk_lo_done[w], a.n - 1)
                        nc.scalar.activation(qk[a.parity][:, 1 - w, :, w, :], bank((BC, BA)[w], a=G), ACT.Copy).then_inc(qk_hi_done[w], 1)
                    if k == 5 and e:
                        act.wait_ge(aT_ready, e.n + 1)
                        act.wait_ge(o_ready, e.n)
                        act.wait_ge(aT_lo_done, e.n)
                        nc.scalar.activation(aT_hi[:, :, :], bank(BB, a=DK), ACT.Copy).then_inc(aT_hi_done, 1)
                    if k == 10 and b:
                        mT_copy(b, 0)
                    if k == 11 and d:
                        u_copy(d, 0)
                    if k == 12 and e:
                        act.wait_ge(x1T_ready, e.n + 1)
                        act.wait_ge(lg_ready, e.n)
                        nc.scalar.activation(x1T[:, :, :], bank(BA, a=DK), ACT.Copy).then_inc(x1T_done, 1)
                    if d:
                        act.wait_ge(st_ready, H * d.n + k + 1)
                        if num is None or num >= 2 or k >= RING:
                            act.wait_ge(pv_ready, QUADS * d.n + k // 4 - 1)
                        nc.scalar.activation(probs[:, k % RING], bank(BD[k % 2], a=QC), ACT.Exp,
                                             scale=SCALE).then_inc(exp_done, 1)
                    if k == 15 and e:
                        act.wait_ge(dmx_done, e.n + 1)
                        act.wait_ge(item_done, e.n)
                        nc.scalar.activation(ex[:, :, :], dmx[:, :, :], ACT.Exp).then_inc(ex_done, 1)

            pipeline(act, step)

        @block.vector
        def _(dve):
            for i in range(2):
                nc.vector.memset(stack[i][:, :, 1, :].bitcast(F32), 0.0).then_inc(keys_cleared, 1)
                nc.vector.memset(v_aug[i][:, :, :, :], 1.0).then_inc(keys_cleared, 1)
            dve.wait_ge(keys_cleared, 4)
            for i in range(2):
                nc.vector.memset(stack[i][ROW_M:STACK, :, 1, :].bitcast(F32), 1.0).then_inc(keys_ready, 1)
            dve.wait_ge(consts_ready, POOL_CONSTS)
            for w in range(4):
                dve.wait_ge(wT_hi_done, w + 1)
                for c in range(DK):
                    ins = nc.vector.tensor_tensor(by_feature(wT_lo, w, c), from_bank(w, c),
                                                  by_feature(wT_hi, w, c).bitcast(F32), ALU.subtract)
                ins.then_inc(wT_lo_done, 1)

            def mT_rest(b, half):
                dve.wait_ge(mT_hi_done[half], b.n + 1)
                nc.vector.tensor_tensor(mT_lo[half][:, :], banks[BB][0:HH, 0:S], mT_hi[half][:, :].bitcast(F32),
                                        ALU.subtract).then_inc(mT_lo_done[half], 1)

            def step(s, num):
                a, b, d, e = (stage(s, num, lag) for lag in (-1, 0, 1, 2))
                for k in range(H):
                    if b:
                        dve.wait_ge(s_ready, H * b.n + k + 1)
                        if k % HH == 0:
                            dve.wait_ge(mT_ready[k // HH], b.n)
                        nc.vector.tensor_reduce(negm[:, :, k], bank(BQ[k % 2], a=QC), X, ALU.max,
                                                negate=True).then_inc(max_done, 1)
                    if k == 1 and a:
                        dve.wait_ge(xT_hi_done, a.n + 1)
                        nc.vector.tensor_tensor(xT_lo[:, :, :], bank(BC, a=DK), xT_hi[:, :, :].bitcast(F32),
                                                ALU.subtract).then_inc(xT_lo_done, 1)
                    if k == 1 and d:
                        mT_rest(d, 1)
                    if k == 2 and e:
                        dve.wait_ge(uT_ready, e.n + 1)
                        dve.wait_ge(attn_done, e.n)
                        for c in range(QC):
                            sums = banks[(BA, BB)[c]][:, :].rearrange("p (u r) -> p u r", r=32)[:, :, R]
                            ins = nc.vector.reciprocal(rec[:, c, :], sums)
                        ins.then_inc(rec_done, 1)
                        dve.wait_ge(rec_done, e.n + 1)
                        dve.wait_ge(aT_ready, e.n)
                        for c in range(QC):
                            dst = attn[:, c, :].rearrange("p (g h r) -> p h g r", g=G, r=R)
                            src = banks[(BA, BB)[c]][:, :].rearrange("p (h g r) -> p h g r", g=G, r=32)[:, :, :, 0:R]
                            rc = rec[:, c, :].rearrange("p (h g) -> p h g", g=G).unsqueeze(3).to_broadcast([P, HH, G, R])
                            ins = nc.vector.tensor_tensor(dst, src, rc, ALU.mult)
                        ins.then_inc(attn_done, 1)
                    if k in (4, 5) and a:
                        w = k - 4
                        dve.wait_ge(qk_hi_done[w], a.n + 1)
                        nc.vector.tensor_tensor(qk[a.parity][:, w, :, w, :], bank((BC, BA)[w], a=G),
                                                qk[a.parity][:, 1 - w, :, w, :].bitcast(F32), ALU.subtract).then_inc(qk_lo_done[w], 1)
                    if k == 6 and e:
                        dve.wait_ge(aT_hi_done, e.n + 1)
                        nc.vector.tensor_tensor(aT_lo[:, :, :], bank(BB, a=DK), aT_hi[:, :, :].bitcast(F32),
                                                ALU.subtract).then_inc(aT_lo_done, 1)
                    if k == 8 and e:
                        dve.wait_ge(o_ready, e.n + 1)
                        dve.wait_ge(xres_loaded[e.parity], 16 * (e.half + 1))
                        dve.wait_ge(x1_done, e.n)
                        nc.vector.tensor_tensor(y[:, :, :], bank(BA, a=QC), xres[e.parity][:, :, :], ALU.add).then_inc(y_done, 1)
                        dve.wait_ge(y_done, e.n + 1)
                        for c in range(QC):
                            nc.vector.bn_stats(stats[:, c, :], y[:, c, :]).then_inc(stats_done, 1)
                        wait_apart(dve, dve_passed, (stats_done, QC * e.n + QC), (rstd_done, e.n))
                        for c in range(QC):
                            ins = nc.vector.bn_aggr(mv[:, c, :], stats[:, c, :])
                        ins.then_inc(mv_done, 1)
                    if k == 9 and e:
                        dve.wait_ge(mv_done, e.n + 1)
                        dve.wait_ge(rstd_done, e.n + 1)
                        if num is None or num >= 3:
                            dve.wait_ge(x1T_ready, e.n)
                            dve.wait_ge(x1_stored[1 - e.parity], 32 * (e.half + e.parity))
                        for c in range(QC):
                            ins = nc.vector.tensor_scalar(x1[:, c, :], y[:, c, :], mv[:, c, 0:1], rstd[:, c:c + 1],
                                                          ALU.subtract, ALU.mult)
                        ins.then_inc(x1_done, 1)
                    if k == 10 and b:
                        mT_rest(b, 0)
                    if k == 14 and e:
                        route(e, num)
                if e:
                    place(e, num)

            def route(e, num):
                dve.wait_ge(lg_ready, e.n + 1)
                dve.wait_ge(ix_done, e.n)
                nc.vector.tensor_copy(lg[:, :, :], banks[BB][:, 0:QC * NE].rearrange("p (c e) -> p c e", c=QC)).then_inc(lg_done, 1)
                wait_apart(dve, dve_passed, (lg_done, e.n + 1), (dmx_done, e.n))
                for c in range(QC):
                    ins = nc.vector.max(mx[:, c, :], lg[:, c, :])
                ins.then_inc(mx_done, 1)
                wait_apart(dve, dve_passed, (mx_done, e.n + 1), (ixf_done, e.n))
                for c in range(QC):
                    ins = nc.vector.max_index(ix[:, c, :], mx[:, c, :], lg[:, c, :])
                ins.then_inc(ix_done, 1)
                dve.wait_ge(ex_done, e.n)
                nc.vector.tensor_tensor(dmx[:, :, :], mx[:, :, :], mx[:, :, 0:1].to_broadcast([P, QC, NE]),
                                        ALU.subtract).then_inc(dmx_done, 1)
                dve.wait_ge(ix_done, e.n + 1)
                dve.wait_ge(hot_done, e.n)
                nc.vector.tensor_copy(ixf[:, :, :], ix[:, :, 0:TOPK]).then_inc(ixf_done, 1)
                dve.wait_ge(ixf_done, e.n + 1)
                dve.wait_ge(pick_done, QC * e.n)
                for c in range(QC):
                    ins = nc.vector.tensor_tensor(hot[:, c], iota_e[:, :].unsqueeze(1).to_broadcast([P, TOPK, NE]),
                                                  ixf[:, c, :].unsqueeze(2).to_broadcast([P, TOPK, NE]), ALU.is_equal)
                ins.then_inc(hot_done, 1)
                dve.wait_ge(hot_done, e.n + 1)
                dve.wait_ge(pos_ready, e.n)
                dve.wait_ge(seen_done, e.n)
                nc.vector.tensor_tensor(mask[:, :, :], hot[:, :, 0, :], hot[:, :, 1, :], ALU.add).then_inc(mask_done, 1)
                dve.wait_ge(mask_done, e.n + 1)
                nc.vector.tensor_tensor(seen_t[:, :], seen[e.parity][:, :], mask[:, 0, :], ALU.add).then_inc(seen_mid, 1)
                dve.wait_ge(seen_mid, e.n + 1)
                nc.vector.tensor_tensor(seen[1 - e.parity][:, :], seen_t[:, :], mask[:, 1, :], ALU.add).then_inc(seen_done, 1)

            def place(e, num):
                dve.wait_ge(pos_ready, e.n + 1)
                pos = banks[BA][:, 0:QC * NE].rearrange("p (c e) -> p c e", c=QC)
                dve.wait_ge(slotb_done, e.n)
                nc.vector.tensor_scalar(over[:, :, :], pos, float(CAP), float(NE * CAP), ALU.is_ge, ALU.mult).then_inc(over_done, 1)
                nc.vector.tensor_tensor(slot[:, :, :], pos, slot0[:, :].unsqueeze(1).to_broadcast([P, QC, NE]), ALU.add).then_inc(slot_done, 1)
                dve.wait_ge(over_done, e.n + 1)
                dve.wait_ge(slot_done, e.n + 1)
                dve.wait_ge(pick_done, QC * e.n)
                nc.vector.tensor_tensor(slot_b[:, :, :], slot[:, :, :], over[:, :, :], ALU.add).then_inc(slotb_done, 1)
                dve.wait_ge(slotb_done, e.n + 1)
                dve.wait_ge(destf_done, e.n)
                for c in range(QC):
                    nc.vector.tensor_tensor(pick[:, c], hot[:, c], slot_b[:, c, :].unsqueeze(1).to_broadcast([P, TOPK, NE]),
                                            ALU.mult).then_inc(pick_done, 1)
                dve.wait_ge(pick_done, QC * e.n + QC)
                dve.wait_ge(dest_done, e.n)
                nc.vector.tensor_reduce(dest_f[:, :, :], pick[:, :, :, :], X, ALU.add).then_inc(destf_done, 1)
                dve.wait_ge(destf_done, e.n + 1)
                if num is None or num >= 4:
                    dve.wait_ge(listed[e.parity], 16 * QC * TOPK * e.half)
                nc.vector.tensor_copy(dest[e.parity][:, :].rearrange("p (c k) -> p c k", c=QC), dest_f[:, :, :]).then_inc(dest_done, 1)
                dve.wait_ge(ex_done, e.n + 1)
                nc.vector.tensor_reduce(zsum[:, :], ex[:, :, :], X, ALU.add).then_inc(zsum_done, 1)
                dve.wait_ge(zsum_done, e.n + 1)
                nc.vector.tensor_scalar(den[:, :], zsum[:, :], 1e-8, 1.0, ALU.mult, ALU.add).then_inc(den_done, 1)
                dve.wait_ge(den_done, e.n + 1)
                nc.vector.tensor_tensor(den2[:, :], den[:, :], ex[:, :, 1], ALU.add).then_inc(den2_done, 1)
                dve.wait_ge(den2_done, e.n + 1)
                nc.vector.reciprocal(den[:, :], den2[:, :]).then_inc(w0_done, 1)
                dve.wait_ge(w0_done, e.n + 1)
                it = item[e.parity][:, :, :].rearrange("p (c k) w -> p c k w", c=QC)
                nc.vector.tensor_tensor(it[:, :, :, 1].bitcast(F32), ex[:, :, 0:TOPK], den[:, :].unsqueeze(2).to_broadcast([P, QC, TOPK]), ALU.mult)
                dve.wait_ge(tok_done, e.n + 1)
                nc.vector.tensor_copy(it[:, :, :, 0], tok[:, :].unsqueeze(2).to_broadcast([P, QC, TOPK])).then_inc(item_done, 1)
                dve.wait_ge(item_done, e.n + 1)
                nc.vector.tensor_scalar(tok[:, :], tok[:, :], float(S), None, ALU.add).then_inc(tok_done, 1)

            pipeline(dve, step)

        @block.tensor
        def _(pe):
            pe.wait_ge(consts_ready, POOL_CONSTS)
            pe.wait_ge(keys_ready, 2)
            pe.wait_ge(w_loaded, 64)
            for w in range(4):
                for c in range(DK):
                    for r in range(QC):
                        ins = nc.tensor.transpose(banks[4 + w][:, c * D + r * P:c * D + r * P + P],
                                                  w_raw[:, w, r, c * P:c * P + P], ident[:, :])
                ins.then_inc(wT_ready, 1)
            pe.wait_ge(small_loaded, 32)
            nc.tensor.transpose(banks[0][:, 0:NE * FT], b1_raw[:, :], ident[0:NE * FT, 0:NE * FT]).then_inc(b1T_ready, 1)
            pe.wait_ge(b1T_done, 1)
            pe.wait_ge(wT_hi_done, 4)
            pe.wait_ge(wT_lo_done, 4)

            def product(out, pairs):
                for n, (l, r) in enumerate(pairs):
                    ins = nc.tensor.matmul(out, l, r, start=(n == 0), stop=(n == len(pairs) - 1))
                return ins

            def split_pairs(l_hi, l_lo, r_hi, r_lo):
                return [p for c in range(DK) for p in ((l_hi(c), r_hi(c)), (l_hi(c), r_lo(c)), (l_lo(c), r_hi(c)))]

            def pv(b, t):
                pe.wait_ge(exp_done, H * b.n + 4 * t + 4)
                if t == 0:
                    pe.wait_ge(v_done, b.n + 1)
                if t % 2 == 0:
                    pe.wait_ge(u_done, 2 * b.n + t // 2)
                for c in range(QC):
                    for j in range(4):
                        u = 4 * t + j
                        out = banks[BU][32 * j:32 * j + 32, (t % 2) * S:(t % 2) * S + S]
                        ins = nc.tensor.matmul(out, v_aug[b.parity][:, c, u, :], probs[:, u % RING, c, :],
                                               start=(c == 0), stop=(c == QC - 1), tile_position=(0, 32 * j))
                ins.then_inc(pv_ready, 1)

            def mT(b, half):
                pe.wait_ge(max_done, H * b.n + HH * half + HH)
                for c in range(QC):
                    ins = nc.tensor.transpose(banks[BB][0:HH, c * P:c * P + P], negm[:, c, HH * half:HH * half + HH], ident[:, :])
                ins.then_inc(mT_ready[half], 1)

            def step(s, num):
                a, b, d, e = (stage(s, num, lag) for lag in (-1, 0, 1, 2))
                if e:
                    pv(e, QUADS - 1)
                for k in range(H):
                    if k == 0 and b:
                        pe.wait_ge(xT_lo_done, b.n + 1)
                        if num is None or num >= 3:
                            pe.wait_ge(dest_done, b.n - 2)
                        pe.wait_ge(qk_lo_done[1], b.n + 1)
                        for c in range(QC):
                            ins = product(banks[BA][:, c * D:c * D + D], split_pairs(
                                lambda i: xT_hi[:, i, c * P:c * P + P], lambda i: xT_lo[:, i, c * P:c * P + P],
                                lambda i: wT_hi[:, 2, i, :], lambda i: wT_lo[:, 2, i, :]))
                        ins.then_inc(v_ready, 1)
                    if k == 1 and a:
                        pe.wait_ge(x_loaded[a.parity], 16 * (a.half + 1))
                        pe.wait_ge(qk_lo_done[0], a.n)
                        for c in range(DK):
                            for r in range(QC):
                                ins = nc.tensor.transpose(banks[BC][:, c * S + r * P:c * S + r * P + P],
                                                          x_sb[a.parity][:, r, c * P:c * P + P], ident[:, :])
                        ins.then_inc(xT_ready, 1)
                    if k == 1 and d:
                        if num is None or num >= 3:
                            pe.wait_ge(lg_done, d.n - 1)
                        pe.wait_ge(mT_lo_done[0], d.n + 1)
                        mT(d, 1)
                    if k == 2 and e:
                        pe.wait_ge(u_done, 2 * e.n + 2)
                        if not b:
                            pe.wait_ge(dest_done, e.n)
                        pe.wait_ge(v_done, e.n + (3 if b else 2 if d else 1))
                        pe.wait_ge(mT_lo_done[1], e.n + (2 if d else 1))
                        for c in range(QC):
                            for t in range(QUADS):
                                ins = nc.tensor.transpose(banks[(BA, BB)[c]][:, t * P:t * P + P],
                                                          u_sb[:, t, c * P:c * P + P], ident[:, :])
                        ins.then_inc(uT_ready, 1)
                    if k in (3, 4) and a:
                        w = k - 3
                        if w == 0:
                            pe.wait_ge(xT_lo_done, a.n + 1)
                        elif e:
                            pe.wait_ge(attn_done, e.n + 1)
                        elif b:
                            pe.wait_ge(v_done, b.n + 1)
                        for o in range(G):
                            ins = product(banks[(BC, BA)[w]][:, o * S:o * S + S], split_pairs(
                                lambda i: wT_hi[:, w, i, o * P:o * P + P], lambda i: wT_lo[:, w, i, o * P:o * P + P],
                                lambda i: xT_hi[:, i, :], lambda i: xT_lo[:, i, :]))
                        ins.then_inc(qk_ready[w], 1)
                    if k == 5 and e:
                        pe.wait_ge(attn_done, e.n + 1)
                        for c in range(DK):
                            for r in range(QC):
                                ins = nc.tensor.transpose(banks[BB][:, c * S + r * P:c * S + r * P + P],
                                                          attn[:, r, c * P:c * P + P], ident[:, :])
                        ins.then_inc(aT_ready, 1)
                    if k == 7 and e:
                        pe.wait_ge(aT_lo_done, e.n + 1)
                        if a:
                            pe.wait_ge(qk_lo_done[1], a.n + 1)
                        for c in range(QC):
                            ins = product(banks[BA][:, c * D:c * D + D], split_pairs(
                                lambda i: aT_hi[:, i, c * P:c * P + P], lambda i: aT_lo[:, i, c * P:c * P + P],
                                lambda i: wT_hi[:, 3, i, :], lambda i: wT_lo[:, 3, i, :]))
                        ins.then_inc(o_ready, 1)
                    if k == 10 and b:
                        if e:
                            pe.wait_ge(aT_lo_done, e.n + 1)
                        elif d:
                            pe.wait_ge(mT_lo_done[1], d.n + 1)
                        mT(b, 0)
                    if k == 11 and e:
                        pe.wait_ge(x1_done, e.n + 1)
                        for c in range(DK):
                            for r in range(QC):
                                ins = nc.tensor.transpose(banks[BA][:, c * S + r * P:c * S + r * P + P],
                                                          x1[:, r, c * P:c * P + P], ident[:, :])
                        ins.then_inc(x1T_ready, 1)
                    if k == 13 and e:
                        pe.wait_ge(x1T_done, e.n + 1)
                        if b:
                            pe.wait_ge(mT_lo_done[0], b.n + 1)
                        for c in range(QC):
                            for i in range(DK):
                                ins = nc.tensor.matmul(banks[BB][:, c * NE:c * NE + NE], x1T[:, i, c * P:c * P + P],
                                                       gate_w[:, i, :], start=(i == 0), stop=(i == DK - 1))
                        ins.then_inc(lg_ready, 1)
                    if b:
                        if k % HH == 0:
                            pe.wait_ge(stacked[k // HH], 64 * (b.n + 1))
                        if num is None or num >= 1 or k >= 2:
                            pe.wait_ge(max_done, H * b.n + k - 1)
                        for c in range(QC):
                            ins = nc.tensor.matmul(banks[BQ[k % 2]][:, c * S:c * S + S],
                                                   stack[b.parity][0:ROW_M, k, 0, c * P:c * P + P],
                                                   stack[b.parity][0:ROW_M, k, 1, :], start=True, stop=True)
                        ins.then_inc(s_ready, 1)
                    if d:
                        if k % HH == 0:
                            pe.wait_ge(shift_in[k // HH], 32 * (d.n + 1))
                        if num is None or num >= 2 or k >= 2:
                            pe.wait_ge(exp_done, H * d.n + k - 1)
                        for c in range(QC):
                            ins = nc.tensor.matmul(banks[BD[k % 2]][:, c * S:c * S + S],
                                                   stack[d.parity][:, k, 1, c * P:c * P + P],
                                                   stack[d.parity][:, k, 0, :], start=True, stop=True)
                        ins.then_inc(st_ready, 1)
                        if k % 4 == 2 and k > 4:
                            pv(d, k // 4 - 1)
                if e:
                    pe.wait_ge(seen_done, e.n + 1)
                    for c in range(QC):
                        out = banks[BA][:, c * NE:c * NE + NE]
                        nc.tensor.matmul(out, tri[:, :], mask[:, c, :], start=True, stop=False)
                        ins = nc.tensor.matmul(out, ones[:, :], (seen[e.parity], seen_t)[c][:, :], start=False, stop=True)
                    ins.then_inc(pos_ready, 1)

            pipeline(pe, step)


POOL_CONSTS = 9


def experts(nc, g):
    x1_d, acc_d, list_v, w1_d, w2_d, b2_d = g["x1_d"], g["acc_d"], g["list_v"], g["w1_d"], g["w2_d"], g["b2_d"]
    NE, FT, D, DK, FF, C, BLK, NC, QC = g["NE"], g["FT"], g["D"], g["DK"], g["FF"], g["C"], g["BLK"], g["NC"], g["QC"]
    banks, ident, b1T, w1_raw, w2_raw = g["banks"], g["ident"], g["b1T"], g["w1_raw"], g["w2_raw"]
    w1_loaded, w2_loaded = g["w1_loaded"], g["w2_loaded"]
    AHEAD = 3
    PARTS = 2
    PAIRS = FT // 2
    ctx = ExitStack()
    with ctx:
        def sem(name):
            return ctx.enter_context(nc.semaphore(name))

        def sb(name, shape, dt=F32):
            return ctx.enter_context(nc.sbuf_tensor(name, shape, dt))

        w1_hi, w1_lo = sb("w1_hi", [P, DK, FF], F32R), sb("w1_lo", [P, DK, FF], F32R)
        w2_hi, w2_lo = sb("w2_hi", [P, FT, D], F32R), sb("w2_lo", [P, FT, D], F32R)
        b2_all = sb("b2_all", [P, NE, D])
        lists = sb("lists", [P, NE, BLK, 2], I32)
        meta = [sb(f"meta{c}", [P, QC, 2], I32) for c in range(NC)]
        rows = [sb(f"rows{c}", [P, QC, D]) for c in range(NC)]
        g_hi = [sb(f"g_hi{i}", [P, DK, C], F32R) for i in range(3)]
        g_lo = [sb(f"g_lo{i}", [P, DK, C], F32R) for i in range(3)]
        h = [sb(f"h{i}", [P, 2, C]) for i in range(2)]
        h_hi = [sb(f"h_hi{i}", [P, FT, C], F32R) for i in range(3)]
        h_lo = [sb(f"h_lo{i}", [P, FT, C], F32R) for i in range(3)]
        o_b = [sb(f"o_b{i}", [P, QC, D]) for i in range(2)]
        o_w = [sb(f"o_w{c}", [P, QC, D]) for c in range(NC)]

        lists_loaded, b2_loaded = sem("lists_loaded"), g["b2_loaded"]
        w1_hi_done, w1_lo_done, w2_hi_done, w2_lo_done = sem("w1_hi_done"), sem("w1_lo_done"), sem("w2_hi_done"), sem("w2_lo_done")
        pool_passed, act_passed = sem("pool_passed2"), sem("act_passed")
        meta_done = sem("meta_done")
        gathered = [sem(f"gathered{c}") for c in range(NC)]
        gT_ready, g_hi_done, g_lo_done = sem("gT_ready"), sem("g_hi_done"), sem("g_lo_done")
        z_ready, h_done, h_hi_done, h_lo_done = sem("z_ready"), sem("h_done"), sem("h_hi_done"), sem("h_lo_done")
        eo_ready, ob_done, ow_done, added = sem("eo_ready"), sem("ob_done"), sem("ow_done"), sem("added")
        BZ, BO, BT = (0, 1, 2, 3), (4, 5), (6, 7)

        def bank(i, **kw):
            return banks[i][:, :].rearrange("p (a b) -> p a b", **kw)

        block = ctx.enter_context(nc.Block())

        @block.sync
        def _(sp):
            sp.dma_start(lists[:, :, :, :].rearrange("p e j w -> p e (j w)"), list_v).then_inc(lists_loaded, 16)
            for e in range(NE):
                sp.dma_start(b2_all[:, e, :], b2_d[e:e + 1, :].partition_broadcast(P).rearrange("p a d -> p (a d)")).then_inc(b2_loaded, 16)
            with sp.Fori(1, NE) as e:
                sp.wait_ge(w1_hi_done, PARTS * e)
                sp.wait_ge(w1_lo_done, PARTS * e)
                sp.dma_start(w1_raw[:, :, :], w1_d[e].rearrange("(c p) f -> p c f", p=P)).then_inc(w1_loaded, 16)
                sp.wait_ge(w2_hi_done, PARTS * e)
                sp.wait_ge(w2_lo_done, PARTS * e)
                sp.dma_start(w2_raw[:, :, :], w2_d[e].rearrange("(f p) d -> p f d", p=P)).then_inc(w2_loaded, 16)
            sp.wait_ge(added, 16 * NE * BLK)

        @block.gpsimd
        def _(pool):
            pool.wait_ge(lists_loaded, 16)

            def gather(e, c):
                n = NC * e + c
                if not (isinstance(e, int) and e == 0):
                    pool.wait_ge(added, 16 * QC * (n - NC + 1))
                nc.gpsimd.tensor_copy(meta[c][:, :, :], lists[:, e, QC * c:QC * c + QC, :]).then_inc(meta_done, 1)
                wait_apart(pool, pool_passed, (meta_done, n + 1))
                for r in range(QC):
                    nc.gpsimd.indirect_dma_start(
                        out=rows[c][:, r, :], out_offset=None, in_=x1_d,
                        in_offset=bass.IndirectOffsetOnAxis(ap=meta[c][:, r, 0:1], axis=0)).then_inc(gathered[c], 16)

            def add_back(e, c):
                n = NC * e + c
                pool.wait_ge(ow_done, QC * (n + 1))
                for r in range(QC):
                    wait_apart(pool, pool_passed, (added, 16 * (QC * n + r)))
                    nc.gpsimd.indirect_dma_start(
                        out=acc_d, out_offset=bass.IndirectOffsetOnAxis(ap=meta[c][:, r, 0:1], axis=0),
                        in_=o_w[c][:, r, :], in_offset=None, compute_op=ALU.add).then_inc(added, 16)

            def expert(e, last):
                for c in range(NC):
                    if c + AHEAD < NC:
                        gather(e, c + AHEAD)
                    elif not last:
                        gather(e + 1, c + AHEAD - NC)
                    add_back(e, c)

            for c in range(AHEAD):
                gather(0, c)
            expert(0, False)
            with pool.Fori(1, NE - 1) as e:
                expert(e, False)
            expert(NE - 1, True)

        @block.scalar
        def _(act):
            def split_w1(e):
                act.wait_ge(w1_loaded, 16 * (e + 1))
                act.wait_ge(z_ready, PAIRS * NC * e)
                for i in range(PARTS):
                    f = slice(i * (FF // PARTS), (i + 1) * (FF // PARTS))
                    nc.scalar.activation(w1_hi[:, :, f], w1_raw[:, :, f], ACT.Copy).then_inc(w1_hi_done, 1)

            def split_w2(e):
                act.wait_ge(w2_loaded, 16 * (e + 1))
                act.wait_ge(eo_ready, NC * e)
                for i in range(PARTS):
                    f = slice(i * (FT // PARTS), (i + 1) * (FT // PARTS))
                    nc.scalar.activation(w2_hi[:, f, :], w2_raw[:, f, :], ACT.Copy).then_inc(w2_hi_done, 1)

            def rows_hi(e, c):
                n = NC * e + c
                act.wait_ge(gT_ready, n + 1)
                if not (isinstance(n, int) and n < 3):
                    act.wait_ge(z_ready, PAIRS * (n - 1))
                nc.scalar.activation(g_hi[HBUF[c]][:, :, :], bank(BT[c % 2], a=DK), ACT.Copy).then_inc(g_hi_done, 1)

            def relu(e, c):
                for m in range(PAIRS):
                    n = PAIRS * (NC * e + c) + m
                    used = () if isinstance(n, int) and n < 2 else ((h_hi_done, n - 1), (h_lo_done, n - 1))
                    wait_apart(act, act_passed, (z_ready, n + 1), *used)
                    for i in range(2):
                        col = FT * e + 2 * m + i
                        ins = nc.scalar.activation(h[m % 2][:, i, :], bank(BZ[m], a=2)[:, i, :], ACT.Relu,
                                                   bias=b1T[:, col:col + 1] if isinstance(col, int) else b1T[:, bass.ds(col, 1)])
                    ins.then_inc(h_done, 1)

            def weigh(e, c):
                n = NC * e + c
                act.wait_ge(ob_done, n + 1)
                for r in range(QC):
                    nc.scalar.activation(o_w[c][:, r, :], o_b[c % 2][:, r, :], ACT.Copy,
                                         scale=meta[c][:, r, 1:2].bitcast(F32)).then_inc(ow_done, 1)

            expert_order(act, NE, NC, lambda e, c: (rows_hi(e, c)), relu, weigh, split_w1, split_w2)

        @block.vector
        def _(dve):
            def split_w1(e):
                for i in range(PARTS):
                    f = slice(i * (FF // PARTS), (i + 1) * (FF // PARTS))
                    dve.wait_ge(w1_hi_done, PARTS * e + i + 1)
                    nc.vector.tensor_tensor(w1_lo[:, :, f], w1_raw[:, :, f], w1_hi[:, :, f].bitcast(F32),
                                            ALU.subtract).then_inc(w1_lo_done, 1)

            def split_w2(e):
                for i in range(PARTS):
                    f = slice(i * (FT // PARTS), (i + 1) * (FT // PARTS))
                    dve.wait_ge(w2_hi_done, PARTS * e + i + 1)
                    nc.vector.tensor_tensor(w2_lo[:, f, :], w2_raw[:, f, :], w2_hi[:, f, :].bitcast(F32),
                                            ALU.subtract).then_inc(w2_lo_done, 1)

            def rows_lo(e, c):
                dve.wait_ge(g_hi_done, NC * e + c + 1)
                nc.vector.tensor_tensor(g_lo[HBUF[c]][:, :, :], bank(BT[c % 2], a=DK), g_hi[HBUF[c]][:, :, :].bitcast(F32),
                                        ALU.subtract).then_inc(g_lo_done, 1)

            def halves(e, c):
                for m in range(PAIRS):
                    n = PAIRS * (NC * e + c) + m
                    dve.wait_ge(h_done, n + 1)
                    if m == 0 and not (isinstance(e, int) and e == 0 and c < 3):
                        dve.wait_ge(eo_ready, NC * e + c - 1)
                    t = slice(2 * m, 2 * m + 2)
                    nc.vector.tensor_copy(h_hi[HBUF[c]][:, t, :], h[m % 2][:, :, :]).then_inc(h_hi_done, 1)
                    dve.wait_ge(h_hi_done, n + 1)
                    nc.vector.tensor_tensor(h_lo[HBUF[c]][:, t, :], h[m % 2][:, :, :], h_hi[HBUF[c]][:, t, :].bitcast(F32),
                                            ALU.subtract).then_inc(h_lo_done, 1)

            def bias(e, c):
                n = NC * e + c
                dve.wait_ge(eo_ready, n + 1)
                if not (isinstance(n, int) and n < 3):
                    dve.wait_ge(ow_done, QC * (n - (1 if c != 0 else 0)))
                for r in range(QC):
                    ins = nc.vector.tensor_tensor(o_b[c % 2][:, r, :], bank(BO[c % 2], a=QC)[:, r, :], b2_all[:, e, :], ALU.add)
                ins.then_inc(ob_done, 1)

            dve.wait_ge(b2_loaded, 16 * NE)
            expert_order(dve, NE, NC, rows_lo, halves, bias, split_w1, split_w2)

        @block.tensor
        def _(pe):
            def transposes(e, c):
                n = NC * e + c
                pe.wait_ge(gathered[c], 16 * QC * (e + 1))
                if not (isinstance(n, int) and n < 2):
                    pe.wait_ge(g_lo_done, n if c == 0 else n - 1)
                for i in range(DK):
                    for r in range(QC):
                        ins = nc.tensor.transpose(banks[BT[c % 2]][:, i * C + r * P:i * C + r * P + P],
                                                  rows[c][:, r, i * P:i * P + P], ident[:, :])
                ins.then_inc(gT_ready, 1)

            def layer1(e, c):
                n = NC * e + c
                pe.wait_ge(g_lo_done, n + 1)
                G_hi, G_lo = g_hi[HBUF[c]], g_lo[HBUF[c]]
                for m in range(PAIRS):
                    if c == 0 and m % (PAIRS // PARTS) == 0:
                        pe.wait_ge(w1_lo_done, PARTS * e + m // (PAIRS // PARTS) + 1)
                    if not (isinstance(n, int) and n == 0):
                        pe.wait_ge(h_done, PAIRS * (n - 1) + m + 1)
                    for i in range(2):
                        f = slice((2 * m + i) * P, (2 * m + i + 1) * P)
                        out = bank(BZ[m], a=2)[:, i, :]
                        for k in range(DK):
                            nc.tensor.matmul(out, w1_hi[:, k, f], G_hi[:, k, :], start=(k == 0), stop=False)
                            nc.tensor.matmul(out, w1_hi[:, k, f], G_lo[:, k, :], start=False, stop=False)
                            ins = nc.tensor.matmul(out, w1_lo[:, k, f], G_hi[:, k, :], start=False, stop=(k == DK - 1))
                    ins.then_inc(z_ready, 1)

            def layer2(e, c):
                n = NC * e + c
                if not (isinstance(n, int) and n < 2):
                    pe.wait_ge(ob_done, n if c == 0 else n - 1)
                H_hi, H_lo = h_hi[HBUF[c]], h_lo[HBUF[c]]
                for r in range(QC):
                    rs = slice(r * P, r * P + P)
                    out = bank(BO[c % 2], a=QC)[:, r, :]
                    for f in range(FT):
                        if r == 0 and c == 0 and f % (FT // PARTS) == 0:
                            pe.wait_ge(w2_lo_done, PARTS * e + f // (FT // PARTS) + 1)
                        if r == 0 and f % 2 == 0:
                            pe.wait_ge(h_lo_done, PAIRS * n + f // 2 + 1)
                        nc.tensor.matmul(out, H_hi[:, f, rs], w2_hi[:, f, :], start=(f == 0), stop=False)
                        nc.tensor.matmul(out, H_hi[:, f, rs], w2_lo[:, f, :], start=False, stop=False)
                        ins = nc.tensor.matmul(out, H_lo[:, f, rs], w2_hi[:, f, :], start=False, stop=(f == FT - 1))
                ins.then_inc(eo_ready, 1)

            expert_order(pe, NE, NC, transposes, layer1, layer2, None, None)


def expert_order(engine, NE, NC, take_in, layer1, layer2, split_w1, split_w2):
    def split(fn, e):
        if fn:
            fn(e)

    def body(e, last):
        for c in range(NC):
            if c + 2 < NC:
                take_in(e, c + 2)
            elif not last:
                take_in(e + 1, c + 2 - NC)
            if c + 1 < NC:
                layer1(e, c + 1)
            elif not last:
                layer1(e + 1, 0)
            if c + 1 == NC - 1 and not last:
                split(split_w1, e + 1)
            layer2(e, c)
        if not last:
            split(split_w2, e + 1)

    split(split_w1, 0)
    split(split_w2, 0)
    take_in(0, 0)
    take_in(0, 1)
    layer1(0, 0)
    body(0, False)
    with engine.Fori(1, NE - 1) as e:
        body(e, False)
    body(NE - 1, True)


def last_norm(nc, g):
    acc_v, out_d, NB, QC, D, expo = g["acc_v"], g["out_d"], g["NB"], g["QC"], g["D"], g["expo"]
    out_v = out_d.rearrange("b (c p) d -> b p c d", p=P)
    NBUF = 8
    ctx = ExitStack()
    with ctx:
        def sem(name):
            return ctx.enter_context(nc.semaphore(name))

        def sb(name, shape, dt=F32):
            return ctx.enter_context(nc.sbuf_tensor(name, shape, dt))

        a = [sb(f"a{i}", [P, QC, D]) for i in range(NBUF)]
        o = [sb(f"o{i}", [P, QC, D]) for i in range(NBUF)]
        stats = sb("stats2", [P, NB, QC, 6])
        mv = sb("mv2", [P, NB, QC, 2])
        veps = sb("veps2", [P, NB, QC])
        rstd = sb("rstd2", [P, NB, QC])
        loaded = [sem(f"acc_loaded{i}") for i in range(NBUF)]
        stored = [sem(f"out_stored{i}") for i in range(NBUF)]
        stats_done, mv_done, veps_done, rstd_done, o_done = (sem(n) for n in ("stats2_done", "mv2_done", "veps2_done", "rstd2_done", "out_done"))
        block = ctx.enter_context(nc.Block())

        @block.sync
        def _(sp):
            for b in range(NB):
                if b >= NBUF:
                    sp.wait_ge(o_done, QC * (b - NBUF + 1))
                sp.dma_start(a[b % NBUF][:, :, :], acc_v[b]).then_inc(loaded[b % NBUF], 16)

        @block.vector
        def _(dve):
            def apply(b):
                dve.wait_ge(rstd_done, b + 1)
                if b >= NBUF:
                    dve.wait_ge(stored[b % NBUF], 16 * (b // NBUF))
                for c in range(QC):
                    nc.vector.tensor_scalar(o[b % NBUF][:, c, :], a[b % NBUF][:, c, :], mv[:, b, c, 0:1], rstd[:, b, c:c + 1],
                                            ALU.subtract, ALU.mult).then_inc(o_done, 1)

            for b in range(NB):
                dve.wait_ge(loaded[b % NBUF], 16 * (b // NBUF + 1))
                for c in range(QC):
                    nc.vector.bn_stats(stats[:, b, c, :], a[b % NBUF][:, c, :]).then_inc(stats_done, 1)
                dve.wait_ge(stats_done, QC * (b + 1))
                for c in range(QC):
                    ins = nc.vector.bn_aggr(mv[:, b, c, :], stats[:, b, c, :])
                ins.then_inc(mv_done, 1)
                if b >= 2:
                    apply(b - 2)
            for b in (NB - 2, NB - 1):
                apply(b)

        @block.gpsimd
        def _(pool):
            for b in range(NB):
                pool.wait_ge(mv_done, b + 1)
                nc.gpsimd.tensor_scalar(veps[:, b, :], mv[:, b, :, 1], EPS, None, ALU.add).then_inc(veps_done, 1)
                pool.wait_ge(veps_done, b + 1)
                nc.gpsimd.tensor_tensor(rstd[:, b, :], veps[:, b, :], expo[:, :], ALU.pow).then_inc(rstd_done, 1)

        @block.scalar
        def _(act):
            for b in range(NB):
                act.wait_ge(o_done, QC * (b + 1))
                act.dma_start(out_v[b], o[b % NBUF][:, :, :]).then_inc(stored[b % NBUF], 16)
            for i in range(NBUF):
                act.wait_ge(stored[i], 16 * (NB // NBUF))


_INS = ['L0_attn_x', 'L0_attn_w_q', 'L0_attn_w_k', 'L0_attn_w_v', 'L0_attn_w_o', 'L0_ffn_gating_w',
        'L0_ffn_w1', 'L0_ffn_b1', 'L0_ffn_w2', 'L0_ffn_b2']


def kernel(**inputs):
    import numpy as _np
    import concourse.bacc as _bacc
    from concourse import mybir as _mybir
    from concourse.bass_utils import run_bass_kernel_spmd as _run

    nc = _bacc.Bacc("TRN2", target_bir_lowering=False, num_devices=1)
    arrays, args = {}, []
    for name in _INS:
        a = _np.ascontiguousarray(inputs[name])
        arrays[f"in_{name}"] = a
        args.append(nc.dram_tensor(f"in_{name}", a.shape, _mybir.dt.from_np(a.dtype), kind="ExternalInput").ap())
    shape = inputs['L0_attn_x'].shape
    args.append(nc.dram_tensor("out_0", shape, _mybir.dt.float32, kind="ExternalOutput").ap())
    build(nc, *args)
    r = _run(nc, [arrays], core_ids=[0])
    return r.results[0]["out_0"]
```

```python
from contextlib import ExitStack

import concourse.bass as bass
from concourse import mybir

F32 = mybir.dt.float32
F32R = mybir.dt.float32r
BF16 = mybir.dt.bfloat16
I32 = mybir.dt.int32
U32 = mybir.dt.uint32
ALU = mybir.AluOpType
ACT = mybir.ActivationFunctionType
X = mybir.AxisListType.X

P = 128
EPS = 1e-5
ROW_B, ROW_C, ROW_M, STACK = 16, 64, 96, 98
RING = 8
GW = 128
HBUF = (0, 1, 0, 1, 2)


def wait_apart(engine, passed, *waits):
    for semaphore, value in waits:
        engine.wait_ge(semaphore, value)
    engine.sem_inc(passed, 1)


class Seq:

    def __init__(self, i, off):
        self.n = 2 * i + off
        self.parity = off % 2
        self.half = i + off // 2


def build(nc, x_d, wq_d, wk_d, wv_d, wo_d, gw_d, w1_d, b1_d, w2_d, b2_d, out_d):
    NB, S, D = x_d.shape
    T = NB * S
    R = 16
    H = D // R
    NE, _, FF = w1_d.shape
    TOPK = 2
    CAP = -(-(T * TOPK * 5) // (NE * 4))
    SCALE = R ** -0.5
    QC = S // P
    DK = D // P
    HH = P // R
    FT = FF // P
    BLK = CAP // P
    NC = BLK // QC
    C = QC * P
    TRASH = P

    x1_d = nc.dram_tensor("x1_rows", (T + TRASH, D), F32, kind="Internal").ap()
    acc_d = nc.dram_tensor("acc_rows", (T + TRASH, D), F32, kind="Internal").ap()
    list_d = nc.dram_tensor("slot_list", (NE * CAP, 2), I32, kind="Internal").ap()

    x_v = x_d.rearrange("b (c p) d -> b p c d", p=P)
    x1_v = x1_d[0:T, :].rearrange("(b c p) d -> b p c d", p=P, c=QC)
    acc_v = acc_d[0:T, :].rearrange("(b c p) d -> b p c d", p=P, c=QC)
    list_v = list_d.rearrange("(e p j) w -> p e (j w)", e=NE, p=P)

    top = ExitStack()

    def sem(name, ctx=top):
        return ctx.enter_context(nc.semaphore(name))

    def sb(name, shape, dt=F32, ctx=top):
        return ctx.enter_context(nc.sbuf_tensor(name, shape, dt))

    with top:
        banks = [top.enter_context(nc.psum_tensor(f"bank{i}", [P, 512], F32)) for i in range(8)]
        ident = sb("ident", [P, P])
        b1T = sb("b1T", [P, NE * FT])
        w1_raw = sb("w1_raw", [P, DK, FF])
        w2_raw = sb("w2_raw", [P, FT, D])
        expo = sb("expo", [P, QC])
        w1_loaded, w2_loaded, b2_loaded = sem("w1_loaded"), sem("w2_loaded"), sem("b2_loaded")

        attention(nc, locals())
        experts(nc, locals())
        last_norm(nc, locals())


def attention(nc, g):
    (x_v, x1_v, acc_v, list_v, x1_d, acc_d, list_d) = (
        g["x_v"], g["x1_v"], g["acc_v"], g["list_v"], g["x1_d"], g["acc_d"], g["list_d"])
    NB, S, D, T, R, H = g["NB"], g["S"], g["D"], g["T"], g["R"], g["H"]
    QC, DK, HH, NE, FT, CAP, BLK = g["QC"], g["DK"], g["HH"], g["NE"], g["FT"], g["CAP"], g["BLK"]
    SCALE, TRASH, TOPK = g["SCALE"], g["TRASH"], g["TOPK"]
    banks, ident, b1T, expo = g["banks"], g["ident"], g["b1T"], g["expo"]
    G = H // HH
    QUADS = H // 4
    ctx = ExitStack()
    with ctx:
        def sem(name):
            return ctx.enter_context(nc.semaphore(name))

        def sb(name, shape, dt=F32):
            return ctx.enter_context(nc.sbuf_tensor(name, shape, dt))

        tri = sb("tri", [P, P], BF16)
        ones = sb("ones", [P, P], BF16)
        w_raw = sb("w_raw", [P, 4, DK, D])
        wT_hi = sb("wT_hi", [P, 4, DK, D], F32R)
        wT_lo = sb("wT_lo", [P, 4, DK, D], F32R)
        b1_raw = sb("b1_raw", [NE * FT, P])
        gate_raw = sb("gate_raw", [P, DK, NE])
        gate_hi = sb("gate_hi", [P, DK, GW // NE, NE], F32R)
        gate_lo = sb("gate_lo", [P, DK, GW // NE, NE], F32R)
        iota_e = sb("iota_e", [P, NE])
        slot0 = sb("slot0", [P, NE])
        fill = sb("fill", [P, NE, BLK, 2], I32)
        zrow = sb("zrow", [P, D])
        ones_f = sb("ones_f", [P, S])
        tok = sb("tok", [P, QC])
        x_sb = [sb(f"x_sb{i}", [P, QC, D]) for i in range(2)]
        xres = [sb(f"xres{i}", [P, QC, D]) for i in range(2)]
        xT_f = sb("xT_f", [P, DK, S])
        xT_hi = [sb(f"xT_hi{i}", [P, DK, S], F32R) for i in range(2)]
        xT_lo = [sb(f"xT_lo{i}", [P, DK, S], F32R) for i in range(2)]
        qk = [sb(f"qk{i}", [P, 2, G, 2, S], F32R) for i in range(2)]
        stack = [sb(f"stack{i}", [STACK, H, 2, S], F32R) for i in range(2)]
        v_aug = [sb(f"v_aug{i}", [P, QC, H, 32]) for i in range(2)]
        negm = sb("negm", [P, QC, H])
        mT_hi = [sb(f"mT_hi{i}", [HH, S], F32R) for i in range(2)]
        mT_lo = [sb(f"mT_lo{i}", [HH, S], F32R) for i in range(2)]
        probs = sb("probs", [P, RING, QC, S])
        u_sb = sb("u_sb", [P, QUADS, S])
        rec = sb("rec", [P, QC, H])
        attn = sb("attn", [P, QC, D])
        aT_hi = sb("aT_hi", [P, DK, S], F32R)
        aT_lo = sb("aT_lo", [P, DK, S], F32R)
        y = sb("y", [P, QC, D])
        stats = sb("stats", [P, QC, 6])
        mv = sb("mv", [P, QC, 2])
        veps = sb("veps", [P, QC])
        rstd = sb("rstd", [P, QC])
        x1 = sb("x1", [P, QC, D])
        nmean = sb("nmean", [P, QC])
        shift = sb("shift", [P, QC])
        x1T_hi = sb("x1T_hi", [P, DK, S], F32R)
        x1T_lo = sb("x1T_lo", [P, DK, S], F32R)
        lg = sb("lg", [P, QC, NE])
        mx = sb("mx", [P, QC, NE])
        ix = sb("ix", [P, QC, NE], U32)
        ixf = sb("ixf", [P, QC, TOPK])
        hot = sb("hot", [P, QC, TOPK, NE])
        mask = sb("mask", [P, QC, NE], BF16)
        seen = [sb(f"seen{i}", [P, NE], BF16) for i in range(2)]
        seen_t = sb("seen_t", [P, NE], BF16)
        dmx = sb("dmx", [P, QC, NE])
        ex = sb("ex", [P, QC, NE])
        zsum = sb("zsum", [P, QC])
        den = sb("den", [P, QC])
        den2 = sb("den2", [P, QC])
        over = sb("over", [P, QC, NE])
        slot = sb("slot", [P, QC, NE])
        slot_b = sb("slot_b", [P, QC, NE])
        pick = sb("pick", [P, QC, TOPK, NE])
        dest_f = sb("dest_f", [P, QC, TOPK])
        dest = [sb(f"dest{i}", [P, QC * TOPK], I32) for i in range(2)]
        item = [sb(f"item{i}", [P, QC * TOPK, 2], I32) for i in range(2)]

        consts_ready, zeros_ready, filled = sem("consts_ready"), sem("zeros_ready"), sem("filled")
        ident0, wT_ready, wT_hi_done = sem("ident0"), sem("wT_ready"), sem("wT_hi_done")
        w_loaded = [sem(f"w_loaded{w}") for w in range(4)]
        wT_lo_done, b1_loaded, gate_loaded, b1T_ready, b1T_done = (
            sem("wT_lo_done"), sem("b1_loaded"), sem("gate_loaded"), sem("b1T_ready"), sem("b1T_done"))
        x_loaded = [sem(f"x_loaded{i}") for i in range(2)]
        xres_loaded = [sem(f"xres_loaded{i}") for i in range(2)]
        xT_ready, xT_copied, xT_hi_done, xT_lo_done = sem("xT_ready"), sem("xT_copied"), sem("xT_hi_done"), sem("xT_lo_done")
        q_ready, k_ready, v_ready, v_done = sem("q_ready"), sem("k_ready"), sem("v_ready"), sem("v_done")
        qk_ready = (q_ready, k_ready)
        qk_hi_done = (sem("q_hi_done"), sem("k_hi_done"))
        qk_lo_done = (sem("q_lo_done"), sem("k_lo_done"))
        stacked = [sem(f"stacked{i}") for i in range(2)]
        s_ready, max_done = sem("s_ready"), sem("max_done")
        mT_ready, mT_hi_done, mT_lo_done = ([sem(f"{n}{i}") for i in range(2)] for n in ("mT_ready", "mT_hi_done", "mT_lo_done"))
        shift_in = [sem(f"shift_in{i}") for i in range(2)]
        st_ready, exp_done = sem("st_ready"), sem("exp_done")
        pv_ready, u_done = sem("pv_ready"), sem("u_done")
        uT_ready, rec_done, attn_done = sem("uT_ready"), sem("rec_done"), sem("attn_done")
        aT_ready, aT_hi_done, aT_lo_done = sem("aT_ready"), sem("aT_hi_done"), sem("aT_lo_done")
        o_ready, y_done, stats_done, mv_done = sem("o_ready"), sem("y_done"), sem("stats_done"), sem("mv_done")
        veps_done, rstd_done, x1_done = sem("veps_done"), sem("rstd_done"), sem("x1_done")
        x1_stored = [sem(f"x1_stored{i}") for i in range(2)]
        nmean_done, shift_done = sem("nmean_done"), sem("shift_done")
        x1T_ready, x1T_hi_done, x1T_lo_done = sem("x1T_ready"), sem("x1T_hi_done"), sem("x1T_lo_done")
        gate_done, lg_ready, lg_done = sem("gate_done"), sem("lg_ready"), sem("lg_done")
        mx_done, ix_done, ixf_done, hot_done = sem("mx_done"), sem("ix_done"), sem("ixf_done"), sem("hot_done")
        mask_done, seen_mid, seen_done, pos_ready = sem("mask_done"), sem("seen_mid"), sem("seen_done"), sem("pos_ready")
        dmx_done, ex_done, zsum_done, den_done = sem("dmx_done"), sem("ex_done"), sem("zsum_done"), sem("den_done")
        den2_done, w0_done, item_done, tok_done = sem("den2_done"), sem("w0_done"), sem("item_done"), sem("tok_done")
        over_done, slot_done, slotb_done, pick_done = sem("over_done"), sem("slot_done"), sem("slotb_done"), sem("pick_done")
        destf_done, dest_done = sem("destf_done"), sem("dest_done")
        ident_ready, ones_ready, v_ones = sem("ident_ready"), sem("ones_ready"), sem("v_ones")
        queries_cleared = [sem(f"queries_cleared{i}") for i in range(2)]
        keys_cleared = [sem(f"keys_cleared{i}") for i in range(2)]
        keys_ready = [sem(f"keys_ready{i}") for i in range(2)]
        sp_passed, pool_passed, dve_passed = sem("sp_passed"), sem("pool_passed"), sem("dve_passed")
        listed = [sem(f"listed{i}") for i in range(2)]

        BQ, BD, BU, BA, BB, BC = (0, 1), (2, 3), 4, 5, 6, 7

        def bank(i, **kw):
            return banks[i][:, :].rearrange("p (a b) -> p a b", **kw)

        def from_bank(w, c):
            t = banks[4 + w][:, c * D:c * D + D]
            return t.rearrange("p (x h r) -> p x h r", h=HH // 2, r=R) if w < 2 else t

        def by_feature(t, w, c):
            return t[:, w, c].rearrange("p (x r h) -> p x h r", h=HH // 2, r=R) if w < 2 else t[:, w, c]

        block = ctx.enter_context(nc.Block())

        first, last = -1, NB + 2

        def pipeline(engine, step):
            lo, hi = 2, (NB - 2) // 2
            for s in range(first, 2 * lo):
                step(Seq(0, s), s)
            with engine.Fori(lo, hi) as i:
                for j in range(2):
                    step(Seq(i, j), None)
            for s in range(2 * hi, last + 1):
                step(Seq(s // 2, s % 2), s)

        def stage(s, num, lag):
            if num is not None:
                n = num - lag
                return Seq(n // 2, n % 2) if 0 <= n < NB else None
            return Seq(s.half, s.parity - lag)

        @block.sync
        def _(sp):
            for w, name in enumerate(("wq_d", "wk_d", "wv_d", "wo_d")):
                sp.dma_start(w_raw[:, w], g[name].rearrange("(c p) d -> p c d", p=P)).then_inc(w_loaded[w], 16)
                if w == 0:
                    sp.dma_start(x_sb[0][:, :, :], x_v[0]).then_inc(x_loaded[0], 16)
            sp.dma_start(b1_raw[:, :], g["b1_d"].rearrange("e (f p) -> (e f) p", p=P)).then_inc(b1_loaded, 16)
            sp.dma_start(gate_raw[:, :, :], g["gw_d"].rearrange("(c p) e -> p c e", p=P)).then_inc(gate_loaded, 16)
            def fill_dram():
                sp.wait_ge(zeros_ready, 2)
                sp.dma_start(list_v, fill[:, :, :, :].rearrange("p e j w -> p e (j w)")).then_inc(filled, 16)
                sp.dma_start(x1_d[T:T + TRASH, :], zrow[:, :]).then_inc(filled, 16)
                sp.dma_start(acc_d[T:T + TRASH, :], zrow[:, :]).then_inc(filled, 16)
                sp.dma_start(g["w1_raw"][:, :, :], g["w1_d"][0].rearrange("(c p) f -> p c f", p=P)).then_inc(g["w1_loaded"], 16)
                sp.dma_start(g["w2_raw"][:, :, :], g["w2_d"][0].rearrange("(f p) d -> p f d", p=P)).then_inc(g["w2_loaded"], 16)

            def shift_rows(b, half):
                sp.wait_ge(mT_hi_done[half], b.n + 1)
                sp.wait_ge(mT_lo_done[half], b.n + 1)
                heads = slice(HH * half, HH * (half + 1))
                for row, src in ((ROW_M, mT_hi[half]), (ROW_M + 1, mT_lo[half])):
                    sp.dma_start(stack[b.parity][row:row + 1, heads, 0, :].bitcast(F32), src[:, :].bitcast(F32)).then_inc(shift_in[half], 16)

            def stack_rows(a, half):
                src = qk[a.parity][P // 2 * half:P // 2 * (half + 1)].bitcast(F32)
                dst = stack[a.parity][:, HH * half:HH * (half + 1)].bitcast(F32)
                pair = src.rearrange("p c g w t -> p c (g w t)")
                both = dst.rearrange("r h w t -> r (h w t)")
                for out, in_ in ((dst[0:R, :, 0, :], src[:, 1, :, 0, :]), (dst[0:R, :, 1, :], src[:, 0, :, 1, :]),
                                 (both[ROW_B:ROW_B + R], pair[:, 0, :]), (both[ROW_C:ROW_C + R], pair[:, 1, :])):
                    sp.dma_start(out, in_).then_inc(stacked[half], 16)

            def step(s, num):
                a, b, d, e = (stage(s, num, lag) for lag in (-1, 0, 1, 2))
                nxt = stage(s, num, -2)
                if nxt:
                    if num is None or num >= 0:
                        sp.wait_ge(xT_ready, nxt.n - 1)
                    sp.dma_start(x_sb[nxt.parity][:, :, :], x_v[nxt.n]).then_inc(x_loaded[nxt.parity], 16)
                if e:
                    if num is None or num >= 4:
                        sp.wait_ge(y_done, e.n - 1)
                    sp.dma_start(xres[e.parity][:, :, :], x_v[e.n]).then_inc(xres_loaded[e.parity], 16)
                if d:
                    shift_rows(d, 1)
                if a:
                    if num in (-1, 0):
                        sp.wait_ge(keys_cleared[a.parity], 1)
                        sp.wait_ge(queries_cleared[a.parity], 1)
                    for w in range(2):
                        sp.wait_ge(qk_hi_done[w], a.n + 1)
                        sp.wait_ge(qk_lo_done[w], a.n + 1)
                for half in range(2):
                    if a:
                        if b:
                            wait_apart(sp, sp_passed, (s_ready, H * b.n + HH * half + 1))
                        if num is None or num >= 1:
                            wait_apart(sp, sp_passed, (st_ready, H * (a.n - 2) + HH * (half + 1)))
                        stack_rows(a, half)
                        if num == 0 and half == 1:
                            sp.wait_ge(keys_ready[0], 1)
                            sp.dma_start(stack[1][ROW_M:STACK, :, 1, :].bitcast(F32),
                                         stack[0][ROW_M:STACK, :, 1, :].bitcast(F32)).then_inc(keys_ready[1], 16)
                            fill_dram()
                    if half == 0 and b:
                        shift_rows(b, 0)
                    if half == 0 and e:
                        sp.wait_ge(x1_done, e.n + 1)
                        sp.dma_start(x1_v[e.n], x1[:, :, :]).then_inc(x1_stored[e.parity], 16)
                        sp.dma_start(acc_v[e.n], x1[:, :, :]).then_inc(x1_stored[e.parity], 16)

            pipeline(sp, step)
            for i in range(2):
                sp.wait_ge(x1_stored[i], 32 * (NB // 2))
                sp.wait_ge(listed[i], 16 * QC * TOPK * (NB // 2))
            sp.wait_ge(filled, 48)

        @block.gpsimd
        def _(pool):
            nc.gpsimd.memset(ident[:, :], 0.0).then_inc(ident0, 1)
            pool.wait_ge(ident0, 1)
            nc.gpsimd.affine_select(out=ident[:, :], in_=ident[:, :], compare_op=ALU.not_equal, fill=1.0,
                                    base=0, pattern=[[-1, P]], channel_multiplier=1).then_inc(ident_ready, 1)
            nc.gpsimd.memset(stack[0][:, :, 0, :].bitcast(F32), 0.0).then_inc(queries_cleared[0], 1)
            nc.gpsimd.memset(tri[:, :], 1.0).then_inc(ident0, 1)
            nc.gpsimd.memset(ones[:, :], 1.0).then_inc(consts_ready, 1)
            nc.gpsimd.memset(fill[:, :, :, :], 0).then_inc(ident0, 1)
            nc.gpsimd.memset(zrow[:, :], 0.0).then_inc(zeros_ready, 1)
            pool.wait_ge(ident0, 3)
            nc.gpsimd.affine_select(out=tri[:, :], in_=tri[:, :], compare_op=ALU.is_gt, fill=0.0,
                                    base=0, pattern=[[1, P]], channel_multiplier=-1).then_inc(consts_ready, 1)
            nc.gpsimd.iota(fill[:, :, :, 0], pattern=[[0, NE], [0, BLK]], base=T, channel_multiplier=1).then_inc(zeros_ready, 1)
            nc.gpsimd.iota(iota_e[:, :], pattern=[[1, NE]], base=0, channel_multiplier=0,
                           allow_small_or_imprecise_dtypes=True).then_inc(consts_ready, 1)
            nc.gpsimd.iota(slot0[:, :], pattern=[[CAP, NE]], base=0, channel_multiplier=0,
                           allow_small_or_imprecise_dtypes=True).then_inc(consts_ready, 1)
            nc.gpsimd.iota(tok[:, :], pattern=[[P, QC]], base=0, channel_multiplier=1,
                           allow_small_or_imprecise_dtypes=True).then_inc(tok_done, 1)
            nc.gpsimd.memset(expo[:, :], -0.5).then_inc(consts_ready, 1)
            nc.gpsimd.memset(seen[0][:, :], 0.0).then_inc(consts_ready, 1)
            pool.wait_ge(consts_ready, POOL_CONSTS)

            def step(s, num):
                a, b, d, e, f = (stage(s, num, lag) for lag in (-1, 0, 1, 2, 3))
                if a:
                    used = ((v_ready, a.n - 1),) if num is None or num >= 1 else ()
                    wait_apart(pool, pool_passed, (xT_copied, a.n + 1), *used)
                    nc.gpsimd.tensor_copy(xT_hi[a.parity][:, :, :], xT_f[:, :, :]).then_inc(xT_hi_done, 1)
                    pool.wait_ge(xT_hi_done, a.n + 1)
                    nc.gpsimd.tensor_tensor(xT_lo[a.parity][:, :, :], xT_f[:, :, :], xT_hi[a.parity][:, :, :].bitcast(F32),
                                            ALU.subtract).then_inc(xT_lo_done, 1)
                if num == first:
                    nc.gpsimd.memset(stack[1][:, :, 0, :].bitcast(F32), 0.0).then_inc(queries_cleared[1], 1)
                if e:
                    wait_apart(pool, pool_passed, (mv_done, e.n + 1), (x1_done, e.n))
                    nc.gpsimd.tensor_scalar(veps[:, :], mv[:, :, 1], EPS, None, ALU.add).then_inc(veps_done, 1)
                    nc.gpsimd.tensor_scalar(nmean[:, :], mv[:, :, 0], -1.0, None, ALU.mult).then_inc(nmean_done, 1)
                    pool.wait_ge(veps_done, e.n + 1)
                    nc.gpsimd.tensor_tensor(rstd[:, :], veps[:, :], expo[:, :], ALU.pow).then_inc(rstd_done, 1)
                    pool.wait_ge(nmean_done, e.n + 1)
                    pool.wait_ge(rstd_done, e.n + 1)
                    nc.gpsimd.tensor_tensor(shift[:, :], nmean[:, :], rstd[:, :], ALU.mult).then_inc(shift_done, 1)
                if f:
                    if num == 3:
                        pool.wait_ge(filled, 48)
                    wait_apart(pool, pool_passed, (dest_done, f.n + 1), (item_done, f.n + 1))
                    for n in range(QC * TOPK):
                        nc.gpsimd.indirect_dma_start(
                            out=list_d, out_offset=bass.IndirectOffsetOnAxis(ap=dest[f.parity][:, n:n + 1], axis=0),
                            in_=item[f.parity][:, n, :], in_offset=None, bounds_check=NE * CAP - 1,
                            oob_is_err=False).then_inc(listed[f.parity], 16)
            pipeline(pool, step)

        @block.scalar
        def _(act):
            act.wait_ge(ones_ready, 1)
            nc.scalar.activation(stack[0][ROW_M:STACK, :, 1, :], ones_f[ROW_M:STACK, :].unsqueeze(1).to_broadcast([STACK - ROW_M, H, S]),
                                 ACT.Copy).then_inc(keys_ready[0], 1)
            for w in range(4):
                act.wait_ge(wT_ready, w + 1)
                for c in range(DK):
                    ins = nc.scalar.activation(by_feature(wT_hi, w, c), from_bank(w, c), ACT.Copy)
                ins.then_inc(wT_hi_done, 1)
            act.wait_ge(b1T_ready, 1)
            nc.scalar.activation(b1T[:, :], banks[0][:, 0:NE * FT], ACT.Copy).then_inc(b1T_done, 1)
            act.wait_ge(gate_loaded, 16)
            nc.scalar.activation(gate_hi[:, :, :, :], gate_raw[:, :, :].unsqueeze(2).to_broadcast([P, DK, GW // NE, NE]),
                                 ACT.Copy).then_inc(gate_done, 1)

            def u_copy(b, half):
                act.wait_ge(pv_ready, QUADS * b.n + 2 * half + 2)
                act.wait_ge(uT_ready, b.n)
                nc.scalar.activation(u_sb[:, 2 * half:2 * half + 2, :], bank(BU, a=2), ACT.Copy).then_inc(u_done, 1)

            def mT_copy(b, half):
                act.wait_ge(mT_ready[half], b.n + 1)
                act.wait_ge(shift_in[half], 32 * b.n)
                act.wait_ge(mT_lo_done[half], b.n)
                nc.scalar.activation(mT_hi[half][:, :], banks[BB][0:HH, 0:S], ACT.Copy).then_inc(mT_hi_done[half], 1)

            def step(s, num):
                a, b, d, e, f = (stage(s, num, lag) for lag in (-1, 0, 1, 2, 3))
                if e:
                    u_copy(e, 1)
                for k in range(H):
                    if k == 1 and a:
                        act.wait_ge(xT_ready, a.n + 1)
                        act.wait_ge(xT_lo_done, a.n)
                        nc.scalar.activation(xT_f[:, :, :], bank(BC, a=DK), ACT.Copy).then_inc(xT_copied, 1)
                    if k == 2 and d:
                        mT_copy(d, 1)
                    if k == 3 and b:
                        act.wait_ge(v_ready, b.n + 1)
                        if num is None or num >= 2:
                            act.wait_ge(pv_ready, QUADS * (b.n - 1))
                        for c in range(QC):
                            dst = v_aug[b.parity][:, c, :, 0:R].rearrange("p (h g) r -> p g h r", g=G)
                            src = banks[BA][:, c * D:c * D + D].rearrange("p (g h r) -> p g h r", g=G, r=R)
                            ins = nc.scalar.activation(dst, src, ACT.Copy)
                        ins.then_inc(v_done, 1)
                    if k in (6, 9) and a:
                        w = (6, 9).index(k)
                        act.wait_ge(qk_ready[w], a.n + 1)
                        if num is None or num >= 1:
                            act.wait_ge(s_ready, H * (a.n - 1))
                            act.wait_ge(qk_lo_done[w], a.n - 1)
                        nc.scalar.activation(qk[a.parity][:, 1 - w, :, w, :], bank(BC, a=G), ACT.Copy).then_inc(qk_hi_done[w], 1)
                    if k == 8 and e:
                        act.wait_ge(aT_ready, e.n + 1)
                        act.wait_ge(o_ready, e.n)
                        act.wait_ge(aT_lo_done, e.n)
                        nc.scalar.activation(aT_hi[:, :, :], bank(BB, a=DK), ACT.Copy).then_inc(aT_hi_done, 1)
                    if k == 11 and d:
                        u_copy(d, 0)
                    if k == 12 and b:
                        mT_copy(b, 0)
                    if k == 13 and e:
                        act.wait_ge(shift_done, e.n + 1)
                        act.wait_ge(x1T_ready, e.n)
                        if num is None or num >= 3:
                            act.wait_ge(x1_stored[1 - e.parity], 32 * (e.half + e.parity))
                        for c in range(QC):
                            ins = nc.scalar.activation(x1[:, c, :], y[:, c, :], ACT.Identity, bias=shift[:, c:c + 1],
                                                       scale=rstd[:, c:c + 1])
                        ins.then_inc(x1_done, 1)
                    if k == 15 and e:
                        act.wait_ge(x1T_ready, e.n + 1)
                        act.wait_ge(lg_ready, e.n)
                        act.wait_ge(x1T_lo_done, e.n)
                        nc.scalar.activation(x1T_hi[:, :, :], bank(BA, a=DK), ACT.Copy).then_inc(x1T_hi_done, 1)
                    if d:
                        act.wait_ge(st_ready, H * d.n + k + 1)
                        if num is None or num >= 2 or k >= RING:
                            act.wait_ge(pv_ready, QUADS * d.n + k // 4 - 1)
                        nc.scalar.activation(probs[:, k % RING], bank(BD[k % 2], a=QC), ACT.Exp,
                                             scale=SCALE).then_inc(exp_done, 1)
                    if k == 9 and f:
                        act.wait_ge(dmx_done, f.n + 1)
                        act.wait_ge(item_done, f.n)
                        nc.scalar.activation(ex[:, :, :], dmx[:, :, :], ACT.Exp).then_inc(ex_done, 1)

            pipeline(act, step)

        @block.vector
        def _(dve):
            nc.vector.memset(ones_f[:, :], 1.0).then_inc(ones_ready, 1)
            nc.vector.memset(stack[0][0:ROW_M, :, 1, :].bitcast(F32), 0.0).then_inc(keys_cleared[0], 1)
            for w in range(4):
                dve.wait_ge(wT_hi_done, w + 1)
                for c in range(DK):
                    ins = nc.vector.tensor_tensor(by_feature(wT_lo, w, c), from_bank(w, c),
                                                  by_feature(wT_hi, w, c).bitcast(F32), ALU.subtract)
                ins.then_inc(wT_lo_done, 1)
            dve.wait_ge(gate_done, 1)
            nc.vector.tensor_tensor(gate_lo[:, :, :, :], gate_raw[:, :, :].unsqueeze(2).to_broadcast([P, DK, GW // NE, NE]),
                                    gate_hi[:, :, :, :].bitcast(F32), ALU.subtract).then_inc(gate_done, 1)
            for i in range(2):
                nc.vector.memset(v_aug[i][:, :, :, R:2 * R], 1.0).then_inc(v_ones, 1)
            nc.vector.memset(stack[1][0:ROW_M, :, 1, :].bitcast(F32), 0.0).then_inc(keys_cleared[1], 1)
            dve.wait_ge(consts_ready, POOL_CONSTS)

            def mT_rest(b, half):
                dve.wait_ge(mT_hi_done[half], b.n + 1)
                nc.vector.tensor_tensor(mT_lo[half][:, :], banks[BB][0:HH, 0:S], mT_hi[half][:, :].bitcast(F32),
                                        ALU.subtract).then_inc(mT_lo_done[half], 1)

            def step(s, num):
                a, b, d, e, f = (stage(s, num, lag) for lag in (-1, 0, 1, 2, 3))
                for k in range(H):
                    if b:
                        dve.wait_ge(s_ready, H * b.n + k + 1)
                        if k % HH == 0:
                            dve.wait_ge(mT_ready[k // HH], b.n)
                        nc.vector.tensor_reduce(negm[:, :, k], bank(BQ[k % 2], a=QC), X, ALU.max,
                                                negate=True).then_inc(max_done, 1)
                    if k == 2 and d:
                        mT_rest(d, 1)
                    if k == 3 and f:
                        logits(f)
                    if k == 4 and e:
                        dve.wait_ge(uT_ready, e.n + 1)
                        dve.wait_ge(attn_done, e.n)
                        for c in range(QC):
                            sums = banks[(BA, BB)[c]][:, :].rearrange("p (u r) -> p u r", r=32)[:, :, R]
                            ins = nc.vector.reciprocal(rec[:, c, :], sums)
                        ins.then_inc(rec_done, 1)
                        dve.wait_ge(rec_done, e.n + 1)
                        dve.wait_ge(aT_ready, e.n)
                        for c in range(QC):
                            dst = attn[:, c, :].rearrange("p (g h r) -> p h g r", g=G, r=R)
                            src = banks[(BA, BB)[c]][:, :].rearrange("p (h g r) -> p h g r", g=G, r=32)[:, :, :, 0:R]
                            rc = rec[:, c, :].rearrange("p (h g) -> p h g", g=G).unsqueeze(3).to_broadcast([P, HH, G, R])
                            ins = nc.vector.tensor_tensor(dst, src, rc, ALU.mult)
                        ins.then_inc(attn_done, 1)
                    if k == 5 and f:
                        best_two(f)
                    if k in (6, 9) and a:
                        w = (6, 9).index(k)
                        dve.wait_ge(qk_hi_done[w], a.n + 1)
                        nc.vector.tensor_tensor(qk[a.parity][:, w, :, w, :], bank(BC, a=G),
                                                qk[a.parity][:, 1 - w, :, w, :].bitcast(F32), ALU.subtract).then_inc(qk_lo_done[w], 1)
                    if k == 7 and f:
                        one_hot(f)
                    if k == 8 and e:
                        dve.wait_ge(aT_hi_done, e.n + 1)
                        nc.vector.tensor_tensor(aT_lo[:, :, :], bank(BB, a=DK), aT_hi[:, :, :].bitcast(F32),
                                                ALU.subtract).then_inc(aT_lo_done, 1)
                    if k == 9 and f:
                        count_rows(f)
                    if k == 10 and e:
                        dve.wait_ge(o_ready, e.n + 1)
                        dve.wait_ge(xres_loaded[e.parity], 16 * (e.half + 1))
                        dve.wait_ge(x1_done, e.n)
                        nc.vector.tensor_tensor(y[:, :, :], bank(BA, a=QC), xres[e.parity][:, :, :], ALU.add).then_inc(y_done, 1)
                        dve.wait_ge(y_done, e.n + 1)
                        for c in range(QC):
                            nc.vector.bn_stats(stats[:, c, :], y[:, c, :]).then_inc(stats_done, 1)
                    if k == 11 and e:
                        wait_apart(dve, dve_passed, (stats_done, QC * e.n + QC), (shift_done, e.n))
                        for c in range(QC):
                            ins = nc.vector.bn_aggr(mv[:, c, :], stats[:, c, :])
                        ins.then_inc(mv_done, 1)
                    if k == 12 and b:
                        mT_rest(b, 0)
                    if k == 13 and f:
                        slots(f, num)
                    if k == 14 and f:
                        weights(f)
                    if k == 15 and e:
                        dve.wait_ge(x1T_hi_done, e.n + 1)
                        nc.vector.tensor_tensor(x1T_lo[:, :, :], bank(BA, a=DK), x1T_hi[:, :, :].bitcast(F32),
                                                ALU.subtract).then_inc(x1T_lo_done, 1)

            def logits(f):
                dve.wait_ge(lg_ready, f.n + 1)
                dve.wait_ge(ix_done, f.n)
                nc.vector.tensor_copy(lg[:, :, :], banks[BC][:, 0:QC * GW].rearrange("p (c e) -> p c e", c=QC)[:, :, 0:NE]).then_inc(lg_done, 1)

            def best_two(f):
                wait_apart(dve, dve_passed, (lg_done, f.n + 1), (dmx_done, f.n))
                for c in range(QC):
                    ins = nc.vector.max(mx[:, c, :], lg[:, c, :])
                ins.then_inc(mx_done, 1)
                wait_apart(dve, dve_passed, (mx_done, f.n + 1), (ixf_done, f.n))
                for c in range(QC):
                    ins = nc.vector.max_index(ix[:, c, :], mx[:, c, :], lg[:, c, :])
                ins.then_inc(ix_done, 1)

            def one_hot(f):
                dve.wait_ge(ex_done, f.n)
                nc.vector.tensor_tensor(dmx[:, :, :], mx[:, :, :], mx[:, :, 0:1].to_broadcast([P, QC, NE]),
                                        ALU.subtract).then_inc(dmx_done, 1)
                dve.wait_ge(ix_done, f.n + 1)
                dve.wait_ge(hot_done, f.n)
                nc.vector.tensor_copy(ixf[:, :, :], ix[:, :, 0:TOPK]).then_inc(ixf_done, 1)
                dve.wait_ge(ixf_done, f.n + 1)
                dve.wait_ge(pick_done, QC * f.n)
                for c in range(QC):
                    ins = nc.vector.tensor_tensor(hot[:, c], iota_e[:, :].unsqueeze(1).to_broadcast([P, TOPK, NE]),
                                                  ixf[:, c, :].unsqueeze(2).to_broadcast([P, TOPK, NE]), ALU.is_equal)
                ins.then_inc(hot_done, 1)

            def count_rows(f):
                dve.wait_ge(hot_done, f.n + 1)
                dve.wait_ge(pos_ready, f.n)
                dve.wait_ge(seen_done, f.n)
                nc.vector.tensor_tensor(mask[:, :, :], hot[:, :, 0, :], hot[:, :, 1, :], ALU.add).then_inc(mask_done, 1)
                dve.wait_ge(mask_done, f.n + 1)
                nc.vector.tensor_tensor(seen_t[:, :], seen[f.parity][:, :], mask[:, 0, :], ALU.add).then_inc(seen_mid, 1)
                dve.wait_ge(seen_mid, f.n + 1)
                nc.vector.tensor_tensor(seen[1 - f.parity][:, :], seen_t[:, :], mask[:, 1, :], ALU.add).then_inc(seen_done, 1)

            def slots(f, num):
                dve.wait_ge(pos_ready, f.n + 1)
                pos = banks[BC][:, 0:QC * NE].rearrange("p (c e) -> p c e", c=QC)
                dve.wait_ge(slotb_done, f.n)
                nc.vector.tensor_scalar(over[:, :, :], pos, float(CAP), float(NE * CAP), ALU.is_ge, ALU.mult).then_inc(over_done, 1)
                nc.vector.tensor_tensor(slot[:, :, :], pos, slot0[:, :].unsqueeze(1).to_broadcast([P, QC, NE]), ALU.add).then_inc(slot_done, 1)
                dve.wait_ge(over_done, f.n + 1)
                dve.wait_ge(slot_done, f.n + 1)
                dve.wait_ge(pick_done, QC * f.n)
                nc.vector.tensor_tensor(slot_b[:, :, :], slot[:, :, :], over[:, :, :], ALU.add).then_inc(slotb_done, 1)
                dve.wait_ge(slotb_done, f.n + 1)
                dve.wait_ge(destf_done, f.n)
                for c in range(QC):
                    nc.vector.tensor_tensor(pick[:, c], hot[:, c], slot_b[:, c, :].unsqueeze(1).to_broadcast([P, TOPK, NE]),
                                            ALU.mult).then_inc(pick_done, 1)
                dve.wait_ge(pick_done, QC * f.n + QC)
                dve.wait_ge(dest_done, f.n)
                nc.vector.tensor_reduce(dest_f[:, :, :], pick[:, :, :, :], X, ALU.add).then_inc(destf_done, 1)
                dve.wait_ge(destf_done, f.n + 1)
                if num is None or num >= 5:
                    dve.wait_ge(listed[f.parity], 16 * QC * TOPK * f.half)
                nc.vector.tensor_copy(dest[f.parity][:, :].rearrange("p (c k) -> p c k", c=QC), dest_f[:, :, :]).then_inc(dest_done, 1)

            def weights(f):
                dve.wait_ge(ex_done, f.n + 1)
                nc.vector.tensor_reduce(zsum[:, :], ex[:, :, :], X, ALU.add).then_inc(zsum_done, 1)
                dve.wait_ge(zsum_done, f.n + 1)
                nc.vector.tensor_scalar(den[:, :], zsum[:, :], 1e-8, 1.0, ALU.mult, ALU.add).then_inc(den_done, 1)
                dve.wait_ge(den_done, f.n + 1)
                nc.vector.tensor_tensor(den2[:, :], den[:, :], ex[:, :, 1], ALU.add).then_inc(den2_done, 1)
                dve.wait_ge(den2_done, f.n + 1)
                nc.vector.reciprocal(den[:, :], den2[:, :]).then_inc(w0_done, 1)
                dve.wait_ge(w0_done, f.n + 1)
                it = item[f.parity][:, :, :].rearrange("p (c k) w -> p c k w", c=QC)
                nc.vector.tensor_tensor(it[:, :, :, 1].bitcast(F32), ex[:, :, 0:TOPK], den[:, :].unsqueeze(2).to_broadcast([P, QC, TOPK]), ALU.mult)
                dve.wait_ge(tok_done, f.n + 1)
                nc.vector.tensor_copy(it[:, :, :, 0], tok[:, :].unsqueeze(2).to_broadcast([P, QC, TOPK])).then_inc(item_done, 1)
                dve.wait_ge(item_done, f.n + 1)
                nc.vector.tensor_scalar(tok[:, :], tok[:, :], float(S), None, ALU.add).then_inc(tok_done, 1)

            pipeline(dve, step)

        @block.tensor
        def _(pe):
            pe.wait_ge(ident_ready, 1)
            for w in range(4):
                pe.wait_ge(w_loaded[w], 16)
                for c in range(DK):
                    for r in range(QC):
                        ins = nc.tensor.transpose(banks[4 + w][:, c * D + r * P:c * D + r * P + P],
                                                  w_raw[:, w, r, c * P:c * P + P], ident[:, :])
                ins.then_inc(wT_ready, 1)
            pe.wait_ge(b1_loaded, 16)
            nc.tensor.transpose(banks[0][:, 0:NE * FT], b1_raw[:, :], ident[0:NE * FT, 0:NE * FT]).then_inc(b1T_ready, 1)
            pe.wait_ge(wT_hi_done, 4)
            pe.wait_ge(wT_lo_done, 4)

            def product(out, pairs):
                for n, (l, r) in enumerate(pairs):
                    ins = nc.tensor.matmul(out, l, r, start=(n == 0), stop=(n == len(pairs) - 1))
                return ins

            def split_pairs(l_hi, l_lo, r_hi, r_lo):
                return [p for c in range(DK) for p in ((l_hi(c), r_hi(c)), (l_hi(c), r_lo(c)), (l_lo(c), r_hi(c)))]

            def pv(b, t):
                pe.wait_ge(exp_done, H * b.n + 4 * t + 4)
                if t == 0:
                    pe.wait_ge(v_done, b.n + 1)
                    if isinstance(b.n, int) and b.n < 2:
                        pe.wait_ge(v_ones, b.n + 1)
                if t % 2 == 0:
                    pe.wait_ge(u_done, 2 * b.n + t // 2)
                for c in range(QC):
                    for j in range(4):
                        u = 4 * t + j
                        out = banks[BU][32 * j:32 * j + 32, (t % 2) * S:(t % 2) * S + S]
                        ins = nc.tensor.matmul(out, v_aug[b.parity][:, c, u, :], probs[:, u % RING, c, :],
                                               start=(c == 0), stop=(c == QC - 1), tile_position=(0, 32 * j))
                ins.then_inc(pv_ready, 1)

            def mT(b, half):
                pe.wait_ge(max_done, H * b.n + HH * half + HH)
                for c in range(QC):
                    ins = nc.tensor.transpose(banks[BB][0:HH, c * P:c * P + P], negm[:, c, HH * half:HH * half + HH], ident[:, :])
                ins.then_inc(mT_ready[half], 1)

            def transpose4(bk, src):
                for c in range(DK):
                    for r in range(QC):
                        ins = nc.tensor.transpose(banks[bk][:, c * S + r * P:c * S + r * P + P], src[:, r, c * P:c * P + P], ident[:, :])
                return ins

            def project(w, a):
                hi, lo = xT_hi[a.parity], xT_lo[a.parity]
                for o in range(G):
                    ins = product(banks[BC][:, o * S:o * S + S], split_pairs(
                        lambda i: wT_hi[:, w, i, o * P:o * P + P], lambda i: wT_lo[:, w, i, o * P:o * P + P],
                        lambda i: hi[:, i, :], lambda i: lo[:, i, :]))
                ins.then_inc(qk_ready[w], 1)

            def by_row_tile(src_hi, src_lo, w):
                for c in range(QC):
                    ins = product(banks[BA][:, c * D:c * D + D], split_pairs(
                        lambda i: src_hi[:, i, c * P:c * P + P], lambda i: src_lo[:, i, c * P:c * P + P],
                        lambda i: wT_hi[:, w, i, :], lambda i: wT_lo[:, w, i, :]))
                return ins

            def step(s, num):
                a, b, d, e, f = (stage(s, num, lag) for lag in (-1, 0, 1, 2, 3))
                if e:
                    pv(e, QUADS - 1)
                for k in range(H):
                    if k == 0 and a:
                        pe.wait_ge(x_loaded[a.parity], 16 * (a.half + 1))
                        pe.wait_ge(qk_lo_done[1], a.n)
                        if num is None or num >= 4:
                            pe.wait_ge(slotb_done, f.n)
                        transpose4(BC, x_sb[a.parity]).then_inc(xT_ready, 1)
                    if k == 1 and d:
                        pe.wait_ge(mT_lo_done[0], d.n + 1)
                        mT(d, 1)
                    if k == 2 and b:
                        pe.wait_ge(xT_lo_done, b.n + 1)
                        if f:
                            pe.wait_ge(x1T_lo_done, f.n + 1)
                        else:
                            pe.wait_ge(v_done, b.n)
                        by_row_tile(xT_hi[b.parity], xT_lo[b.parity], 2).then_inc(v_ready, 1)
                    if k == 3 and f:
                        pe.wait_ge(x1T_lo_done, f.n + 1)
                        if num == 3:
                            pe.wait_ge(gate_done, 2)
                        if a:
                            pe.wait_ge(xT_copied, a.n + 1)
                        else:
                            pe.wait_ge(slotb_done, f.n)
                        for c in range(QC):
                            ins = product(banks[BC][:, c * GW:c * GW + GW], split_pairs(
                                lambda i: x1T_hi[:, i, c * P:c * P + P], lambda i: x1T_lo[:, i, c * P:c * P + P],
                                lambda i: gate_hi[:, i, :, :].rearrange("p t e -> p (t e)"),
                                lambda i: gate_lo[:, i, :, :].rearrange("p t e -> p (t e)")))
                        ins.then_inc(lg_ready, 1)
                    if k == 4 and e:
                        pe.wait_ge(u_done, 2 * e.n + 2)
                        if b:
                            pe.wait_ge(v_done, b.n + 1)
                        else:
                            pe.wait_ge(x1T_lo_done, f.n + 1)
                        if d:
                            pe.wait_ge(mT_lo_done[1], d.n + 1)
                        for c in range(QC):
                            for t in range(QUADS):
                                ins = nc.tensor.transpose(banks[(BA, BB)[c]][:, t * P:t * P + P],
                                                          u_sb[:, t, c * P:c * P + P], ident[:, :])
                        ins.then_inc(uT_ready, 1)
                    if k == 5 and a:
                        pe.wait_ge(xT_lo_done, a.n + 1)
                        if f:
                            pe.wait_ge(lg_done, f.n + 1)
                        project(0, a)
                    if k == 7 and e:
                        pe.wait_ge(attn_done, e.n + 1)
                        transpose4(BB, attn).then_inc(aT_ready, 1)
                    if k == 8 and a:
                        pe.wait_ge(qk_lo_done[0], a.n + 1)
                        project(1, a)
                    if k == 10 and e:
                        pe.wait_ge(aT_lo_done, e.n + 1)
                        by_row_tile(aT_hi, aT_lo, 3).then_inc(o_ready, 1)
                    if k == 11 and b:
                        if e:
                            pe.wait_ge(aT_lo_done, e.n + 1)
                        elif d:
                            pe.wait_ge(mT_lo_done[1], d.n + 1)
                        mT(b, 0)
                    if k == 12 and f:
                        pe.wait_ge(seen_done, f.n + 1)
                        if a:
                            pe.wait_ge(qk_lo_done[1], a.n + 1)
                        for c in range(QC):
                            out = banks[BC][:, c * NE:c * NE + NE]
                            nc.tensor.matmul(out, tri[:, :], mask[:, c, :], start=True, stop=False)
                            ins = nc.tensor.matmul(out, ones[:, :], (seen[f.parity], seen_t)[c][:, :], start=False, stop=True)
                        ins.then_inc(pos_ready, 1)
                    if k == 14 and e:
                        pe.wait_ge(x1_done, e.n + 1)
                        transpose4(BA, x1).then_inc(x1T_ready, 1)
                    if b:
                        if k == 0 and num == 0:
                            pe.wait_ge(b1T_done, 1)
                        if k % HH == 0:
                            pe.wait_ge(stacked[k // HH], 64 * (b.n + 1))
                        if num is None or num >= 1 or k >= 2:
                            pe.wait_ge(max_done, H * b.n + k - 1)
                        for c in range(QC):
                            ins = nc.tensor.matmul(banks[BQ[k % 2]][:, c * S:c * S + S],
                                                   stack[b.parity][0:ROW_M, k, 0, c * P:c * P + P],
                                                   stack[b.parity][0:ROW_M, k, 1, :], start=True, stop=True)
                        ins.then_inc(s_ready, 1)
                    if d:
                        if k == 0 and num in (1, 2):
                            pe.wait_ge(keys_ready[d.parity], (1, 16)[d.parity])
                        if k % HH == 0:
                            pe.wait_ge(shift_in[k // HH], 32 * (d.n + 1))
                        if num is None or num >= 2 or k >= 2:
                            pe.wait_ge(exp_done, H * d.n + k - 1)
                        for c in range(QC):
                            ins = nc.tensor.matmul(banks[BD[k % 2]][:, c * S:c * S + S],
                                                   stack[d.parity][:, k, 1, c * P:c * P + P],
                                                   stack[d.parity][:, k, 0, :], start=True, stop=True)
                        ins.then_inc(st_ready, 1)
                        if k % 4 == 2 and k > 4:
                            pv(d, k // 4 - 1)

            pipeline(pe, step)


POOL_CONSTS = 6


def experts(nc, g):
    x1_d, acc_d, list_v, w1_d, w2_d, b2_d = g["x1_d"], g["acc_d"], g["list_v"], g["w1_d"], g["w2_d"], g["b2_d"]
    NE, FT, D, DK, FF, C, BLK, NC, QC = g["NE"], g["FT"], g["D"], g["DK"], g["FF"], g["C"], g["BLK"], g["NC"], g["QC"]
    banks, ident, b1T, w1_raw, w2_raw = g["banks"], g["ident"], g["b1T"], g["w1_raw"], g["w2_raw"]
    w1_loaded, w2_loaded = g["w1_loaded"], g["w2_loaded"]
    AHEAD = 3
    PARTS = 2
    PAIRS = FT // 2
    ctx = ExitStack()
    with ctx:
        def sem(name):
            return ctx.enter_context(nc.semaphore(name))

        def sb(name, shape, dt=F32):
            return ctx.enter_context(nc.sbuf_tensor(name, shape, dt))

        w1_hi, w1_lo = sb("w1_hi", [P, DK, FF], F32R), sb("w1_lo", [P, DK, FF], F32R)
        w2_hi, w2_lo = sb("w2_hi", [P, FT, D], F32R), sb("w2_lo", [P, FT, D], F32R)
        b2_all = sb("b2_all", [P, NE, D])
        lists = sb("lists", [P, NE, BLK, 2], I32)
        meta = [sb(f"meta{c}", [P, QC, 2], I32) for c in range(NC)]
        rows = [sb(f"rows{c}", [P, QC, D]) for c in range(NC)]
        g_hi = [sb(f"g_hi{i}", [P, DK, C], F32R) for i in range(3)]
        g_lo = [sb(f"g_lo{i}", [P, DK, C], F32R) for i in range(3)]
        h = [sb(f"h{i}", [P, 2, C]) for i in range(2)]
        h_hi = [sb(f"h_hi{i}", [P, FT, C], F32R) for i in range(3)]
        h_lo = [sb(f"h_lo{i}", [P, FT, C], F32R) for i in range(3)]
        o_b = [sb(f"o_b{i}", [P, QC, D]) for i in range(2)]
        o_w = [sb(f"o_w{c}", [P, QC, D]) for c in range(NC)]

        lists_loaded, b2_loaded = sem("lists_loaded"), g["b2_loaded"]
        w1_hi_done, w1_lo_done, w2_hi_done, w2_lo_done = sem("w1_hi_done"), sem("w1_lo_done"), sem("w2_hi_done"), sem("w2_lo_done")
        pool_passed, act_passed = sem("pool_passed2"), sem("act_passed")
        meta_done = sem("meta_done")
        gathered = [sem(f"gathered{c}") for c in range(NC)]
        gT_ready, g_hi_done, g_lo_done = sem("gT_ready"), sem("g_hi_done"), sem("g_lo_done")
        z_ready, h_done, h_hi_done, h_lo_done = sem("z_ready"), sem("h_done"), sem("h_hi_done"), sem("h_lo_done")
        eo_ready, ob_done, ow_done, added = sem("eo_ready"), sem("ob_done"), sem("ow_done"), sem("added")
        BZ, BO, BT = (0, 1, 2, 3), (4, 5), (6, 7)

        def bank(i, **kw):
            return banks[i][:, :].rearrange("p (a b) -> p a b", **kw)

        block = ctx.enter_context(nc.Block())

        @block.sync
        def _(sp):
            sp.dma_start(lists[:, :, :, :].rearrange("p e j w -> p e (j w)"), list_v).then_inc(lists_loaded, 16)
            for e in range(NE):
                sp.dma_start(b2_all[:, e, :], b2_d[e:e + 1, :].partition_broadcast(P).rearrange("p a d -> p (a d)")).then_inc(b2_loaded, 16)
            with sp.Fori(1, NE) as e:
                sp.wait_ge(w1_hi_done, PARTS * e)
                sp.wait_ge(w1_lo_done, PARTS * e)
                sp.dma_start(w1_raw[:, :, :], w1_d[e].rearrange("(c p) f -> p c f", p=P)).then_inc(w1_loaded, 16)
                sp.wait_ge(w2_hi_done, PARTS * e)
                sp.wait_ge(w2_lo_done, PARTS * e)
                sp.dma_start(w2_raw[:, :, :], w2_d[e].rearrange("(f p) d -> p f d", p=P)).then_inc(w2_loaded, 16)
            sp.wait_ge(added, 16 * NE * BLK)

        @block.gpsimd
        def _(pool):
            pool.wait_ge(lists_loaded, 16)

            def gather(e, c):
                n = NC * e + c
                if not (isinstance(e, int) and e == 0):
                    pool.wait_ge(added, 16 * QC * (n - NC + 1))
                nc.gpsimd.tensor_copy(meta[c][:, :, :], lists[:, e, QC * c:QC * c + QC, :]).then_inc(meta_done, 1)
                wait_apart(pool, pool_passed, (meta_done, n + 1))
                for r in range(QC):
                    nc.gpsimd.indirect_dma_start(
                        out=rows[c][:, r, :], out_offset=None, in_=x1_d,
                        in_offset=bass.IndirectOffsetOnAxis(ap=meta[c][:, r, 0:1], axis=0)).then_inc(gathered[c], 16)

            def add_back(e, c):
                n = NC * e + c
                pool.wait_ge(ow_done, QC * (n + 1))
                for r in range(QC):
                    wait_apart(pool, pool_passed, (added, 16 * (QC * n + r)))
                    nc.gpsimd.indirect_dma_start(
                        out=acc_d, out_offset=bass.IndirectOffsetOnAxis(ap=meta[c][:, r, 0:1], axis=0),
                        in_=o_w[c][:, r, :], in_offset=None, compute_op=ALU.add).then_inc(added, 16)

            def expert(e, last):
                for c in range(NC):
                    if c + AHEAD < NC:
                        gather(e, c + AHEAD)
                    elif not last:
                        gather(e + 1, c + AHEAD - NC)
                    add_back(e, c)

            for c in range(AHEAD):
                gather(0, c)
            expert(0, False)
            with pool.Fori(1, NE - 1) as e:
                expert(e, False)
            expert(NE - 1, True)

        @block.scalar
        def _(act):
            def split_w1(e):
                act.wait_ge(w1_loaded, 16 * (e + 1))
                act.wait_ge(z_ready, PAIRS * NC * e)
                for i in range(PARTS):
                    f = slice(i * (FF // PARTS), (i + 1) * (FF // PARTS))
                    nc.scalar.activation(w1_hi[:, :, f], w1_raw[:, :, f], ACT.Copy).then_inc(w1_hi_done, 1)

            def split_w2(e):
                act.wait_ge(w2_loaded, 16 * (e + 1))
                act.wait_ge(eo_ready, NC * e)
                for i in range(PARTS):
                    f = slice(i * (FT // PARTS), (i + 1) * (FT // PARTS))
                    nc.scalar.activation(w2_hi[:, f, :], w2_raw[:, f, :], ACT.Copy).then_inc(w2_hi_done, 1)

            def rows_hi(e, c):
                n = NC * e + c
                act.wait_ge(gT_ready, n + 1)
                if not (isinstance(n, int) and n < 3):
                    act.wait_ge(z_ready, PAIRS * (n - 1))
                nc.scalar.activation(g_hi[HBUF[c]][:, :, :], bank(BT[c % 2], a=DK), ACT.Copy).then_inc(g_hi_done, 1)

            def relu(e, c):
                for m in range(PAIRS):
                    n = PAIRS * (NC * e + c) + m
                    used = () if isinstance(n, int) and n < 2 else ((h_hi_done, n - 1), (h_lo_done, n - 1))
                    wait_apart(act, act_passed, (z_ready, n + 1), *used)
                    for i in range(2):
                        col = FT * e + 2 * m + i
                        ins = nc.scalar.activation(h[m % 2][:, i, :], bank(BZ[m], a=2)[:, i, :], ACT.Relu,
                                                   bias=b1T[:, col:col + 1] if isinstance(col, int) else b1T[:, bass.ds(col, 1)])
                    ins.then_inc(h_done, 1)

            def weigh(e, c):
                n = NC * e + c
                act.wait_ge(ob_done, n + 1)
                for r in range(QC):
                    nc.scalar.activation(o_w[c][:, r, :], o_b[c % 2][:, r, :], ACT.Copy,
                                         scale=meta[c][:, r, 1:2].bitcast(F32)).then_inc(ow_done, 1)

            expert_order(act, NE, NC, lambda e, c: (rows_hi(e, c)), relu, weigh, split_w1, split_w2)

        @block.vector
        def _(dve):
            def split_w1(e):
                for i in range(PARTS):
                    f = slice(i * (FF // PARTS), (i + 1) * (FF // PARTS))
                    dve.wait_ge(w1_hi_done, PARTS * e + i + 1)
                    nc.vector.tensor_tensor(w1_lo[:, :, f], w1_raw[:, :, f], w1_hi[:, :, f].bitcast(F32),
                                            ALU.subtract).then_inc(w1_lo_done, 1)

            def split_w2(e):
                for i in range(PARTS):
                    f = slice(i * (FT // PARTS), (i + 1) * (FT // PARTS))
                    dve.wait_ge(w2_hi_done, PARTS * e + i + 1)
                    nc.vector.tensor_tensor(w2_lo[:, f, :], w2_raw[:, f, :], w2_hi[:, f, :].bitcast(F32),
                                            ALU.subtract).then_inc(w2_lo_done, 1)

            def rows_lo(e, c):
                dve.wait_ge(g_hi_done, NC * e + c + 1)
                nc.vector.tensor_tensor(g_lo[HBUF[c]][:, :, :], bank(BT[c % 2], a=DK), g_hi[HBUF[c]][:, :, :].bitcast(F32),
                                        ALU.subtract).then_inc(g_lo_done, 1)

            def halves(e, c):
                for m in range(PAIRS):
                    n = PAIRS * (NC * e + c) + m
                    dve.wait_ge(h_done, n + 1)
                    if m == 0 and not (isinstance(e, int) and e == 0 and c < 3):
                        dve.wait_ge(eo_ready, NC * e + c - 1)
                    t = slice(2 * m, 2 * m + 2)
                    nc.vector.tensor_copy(h_hi[HBUF[c]][:, t, :], h[m % 2][:, :, :]).then_inc(h_hi_done, 1)
                    dve.wait_ge(h_hi_done, n + 1)
                    nc.vector.tensor_tensor(h_lo[HBUF[c]][:, t, :], h[m % 2][:, :, :], h_hi[HBUF[c]][:, t, :].bitcast(F32),
                                            ALU.subtract).then_inc(h_lo_done, 1)

            def bias(e, c):
                n = NC * e + c
                dve.wait_ge(eo_ready, n + 1)
                if not (isinstance(n, int) and n < 3):
                    dve.wait_ge(ow_done, QC * (n - (1 if c != 0 else 0)))
                for r in range(QC):
                    ins = nc.vector.tensor_tensor(o_b[c % 2][:, r, :], bank(BO[c % 2], a=QC)[:, r, :], b2_all[:, e, :], ALU.add)
                ins.then_inc(ob_done, 1)

            dve.wait_ge(b2_loaded, 16 * NE)
            expert_order(dve, NE, NC, rows_lo, halves, bias, split_w1, split_w2)

        @block.tensor
        def _(pe):
            def transposes(e, c):
                n = NC * e + c
                pe.wait_ge(gathered[c], 16 * QC * (e + 1))
                if not (isinstance(n, int) and n < 2):
                    pe.wait_ge(g_lo_done, n if c == 0 else n - 1)
                for i in range(DK):
                    for r in range(QC):
                        ins = nc.tensor.transpose(banks[BT[c % 2]][:, i * C + r * P:i * C + r * P + P],
                                                  rows[c][:, r, i * P:i * P + P], ident[:, :])
                ins.then_inc(gT_ready, 1)

            def layer1(e, c):
                n = NC * e + c
                pe.wait_ge(g_lo_done, n + 1)
                G_hi, G_lo = g_hi[HBUF[c]], g_lo[HBUF[c]]
                for m in range(PAIRS):
                    if c == 0 and m % (PAIRS // PARTS) == 0:
                        pe.wait_ge(w1_lo_done, PARTS * e + m // (PAIRS // PARTS) + 1)
                    if not (isinstance(n, int) and n == 0):
                        pe.wait_ge(h_done, PAIRS * (n - 1) + m + 1)
                    for i in range(2):
                        f = slice((2 * m + i) * P, (2 * m + i + 1) * P)
                        out = bank(BZ[m], a=2)[:, i, :]
                        for k in range(DK):
                            nc.tensor.matmul(out, w1_hi[:, k, f], G_hi[:, k, :], start=(k == 0), stop=False)
                            nc.tensor.matmul(out, w1_hi[:, k, f], G_lo[:, k, :], start=False, stop=False)
                            ins = nc.tensor.matmul(out, w1_lo[:, k, f], G_hi[:, k, :], start=False, stop=(k == DK - 1))
                    ins.then_inc(z_ready, 1)

            def layer2(e, c):
                n = NC * e + c
                if not (isinstance(n, int) and n < 2):
                    pe.wait_ge(ob_done, n if c == 0 else n - 1)
                H_hi, H_lo = h_hi[HBUF[c]], h_lo[HBUF[c]]
                for r in range(QC):
                    rs = slice(r * P, r * P + P)
                    out = bank(BO[c % 2], a=QC)[:, r, :]
                    for f in range(FT):
                        if r == 0 and c == 0 and f % (FT // PARTS) == 0:
                            pe.wait_ge(w2_lo_done, PARTS * e + f // (FT // PARTS) + 1)
                        if r == 0 and f % 2 == 0:
                            pe.wait_ge(h_lo_done, PAIRS * n + f // 2 + 1)
                        nc.tensor.matmul(out, H_hi[:, f, rs], w2_hi[:, f, :], start=(f == 0), stop=False)
                        nc.tensor.matmul(out, H_hi[:, f, rs], w2_lo[:, f, :], start=False, stop=False)
                        ins = nc.tensor.matmul(out, H_lo[:, f, rs], w2_hi[:, f, :], start=False, stop=(f == FT - 1))
                ins.then_inc(eo_ready, 1)

            expert_order(pe, NE, NC, transposes, layer1, layer2, None, None)


def expert_order(engine, NE, NC, take_in, layer1, layer2, split_w1, split_w2):
    def split(fn, e):
        if fn:
            fn(e)

    def body(e, last):
        for c in range(NC):
            if c + 2 < NC:
                take_in(e, c + 2)
            elif not last:
                take_in(e + 1, c + 2 - NC)
            if c + 1 < NC:
                layer1(e, c + 1)
            elif not last:
                layer1(e + 1, 0)
            if c + 1 == NC - 1 and not last:
                split(split_w1, e + 1)
            layer2(e, c)
        if not last:
            split(split_w2, e + 1)

    split(split_w1, 0)
    split(split_w2, 0)
    take_in(0, 0)
    take_in(0, 1)
    layer1(0, 0)
    body(0, False)
    with engine.Fori(1, NE - 1) as e:
        body(e, False)
    body(NE - 1, True)


def last_norm(nc, g):
    acc_v, out_d, NB, QC, D, expo = g["acc_v"], g["out_d"], g["NB"], g["QC"], g["D"], g["expo"]
    out_v = out_d.rearrange("b (c p) d -> b p c d", p=P)
    NBUF = 8
    ctx = ExitStack()
    with ctx:
        def sem(name):
            return ctx.enter_context(nc.semaphore(name))

        def sb(name, shape, dt=F32):
            return ctx.enter_context(nc.sbuf_tensor(name, shape, dt))

        a = [sb(f"a{i}", [P, QC, D]) for i in range(NBUF)]
        o = [sb(f"o{i}", [P, QC, D]) for i in range(NBUF)]
        stats = sb("stats2", [P, NB, QC, 6])
        mv = sb("mv2", [P, NB, QC, 2])
        veps = sb("veps2", [P, NB, QC])
        rstd = sb("rstd2", [P, NB, QC])
        loaded = [sem(f"acc_loaded{i}") for i in range(NBUF)]
        stored = [sem(f"out_stored{i}") for i in range(NBUF)]
        stats_done, mv_done, veps_done, rstd_done, o_done = (sem(n) for n in ("stats2_done", "mv2_done", "veps2_done", "rstd2_done", "out_done"))
        block = ctx.enter_context(nc.Block())

        @block.sync
        def _(sp):
            for b in range(NB):
                if b >= NBUF:
                    sp.wait_ge(o_done, QC * (b - NBUF + 1))
                sp.dma_start(a[b % NBUF][:, :, :], acc_v[b]).then_inc(loaded[b % NBUF], 16)

        @block.vector
        def _(dve):
            def apply(b):
                dve.wait_ge(rstd_done, b + 1)
                if b >= NBUF:
                    dve.wait_ge(stored[b % NBUF], 16 * (b // NBUF))
                for c in range(QC):
                    nc.vector.tensor_scalar(o[b % NBUF][:, c, :], a[b % NBUF][:, c, :], mv[:, b, c, 0:1], rstd[:, b, c:c + 1],
                                            ALU.subtract, ALU.mult).then_inc(o_done, 1)

            for b in range(NB):
                dve.wait_ge(loaded[b % NBUF], 16 * (b // NBUF + 1))
                for c in range(QC):
                    nc.vector.bn_stats(stats[:, b, c, :], a[b % NBUF][:, c, :]).then_inc(stats_done, 1)
                dve.wait_ge(stats_done, QC * (b + 1))
                for c in range(QC):
                    ins = nc.vector.bn_aggr(mv[:, b, c, :], stats[:, b, c, :])
                ins.then_inc(mv_done, 1)
                if b >= 2:
                    apply(b - 2)
            for b in (NB - 2, NB - 1):
                apply(b)

        @block.gpsimd
        def _(pool):
            for b in range(NB):
                pool.wait_ge(mv_done, b + 1)
                nc.gpsimd.tensor_scalar(veps[:, b, :], mv[:, b, :, 1], EPS, None, ALU.add).then_inc(veps_done, 1)
                pool.wait_ge(veps_done, b + 1)
                nc.gpsimd.tensor_tensor(rstd[:, b, :], veps[:, b, :], expo[:, :], ALU.pow).then_inc(rstd_done, 1)

        @block.scalar
        def _(act):
            for b in range(NB):
                act.wait_ge(o_done, QC * (b + 1))
                act.dma_start(out_v[b], o[b % NBUF][:, :, :]).then_inc(stored[b % NBUF], 16)
            for i in range(NBUF):
                act.wait_ge(stored[i], 16 * (NB // NBUF))


_INS = ['L0_attn_x', 'L0_attn_w_q', 'L0_attn_w_k', 'L0_attn_w_v', 'L0_attn_w_o', 'L0_ffn_gating_w',
        'L0_ffn_w1', 'L0_ffn_b1', 'L0_ffn_w2', 'L0_ffn_b2']


def kernel(**inputs):
    import numpy as _np
    import concourse.bacc as _bacc
    from concourse import mybir as _mybir
    from concourse.bass_utils import run_bass_kernel_spmd as _run

    nc = _bacc.Bacc("TRN2", target_bir_lowering=False, num_devices=1)
    arrays, args = {}, []
    for name in _INS:
        a = _np.ascontiguousarray(inputs[name])
        arrays[f"in_{name}"] = a
        args.append(nc.dram_tensor(f"in_{name}", a.shape, _mybir.dt.from_np(a.dtype), kind="ExternalInput").ap())
    shape = inputs['L0_attn_x'].shape
    args.append(nc.dram_tensor("out_0", shape, _mybir.dt.float32, kind="ExternalOutput").ap())
    build(nc, *args)
    r = _run(nc, [arrays], core_ids=[0])
    return r.results[0]["out_0"]
```

```python
from contextlib import ExitStack

import concourse.bass as bass
from concourse import mybir

F32 = mybir.dt.float32
F32R = mybir.dt.float32r
BF16 = mybir.dt.bfloat16
I32 = mybir.dt.int32
U32 = mybir.dt.uint32
ALU = mybir.AluOpType
ACT = mybir.ActivationFunctionType
X = mybir.AxisListType.X

P = 128
EPS = 1e-5
ROW_B, ROW_C, ROW_M, STACK = 16, 64, 96, 98
RING = 8
GW = 128
POOL_CONSTS = 6
HBUF = (0, 1, 0, 1, 2)


def wait_apart(engine, passed, *waits):
    for semaphore, value in waits:
        engine.wait_ge(semaphore, value)
    engine.sem_inc(passed, 1)


class Seq:

    def __init__(self, i, off):
        self.n = 2 * i + off
        self.parity = off % 2
        self.half = i + off // 2


def build(nc, x_d, wq_d, wk_d, wv_d, wo_d, gw_d, w1_d, b1_d, w2_d, b2_d, out_d):
    NB, S, D = x_d.shape
    T = NB * S
    R = 16
    H = D // R
    NE, _, FF = w1_d.shape
    TOPK = 2
    CAP = -(-(T * TOPK * 5) // (NE * 4))
    SCALE = R ** -0.5
    QC = S // P
    DK = D // P
    HH = P // R
    FT = FF // P
    BLK = CAP // P
    NC = BLK // QC
    C = QC * P
    TRASH = P

    x1_d = nc.dram_tensor("x1_rows", (T + TRASH, D), F32, kind="Internal").ap()
    acc_d = nc.dram_tensor("acc_rows", (T + TRASH, D), F32, kind="Internal").ap()
    list_d = nc.dram_tensor("slot_list", (NE * CAP, 2), I32, kind="Internal").ap()

    x_v = x_d.rearrange("b (c p) d -> b p c d", p=P)
    x1_v = x1_d[0:T, :].rearrange("(b c p) d -> b p c d", p=P, c=QC)
    acc_v = acc_d[0:T, :].rearrange("(b c p) d -> b p c d", p=P, c=QC)
    list_v = list_d.rearrange("(e p j) w -> p e (j w)", e=NE, p=P)

    top = ExitStack()

    def sem(name, ctx=top):
        return ctx.enter_context(nc.semaphore(name))

    def sb(name, shape, dt=F32, ctx=top):
        return ctx.enter_context(nc.sbuf_tensor(name, shape, dt))

    with top:
        banks = [top.enter_context(nc.psum_tensor(f"bank{i}", [P, 512], F32)) for i in range(8)]
        ident = sb("ident", [P, P])
        b1T = sb("b1T", [P, NE * FT])
        w1_raw = sb("w1_raw", [P, DK, FF])
        w2_raw = sb("w2_raw", [P, FT, D])
        expo = sb("expo", [P, QC])
        w1_loaded, w2_loaded, b2_loaded = sem("w1_loaded"), sem("w2_loaded"), sem("b2_loaded")

        attention(nc, locals())
        experts(nc, locals())
        last_norm(nc, locals())


def attention(nc, g):
    (x_v, x1_v, acc_v, list_v, x1_d, acc_d, list_d) = (
        g["x_v"], g["x1_v"], g["acc_v"], g["list_v"], g["x1_d"], g["acc_d"], g["list_d"])
    NB, S, D, T, R, H = g["NB"], g["S"], g["D"], g["T"], g["R"], g["H"]
    QC, DK, HH, NE, FT, CAP, BLK = g["QC"], g["DK"], g["HH"], g["NE"], g["FT"], g["CAP"], g["BLK"]
    SCALE, TRASH, TOPK = g["SCALE"], g["TRASH"], g["TOPK"]
    banks, ident, b1T, expo = g["banks"], g["ident"], g["b1T"], g["expo"]
    G = H // HH
    QUADS = H // 4
    ctx = ExitStack()
    with ctx:
        def sem(name):
            return ctx.enter_context(nc.semaphore(name))

        def sb(name, shape, dt=F32):
            return ctx.enter_context(nc.sbuf_tensor(name, shape, dt))

        tri = sb("tri", [P, P], BF16)
        ones = sb("ones", [P, P], BF16)
        w_raw = sb("w_raw", [P, 4, DK, D])
        wT_hi = sb("wT_hi", [P, 4, DK, D], F32R)
        wT_lo = sb("wT_lo", [P, 4, DK, D], F32R)
        b1_raw = sb("b1_raw", [NE * FT, P])
        gate_raw = sb("gate_raw", [P, DK, NE])
        gate_hi = sb("gate_hi", [P, DK, GW // NE, NE], F32R)
        gate_lo = sb("gate_lo", [P, DK, GW // NE, NE], F32R)
        iota_e = sb("iota_e", [P, NE])
        slot0 = sb("slot0", [P, NE])
        fill = sb("fill", [P, NE, BLK, 2], I32)
        zrow = sb("zrow", [P, D])
        ones_f = sb("ones_f", [P, S])
        tok = sb("tok", [P, QC])
        x_sb = [sb(f"x_sb{i}", [P, QC, D]) for i in range(2)]
        xres = [sb(f"xres{i}", [P, QC, D]) for i in range(2)]
        xT_f = sb("xT_f", [P, DK, S])
        xT_hi = [sb(f"xT_hi{i}", [P, DK, S], F32R) for i in range(2)]
        xT_lo = [sb(f"xT_lo{i}", [P, DK, S], F32R) for i in range(2)]
        qk = [sb(f"qk{i}", [P, 2, G, 2, S], F32R) for i in range(2)]
        stack = [sb(f"stack{i}", [STACK, H, 2, S], F32R) for i in range(2)]
        v_aug = [sb(f"v_aug{i}", [P, QC, H, 32]) for i in range(2)]
        negm = sb("negm", [P, QC, H])
        mT_hi = [sb(f"mT_hi{i}", [HH, S], F32R) for i in range(2)]
        mT_lo = [sb(f"mT_lo{i}", [HH, S], F32R) for i in range(2)]
        probs = sb("probs", [P, RING, QC, S])
        u_sb = sb("u_sb", [P, QUADS, S])
        rec = sb("rec", [P, QC, H])
        attn = sb("attn", [P, QC, D])
        aT_hi = sb("aT_hi", [P, DK, S], F32R)
        aT_lo = sb("aT_lo", [P, DK, S], F32R)
        y = sb("y", [P, QC, D])
        stats = sb("stats", [P, QC, 6])
        mv = sb("mv", [P, QC, 2])
        veps = sb("veps", [P, QC])
        rstd = sb("rstd", [P, QC])
        x1 = sb("x1", [P, QC, D])
        nmean = sb("nmean", [P, QC])
        shift = sb("shift", [P, QC])
        x1T_f = sb("x1T_f", [P, DK, S])
        x1T_hi = sb("x1T_hi", [P, DK, S], F32R)
        x1T_lo = sb("x1T_lo", [P, DK, S], F32R)
        lg = sb("lg", [P, QC, NE])
        mx = sb("mx", [P, QC, NE])
        ix = sb("ix", [P, QC, NE], U32)
        ixf = sb("ixf", [P, QC, TOPK])
        hot = sb("hot", [P, QC, TOPK, NE])
        mask = sb("mask", [P, QC, NE], BF16)
        seen = [sb(f"seen{i}", [P, NE], BF16) for i in range(2)]
        seen_t = sb("seen_t", [P, NE], BF16)
        dmx = sb("dmx", [P, QC, NE])
        ex = sb("ex", [P, QC, NE])
        zsum = sb("zsum", [P, QC])
        den = sb("den", [P, QC])
        den2 = sb("den2", [P, QC])
        over = sb("over", [P, QC, NE])
        slot = sb("slot", [P, QC, NE])
        slot_b = sb("slot_b", [P, QC, NE])
        pick = sb("pick", [P, QC, TOPK, NE])
        dest_f = sb("dest_f", [P, QC, TOPK])
        dest = [sb(f"dest{i}", [P, QC * TOPK], I32) for i in range(2)]
        item = [sb(f"item{i}", [P, QC * TOPK, 2], I32) for i in range(2)]

        consts_ready, zeros_ready, filled = sem("consts_ready"), sem("zeros_ready"), sem("filled")
        ident0, wT_ready, wT_hi_done = sem("ident0"), sem("wT_ready"), sem("wT_hi_done")
        w_loaded = [sem(f"w_loaded{w}") for w in range(4)]
        wT_lo_done, b1_loaded, gate_loaded, b1T_ready, b1T_done = (
            sem("wT_lo_done"), sem("b1_loaded"), sem("gate_loaded"), sem("b1T_ready"), sem("b1T_done"))
        x_loaded = [sem(f"x_loaded{i}") for i in range(2)]
        xres_loaded = [sem(f"xres_loaded{i}") for i in range(2)]
        xT_ready, xT_copied, xT_hi_done, xT_lo_done = sem("xT_ready"), sem("xT_copied"), sem("xT_hi_done"), sem("xT_lo_done")
        q_ready, k_ready, v_ready, v_done = sem("q_ready"), sem("k_ready"), sem("v_ready"), sem("v_done")
        qk_ready = (q_ready, k_ready)
        qk_hi_done = (sem("q_hi_done"), sem("k_hi_done"))
        qk_lo_done = (sem("q_lo_done"), sem("k_lo_done"))
        stacked = [sem(f"stacked{i}") for i in range(2)]
        s_ready, max_done = sem("s_ready"), sem("max_done")
        mT_ready, mT_hi_done, mT_lo_done = ([sem(f"{n}{i}") for i in range(2)] for n in ("mT_ready", "mT_hi_done", "mT_lo_done"))
        shift_in = [sem(f"shift_in{i}") for i in range(2)]
        st_ready, exp_done = sem("st_ready"), sem("exp_done")
        pv_ready, u_done = sem("pv_ready"), sem("u_done")
        uT_ready, rec_done, attn_done = sem("uT_ready"), sem("rec_done"), sem("attn_done")
        aT_ready, aT_hi_done, aT_lo_done = sem("aT_ready"), sem("aT_hi_done"), sem("aT_lo_done")
        o_ready, y_done, stats_done, mv_done = sem("o_ready"), sem("y_done"), sem("stats_done"), sem("mv_done")
        veps_done, rstd_done, x1_done = sem("veps_done"), sem("rstd_done"), sem("x1_done")
        x1_stored = [sem(f"x1_stored{i}") for i in range(2)]
        nmean_done, shift_done = sem("nmean_done"), sem("shift_done")
        x1T_ready, x1T_copied, x1T_hi_done, x1T_lo_done = sem("x1T_ready"), sem("x1T_copied"), sem("x1T_hi_done"), sem("x1T_lo_done")
        gate_done, lg_ready, lg_done = sem("gate_done"), sem("lg_ready"), sem("lg_done")
        mx_done, ix_done, ixf_done, hot_done = sem("mx_done"), sem("ix_done"), sem("ixf_done"), sem("hot_done")
        mask_done, seen_mid, seen_done, pos_ready = sem("mask_done"), sem("seen_mid"), sem("seen_done"), sem("pos_ready")
        dmx_done, ex_done, zsum_done, den_done = sem("dmx_done"), sem("ex_done"), sem("zsum_done"), sem("den_done")
        den2_done, inv_done, item_done, tok_done = sem("den2_done"), sem("inv_done"), sem("item_done"), sem("tok_done")
        over_done, slot_done, slotb_done, pick_done = sem("over_done"), sem("slot_done"), sem("slotb_done"), sem("pick_done")
        destf_done, dest_done = sem("destf_done"), sem("dest_done")
        ident_ready, ones_ready, v_ones = sem("ident_ready"), sem("ones_ready"), sem("v_ones")
        queries_cleared = [sem(f"queries_cleared{i}") for i in range(2)]
        keys_cleared = [sem(f"keys_cleared{i}") for i in range(2)]
        keys_ready = [sem(f"keys_ready{i}") for i in range(2)]
        sp_passed, pool_passed, dve_passed = sem("sp_passed"), sem("pool_passed"), sem("dve_passed")
        listed = [sem(f"listed{i}") for i in range(2)]

        BQ, BD, BU, BA, BB, BC = (0, 1), (2, 3), 4, 5, 6, 7

        def bank(i, **kw):
            return banks[i][:, :].rearrange("p (a b) -> p a b", **kw)

        def from_bank(w, c):
            t = banks[4 + w][:, c * D:c * D + D]
            return t.rearrange("p (x h r) -> p x h r", h=HH // 2, r=R) if w < 2 else t

        def by_feature(t, w, c):
            return t[:, w, c].rearrange("p (x r h) -> p x h r", h=HH // 2, r=R) if w < 2 else t[:, w, c]

        block = ctx.enter_context(nc.Block())

        first, last = -1, NB + 3

        def pipeline(engine, step):
            lo, hi = 3, (NB - 2) // 2
            for s in range(first, 2 * lo):
                step(Seq(0, s), s)
            with engine.Fori(lo, hi) as i:
                for j in range(2):
                    step(Seq(i, j), None)
            for s in range(2 * hi, last + 1):
                step(Seq(s // 2, s % 2), s)

        def stage(s, num, lag):
            if num is not None:
                n = num - lag
                return Seq(n // 2, n % 2) if 0 <= n < NB else None
            return Seq(s.half, s.parity - lag)

        @block.sync
        def _(sp):
            for w, name in enumerate(("wq_d", "wk_d", "wv_d", "wo_d")):
                sp.dma_start(w_raw[:, w], g[name].rearrange("(c p) d -> p c d", p=P)).then_inc(w_loaded[w], 16)
                if w == 0:
                    sp.dma_start(x_sb[0][:, :, :], x_v[0]).then_inc(x_loaded[0], 16)
            sp.dma_start(b1_raw[:, :], g["b1_d"].rearrange("e (f p) -> (e f) p", p=P)).then_inc(b1_loaded, 16)
            sp.dma_start(gate_raw[:, :, :], g["gw_d"].rearrange("(c p) e -> p c e", p=P)).then_inc(gate_loaded, 16)
            def fill_dram():
                sp.wait_ge(zeros_ready, 2)
                sp.dma_start(list_v, fill[:, :, :, :].rearrange("p e j w -> p e (j w)")).then_inc(filled, 16)
                sp.dma_start(x1_d[T:T + TRASH, :], zrow[:, :]).then_inc(filled, 16)
                sp.dma_start(acc_d[T:T + TRASH, :], zrow[:, :]).then_inc(filled, 16)
                sp.dma_start(g["w1_raw"][:, :, :], g["w1_d"][0].rearrange("(c p) f -> p c f", p=P)).then_inc(g["w1_loaded"], 16)
                sp.dma_start(g["w2_raw"][:, :, :], g["w2_d"][0].rearrange("(f p) d -> p f d", p=P)).then_inc(g["w2_loaded"], 16)

            def shift_rows(b, half):
                sp.wait_ge(mT_hi_done[half], b.n + 1)
                sp.wait_ge(mT_lo_done[half], b.n + 1)
                heads = slice(HH * half, HH * (half + 1))
                for row, src in ((ROW_M, mT_hi[half]), (ROW_M + 1, mT_lo[half])):
                    sp.dma_start(stack[b.parity][row:row + 1, heads, 0, :].bitcast(F32), src[:, :].bitcast(F32)).then_inc(shift_in[half], 16)

            def stack_rows(a, half):
                src = qk[a.parity][P // 2 * half:P // 2 * (half + 1)].bitcast(F32)
                dst = stack[a.parity][:, HH * half:HH * (half + 1)].bitcast(F32)
                pair = src.rearrange("p c g w t -> p c (g w t)")
                both = dst.rearrange("r h w t -> r (h w t)")
                for out, in_ in ((dst[0:R, :, 0, :], src[:, 1, :, 0, :]), (dst[0:R, :, 1, :], src[:, 0, :, 1, :]),
                                 (both[ROW_B:ROW_B + R], pair[:, 0, :]), (both[ROW_C:ROW_C + R], pair[:, 1, :])):
                    sp.dma_start(out, in_).then_inc(stacked[half], 16)

            def step(s, num):
                a, b, d, e = (stage(s, num, lag) for lag in (-1, 0, 1, 2))
                nxt = stage(s, num, -2)
                if nxt:
                    if num is None or num >= 0:
                        sp.wait_ge(xT_ready, nxt.n - 1)
                    sp.dma_start(x_sb[nxt.parity][:, :, :], x_v[nxt.n]).then_inc(x_loaded[nxt.parity], 16)
                if e:
                    if num is None or num >= 4:
                        sp.wait_ge(y_done, e.n - 1)
                    sp.dma_start(xres[e.parity][:, :, :], x_v[e.n]).then_inc(xres_loaded[e.parity], 16)
                if d:
                    shift_rows(d, 1)
                if b:
                    shift_rows(b, 0)
                if a:
                    if num in (-1, 0):
                        sp.wait_ge(keys_cleared[a.parity], 1)
                        sp.wait_ge(queries_cleared[a.parity], 1)
                    for w in range(2):
                        sp.wait_ge(qk_hi_done[w], a.n + 1)
                        sp.wait_ge(qk_lo_done[w], a.n + 1)
                for half in range(2):
                    if a:
                        if b:
                            wait_apart(sp, sp_passed, (s_ready, H * b.n + HH * half + 1))
                        if num is None or num >= 1:
                            wait_apart(sp, sp_passed, (st_ready, H * (a.n - 2) + HH * (half + 1)))
                        stack_rows(a, half)
                        if num == 0 and half == 1:
                            sp.wait_ge(keys_ready[0], 1)
                            sp.dma_start(stack[1][ROW_M:STACK, :, 1, :].bitcast(F32),
                                         stack[0][ROW_M:STACK, :, 1, :].bitcast(F32)).then_inc(keys_ready[1], 16)
                            fill_dram()
                    if half == 0 and e:
                        sp.wait_ge(x1_done, e.n + 1)
                        sp.dma_start(x1_v[e.n], x1[:, :, :]).then_inc(x1_stored[e.parity], 16)
                        sp.dma_start(acc_v[e.n], x1[:, :, :]).then_inc(x1_stored[e.parity], 16)

            pipeline(sp, step)
            for i in range(2):
                sp.wait_ge(x1_stored[i], 32 * (NB // 2))
                sp.wait_ge(listed[i], 16 * QC * TOPK * (NB // 2))
            sp.wait_ge(filled, 48)

        @block.gpsimd
        def _(pool):
            nc.gpsimd.memset(ident[:, :], 0.0).then_inc(ident0, 1)
            pool.wait_ge(ident0, 1)
            nc.gpsimd.affine_select(out=ident[:, :], in_=ident[:, :], compare_op=ALU.not_equal, fill=1.0,
                                    base=0, pattern=[[-1, P]], channel_multiplier=1).then_inc(ident_ready, 1)
            nc.gpsimd.memset(stack[0][:, :, 0, :].bitcast(F32), 0.0).then_inc(queries_cleared[0], 1)
            nc.gpsimd.memset(tri[:, :], 1.0).then_inc(ident0, 1)
            nc.gpsimd.memset(ones[:, :], 1.0).then_inc(consts_ready, 1)
            nc.gpsimd.memset(fill[:, :, :, :], 0).then_inc(ident0, 1)
            nc.gpsimd.memset(zrow[:, :], 0.0).then_inc(zeros_ready, 1)
            pool.wait_ge(ident0, 3)
            nc.gpsimd.affine_select(out=tri[:, :], in_=tri[:, :], compare_op=ALU.is_gt, fill=0.0,
                                    base=0, pattern=[[1, P]], channel_multiplier=-1).then_inc(consts_ready, 1)
            nc.gpsimd.iota(fill[:, :, :, 0], pattern=[[0, NE], [0, BLK]], base=T, channel_multiplier=1).then_inc(zeros_ready, 1)
            nc.gpsimd.iota(iota_e[:, :], pattern=[[1, NE]], base=0, channel_multiplier=0,
                           allow_small_or_imprecise_dtypes=True).then_inc(consts_ready, 1)
            nc.gpsimd.iota(slot0[:, :], pattern=[[CAP, NE]], base=0, channel_multiplier=0,
                           allow_small_or_imprecise_dtypes=True).then_inc(consts_ready, 1)
            nc.gpsimd.iota(tok[:, :], pattern=[[P, QC]], base=0, channel_multiplier=1,
                           allow_small_or_imprecise_dtypes=True).then_inc(tok_done, 1)
            nc.gpsimd.memset(expo[:, :], -0.5).then_inc(consts_ready, 1)
            nc.gpsimd.memset(seen[0][:, :], 0.0).then_inc(consts_ready, 1)
            pool.wait_ge(consts_ready, POOL_CONSTS)

            def step(s, num):
                a, e, f, g = (stage(s, num, lag) for lag in (-1, 2, 3, 4))
                if a:
                    used = ((v_ready, a.n - 1),) if num is None or num >= 1 else ()
                    wait_apart(pool, pool_passed, (xT_hi_done, a.n + 1), *used)
                    nc.gpsimd.tensor_tensor(xT_lo[a.parity][:, :, :], xT_f[:, :, :], xT_hi[a.parity][:, :, :].bitcast(F32),
                                            ALU.subtract).then_inc(xT_lo_done, 1)
                if f:
                    wait_apart(pool, pool_passed, (x1T_hi_done, f.n + 1), (lg_ready, f.n))
                    nc.gpsimd.tensor_tensor(x1T_lo[:, :, :], x1T_f[:, :, :], x1T_hi[:, :, :].bitcast(F32),
                                            ALU.subtract).then_inc(x1T_lo_done, 1)
                if num == first:
                    nc.gpsimd.memset(stack[1][:, :, 0, :].bitcast(F32), 0.0).then_inc(queries_cleared[1], 1)
                if g:
                    if num == 4:
                        pool.wait_ge(filled, 48)
                    wait_apart(pool, pool_passed, (dest_done, g.n + 1), (item_done, 2 * g.n + 2))
                    for n in range(QC * TOPK):
                        nc.gpsimd.indirect_dma_start(
                            out=list_d, out_offset=bass.IndirectOffsetOnAxis(ap=dest[g.parity][:, n:n + 1], axis=0),
                            in_=item[g.parity][:, n, :], in_offset=None, bounds_check=NE * CAP - 1,
                            oob_is_err=False).then_inc(listed[g.parity], 16)
                if e:
                    wait_apart(pool, pool_passed, (mv_done, e.n + 1), (x1_done, e.n))
                    nc.gpsimd.tensor_scalar(veps[:, :], mv[:, :, 1], EPS, None, ALU.add).then_inc(veps_done, 1)
                    nc.gpsimd.tensor_scalar(nmean[:, :], mv[:, :, 0], -1.0, None, ALU.mult).then_inc(nmean_done, 1)
                    pool.wait_ge(veps_done, e.n + 1)
                    nc.gpsimd.tensor_tensor(rstd[:, :], veps[:, :], expo[:, :], ALU.pow).then_inc(rstd_done, 1)
                    pool.wait_ge(nmean_done, e.n + 1)
                    pool.wait_ge(rstd_done, e.n + 1)
                    nc.gpsimd.tensor_tensor(shift[:, :], nmean[:, :], rstd[:, :], ALU.mult).then_inc(shift_done, 1)

            pipeline(pool, step)

        @block.scalar
        def _(act):
            act.wait_ge(ones_ready, 1)
            nc.scalar.activation(stack[0][ROW_M:STACK, :, 1, :], ones_f[ROW_M:STACK, :].unsqueeze(1).to_broadcast([STACK - ROW_M, H, S]),
                                 ACT.Copy).then_inc(keys_ready[0], 1)
            for w in range(4):
                act.wait_ge(wT_ready, w + 1)
                for c in range(DK):
                    ins = nc.scalar.activation(by_feature(wT_hi, w, c), from_bank(w, c), ACT.Copy)
                ins.then_inc(wT_hi_done, 1)
            act.wait_ge(b1T_ready, 1)
            nc.scalar.activation(b1T[:, :], banks[0][:, 0:NE * FT], ACT.Copy).then_inc(b1T_done, 1)
            act.wait_ge(gate_loaded, 16)
            nc.scalar.activation(gate_hi[:, :, :, :], gate_raw[:, :, :].unsqueeze(2).to_broadcast([P, DK, GW // NE, NE]),
                                 ACT.Copy).then_inc(gate_done, 1)

            def u_copy(b, half):
                act.wait_ge(pv_ready, QUADS * b.n + 2 * half + 2)
                act.wait_ge(uT_ready, b.n)
                nc.scalar.activation(u_sb[:, 2 * half:2 * half + 2, :], bank(BU, a=2), ACT.Copy).then_inc(u_done, 1)

            def mT_copy(b, half):
                act.wait_ge(mT_ready[half], b.n + 1)
                act.wait_ge(shift_in[half], 32 * b.n)
                act.wait_ge(mT_lo_done[half], b.n)
                nc.scalar.activation(mT_hi[half][:, :], banks[(BA, BB)[half]][0:HH, 0:S], ACT.Copy).then_inc(mT_hi_done[half], 1)

            def step(s, num):
                a, b, d, e, f = (stage(s, num, lag) for lag in (-1, 0, 1, 2, 3))
                for k in range(H):
                    if k == 1 and a:
                        act.wait_ge(xT_ready, a.n + 1)
                        act.wait_ge(xT_lo_done, a.n)
                        nc.scalar.activation(xT_f[:, :, :], bank(BC, a=DK), ACT.Copy).then_inc(xT_copied, 1)
                    if k == 2 and f:
                        act.wait_ge(x1T_ready, f.n + 1)
                        act.wait_ge(x1T_lo_done, f.n)
                        nc.scalar.activation(x1T_f[:, :, :], bank(BA, a=DK), ACT.Copy).then_inc(x1T_copied, 1)
                    if k == 3 and e:
                        u_copy(e, 1)
                    if k == 2 and d:
                        mT_copy(d, 1)
                    if k == 4 and b:
                        act.wait_ge(v_ready, b.n + 1)
                        if num is None or num >= 2:
                            act.wait_ge(pv_ready, QUADS * (b.n - 1))
                        for c in range(QC):
                            dst = v_aug[b.parity][:, c, :, 0:R].rearrange("p (h g) r -> p g h r", g=G)
                            src = banks[BA][:, c * D:c * D + D].rearrange("p (g h r) -> p g h r", g=G, r=R)
                            ins = nc.scalar.activation(dst, src, ACT.Copy)
                        ins.then_inc(v_done, 1)
                    if k == 10 and b:
                        mT_copy(b, 0)
                    if k in (7, 10) and a:
                        w = (7, 10).index(k)
                        act.wait_ge(qk_ready[w], a.n + 1)
                        if num is None or num >= 1:
                            act.wait_ge(s_ready, H * (a.n - 1))
                            act.wait_ge(qk_lo_done[w], a.n - 1)
                        nc.scalar.activation(qk[a.parity][:, 1 - w, :, w, :], bank(BC, a=G), ACT.Copy).then_inc(qk_hi_done[w], 1)
                    if k == 9 and e:
                        act.wait_ge(aT_ready, e.n + 1)
                        act.wait_ge(o_ready, e.n)
                        act.wait_ge(aT_lo_done, e.n)
                        nc.scalar.activation(aT_hi[:, :, :], bank(BB, a=DK), ACT.Copy).then_inc(aT_hi_done, 1)
                    if k == 13 and d:
                        u_copy(d, 0)
                    if k == 15 and e:
                        act.wait_ge(shift_done, e.n + 1)
                        act.wait_ge(x1T_ready, e.n)
                        if num is None or num >= 3:
                            act.wait_ge(x1_stored[1 - e.parity], 32 * (e.half + e.parity))
                        for c in range(QC):
                            ins = nc.scalar.activation(x1[:, c, :], y[:, c, :], ACT.Identity, bias=shift[:, c:c + 1],
                                                       scale=rstd[:, c:c + 1])
                        ins.then_inc(x1_done, 1)
                    if d:
                        act.wait_ge(st_ready, H * d.n + k + 1)
                        if num is None or num >= 2 or k >= RING:
                            act.wait_ge(pv_ready, QUADS * d.n + k // 4 - 1)
                        nc.scalar.activation(probs[:, k % RING], bank(BD[k % 2], a=QC), ACT.Exp,
                                             scale=SCALE).then_inc(exp_done, 1)
                    if k == 9 and f:
                        act.wait_ge(dmx_done, f.n + 1)
                        act.wait_ge(item_done, 2 * f.n)
                        nc.scalar.activation(ex[:, :, :], dmx[:, :, :], ACT.Exp).then_inc(ex_done, 1)

            pipeline(act, step)

        @block.vector
        def _(dve):
            nc.vector.memset(ones_f[:, :], 1.0).then_inc(ones_ready, 1)
            nc.vector.memset(stack[0][0:ROW_M, :, 1, :].bitcast(F32), 0.0).then_inc(keys_cleared[0], 1)
            for w in range(4):
                dve.wait_ge(wT_hi_done, w + 1)
                for c in range(DK):
                    ins = nc.vector.tensor_tensor(by_feature(wT_lo, w, c), from_bank(w, c),
                                                  by_feature(wT_hi, w, c).bitcast(F32), ALU.subtract)
                ins.then_inc(wT_lo_done, 1)
            dve.wait_ge(gate_done, 1)
            nc.vector.tensor_tensor(gate_lo[:, :, :, :], gate_raw[:, :, :].unsqueeze(2).to_broadcast([P, DK, GW // NE, NE]),
                                    gate_hi[:, :, :, :].bitcast(F32), ALU.subtract).then_inc(gate_done, 1)
            for i in range(2):
                nc.vector.memset(v_aug[i][:, :, :, R:2 * R], 1.0).then_inc(v_ones, 1)
            dve.wait_ge(consts_ready, POOL_CONSTS)

            def mT_rest(b, half):
                dve.wait_ge(mT_hi_done[half], b.n + 1)
                nc.vector.tensor_tensor(mT_lo[half][:, :], banks[(BA, BB)[half]][0:HH, 0:S], mT_hi[half][:, :].bitcast(F32),
                                        ALU.subtract).then_inc(mT_lo_done[half], 1)

            def step(s, num):
                a, b, d, e, f, g = (stage(s, num, lag) for lag in (-1, 0, 1, 2, 3, 4))
                for k in range(H):
                    if k == 5 and f:
                        logits(f)
                    if k == 1 and a:
                        dve.wait_ge(xT_copied, a.n + 1)
                        if num is None or num >= 1:
                            dve.wait_ge(v_ready, a.n - 1)
                        nc.vector.tensor_copy(xT_hi[a.parity][:, :, :], xT_f[:, :, :]).then_inc(xT_hi_done, 1)
                    if k == 2 and f:
                        dve.wait_ge(x1T_copied, f.n + 1)
                        dve.wait_ge(lg_ready, f.n)
                        nc.vector.tensor_copy(x1T_hi[:, :, :], x1T_f[:, :, :]).then_inc(x1T_hi_done, 1)
                    if k == 2 and d:
                        mT_rest(d, 1)
                    if k == 3 and g:
                        entries(g, num)
                    if k == 5 and e:
                        dve.wait_ge(uT_ready, e.n + 1)
                        dve.wait_ge(attn_done, e.n)
                        for c in range(QC):
                            sums = banks[(BA, BB)[c]][:, :].rearrange("p (u r) -> p u r", r=32)[:, :, R]
                            ins = nc.vector.reciprocal(rec[:, c, :], sums)
                        ins.then_inc(rec_done, 1)
                        dve.wait_ge(rec_done, e.n + 1)
                        dve.wait_ge(aT_ready, e.n)
                        for c in range(QC):
                            dst = attn[:, c, :].rearrange("p (g h r) -> p h g r", g=G, r=R)
                            src = banks[(BA, BB)[c]][:, :].rearrange("p (h g r) -> p h g r", g=G, r=32)[:, :, :, 0:R]
                            rc = rec[:, c, :].rearrange("p (h g) -> p h g", g=G).unsqueeze(3).to_broadcast([P, HH, G, R])
                            ins = nc.vector.tensor_tensor(dst, src, rc, ALU.mult)
                        ins.then_inc(attn_done, 1)
                    if k == 6 and f:
                        largest(f)
                    if k == 10 and b:
                        mT_rest(b, 0)
                    if k in (7, 10) and a:
                        w = (7, 10).index(k)
                        dve.wait_ge(qk_hi_done[w], a.n + 1)
                        nc.vector.tensor_tensor(qk[a.parity][:, w, :, w, :], bank(BC, a=G),
                                                qk[a.parity][:, 1 - w, :, w, :].bitcast(F32), ALU.subtract).then_inc(qk_lo_done[w], 1)
                    if k == 7 and f:
                        experts_of_largest(f)
                    if k == 9 and e:
                        dve.wait_ge(aT_hi_done, e.n + 1)
                        nc.vector.tensor_tensor(aT_lo[:, :, :], bank(BB, a=DK), aT_hi[:, :, :].bitcast(F32),
                                                ALU.subtract).then_inc(aT_lo_done, 1)
                    if k == 9 and f:
                        one_hot(f)
                    if k == 10 and f:
                        chosen(f)
                    if k == 11 and f:
                        count_first_tile(f)
                    if k == 11 and e:
                        dve.wait_ge(o_ready, e.n + 1)
                        dve.wait_ge(xres_loaded[e.parity], 16 * (e.half + 1))
                        dve.wait_ge(x1_done, e.n)
                        nc.vector.tensor_tensor(y[:, :, :], bank(BA, a=QC), xres[e.parity][:, :, :], ALU.add).then_inc(y_done, 1)
                    if k == 11 and f:
                        count_second_tile(f)
                    if k == 12 and e:
                        dve.wait_ge(y_done, e.n + 1)
                        for c in range(QC):
                            nc.vector.bn_stats(stats[:, c, :], y[:, c, :]).then_inc(stats_done, 1)
                    if k == 13 and f:
                        slots(f)
                    if b:
                        dve.wait_ge(s_ready, H * b.n + k + 1)
                        if k % HH == 0:
                            dve.wait_ge(mT_ready[k // HH], b.n)
                        nc.vector.tensor_reduce(negm[:, :, k], bank(BQ[k % 2], a=QC), X, ALU.max,
                                                negate=True).then_inc(max_done, 1)
                    if k == 12 and e:
                        wait_apart(dve, dve_passed, (stats_done, QC * e.n + QC), (shift_done, e.n))
                        for c in range(QC):
                            ins = nc.vector.bn_aggr(mv[:, c, :], stats[:, c, :])
                        ins.then_inc(mv_done, 1)
                    if k == 13 and f:
                        slots_with_capacity(f)
                if num == first:
                    nc.vector.memset(stack[1][0:ROW_M, :, 1, :].bitcast(F32), 0.0).then_inc(keys_cleared[1], 1)

            def logits(f):
                dve.wait_ge(lg_ready, f.n + 1)
                dve.wait_ge(ix_done, f.n)
                nc.vector.tensor_copy(lg[:, :, :], banks[BC][:, 0:QC * GW].rearrange("p (c e) -> p c e", c=QC)[:, :, 0:NE]).then_inc(lg_done, 1)

            def largest(f):
                wait_apart(dve, dve_passed, (lg_done, f.n + 1), (dmx_done, f.n))
                for c in range(QC):
                    ins = nc.vector.max(mx[:, c, :], lg[:, c, :])
                ins.then_inc(mx_done, 1)

            def experts_of_largest(f):
                wait_apart(dve, dve_passed, (mx_done, f.n + 1), (ixf_done, f.n))
                for c in range(QC):
                    ins = nc.vector.max_index(ix[:, c, :], mx[:, c, :], lg[:, c, :])
                ins.then_inc(ix_done, 1)
                dve.wait_ge(ex_done, f.n)
                nc.vector.tensor_tensor(dmx[:, :, :], mx[:, :, :], mx[:, :, 0:1].to_broadcast([P, QC, NE]),
                                        ALU.subtract).then_inc(dmx_done, 1)
                dve.wait_ge(ix_done, f.n + 1)
                dve.wait_ge(hot_done, f.n)
                nc.vector.tensor_copy(ixf[:, :, :], ix[:, :, 0:TOPK]).then_inc(ixf_done, 1)

            def one_hot(f):
                dve.wait_ge(ixf_done, f.n + 1)
                dve.wait_ge(pick_done, QC * f.n)
                for c in range(QC):
                    ins = nc.vector.tensor_tensor(hot[:, c], iota_e[:, :].unsqueeze(1).to_broadcast([P, TOPK, NE]),
                                                  ixf[:, c, :].unsqueeze(2).to_broadcast([P, TOPK, NE]), ALU.is_equal)
                ins.then_inc(hot_done, 1)

            def chosen(f):
                dve.wait_ge(hot_done, f.n + 1)
                dve.wait_ge(pos_ready, f.n)
                dve.wait_ge(seen_done, f.n)
                nc.vector.tensor_tensor(mask[:, :, :], hot[:, :, 0, :], hot[:, :, 1, :], ALU.add).then_inc(mask_done, 1)

            def count_first_tile(f):
                dve.wait_ge(mask_done, f.n + 1)
                nc.vector.tensor_tensor(seen_t[:, :], seen[f.parity][:, :], mask[:, 0, :], ALU.add).then_inc(seen_mid, 1)

            def count_second_tile(f):
                dve.wait_ge(seen_mid, f.n + 1)
                nc.vector.tensor_tensor(seen[1 - f.parity][:, :], seen_t[:, :], mask[:, 1, :], ALU.add).then_inc(seen_done, 1)

            def slots(f):
                pos = banks[BC][:, 0:QC * NE].rearrange("p (c e) -> p c e", c=QC)
                dve.wait_ge(pos_ready, f.n + 1)
                dve.wait_ge(slotb_done, f.n)
                nc.vector.tensor_scalar(over[:, :, :], pos, float(CAP), float(NE * CAP), ALU.is_ge, ALU.mult).then_inc(over_done, 1)
                nc.vector.tensor_tensor(slot[:, :, :], pos, slot0[:, :].unsqueeze(1).to_broadcast([P, QC, NE]), ALU.add).then_inc(slot_done, 1)

            def slots_with_capacity(f):
                dve.wait_ge(over_done, f.n + 1)
                dve.wait_ge(slot_done, f.n + 1)
                dve.wait_ge(pick_done, QC * f.n)
                nc.vector.tensor_tensor(slot_b[:, :, :], slot[:, :, :], over[:, :, :], ALU.add).then_inc(slotb_done, 1)

            def entries(g, num):
                it = item[g.parity][:, :, :].rearrange("p (c k) w -> p c k w", c=QC)
                dve.wait_ge(ex_done, g.n + 1)
                nc.vector.tensor_reduce(zsum[:, :], ex[:, :, :], X, ALU.add).then_inc(zsum_done, 1)
                dve.wait_ge(slotb_done, g.n + 1)
                dve.wait_ge(destf_done, g.n)
                for c in range(QC):
                    nc.vector.tensor_tensor(pick[:, c], hot[:, c], slot_b[:, c, :].unsqueeze(1).to_broadcast([P, TOPK, NE]),
                                            ALU.mult).then_inc(pick_done, 1)
                dve.wait_ge(zsum_done, g.n + 1)
                nc.vector.tensor_scalar(den[:, :], zsum[:, :], 1e-8, 1.0, ALU.mult, ALU.add).then_inc(den_done, 1)
                dve.wait_ge(pick_done, QC * g.n + QC)
                dve.wait_ge(dest_done, g.n)
                nc.vector.tensor_reduce(dest_f[:, :, :], pick[:, :, :, :], X, ALU.add).then_inc(destf_done, 1)
                dve.wait_ge(den_done, g.n + 1)
                nc.vector.tensor_tensor(den2[:, :], den[:, :], ex[:, :, 1], ALU.add).then_inc(den2_done, 1)
                dve.wait_ge(den2_done, g.n + 1)
                nc.vector.reciprocal(den[:, :], den2[:, :]).then_inc(inv_done, 1)
                if num is None or num >= 6:
                    dve.wait_ge(listed[g.parity], 16 * QC * TOPK * g.half)
                dve.wait_ge(tok_done, g.n + 1)
                nc.vector.tensor_copy(it[:, :, :, 0], tok[:, :].unsqueeze(2).to_broadcast([P, QC, TOPK])).then_inc(item_done, 1)
                dve.wait_ge(destf_done, g.n + 1)
                nc.vector.tensor_copy(dest[g.parity][:, :].rearrange("p (c k) -> p c k", c=QC), dest_f[:, :, :]).then_inc(dest_done, 1)
                dve.wait_ge(inv_done, g.n + 1)
                nc.vector.tensor_tensor(it[:, :, :, 1].bitcast(F32), ex[:, :, 0:TOPK], den[:, :].unsqueeze(2).to_broadcast([P, QC, TOPK]),
                                        ALU.mult).then_inc(item_done, 1)
                dve.wait_ge(item_done, 2 * g.n + 1)
                nc.vector.tensor_scalar(tok[:, :], tok[:, :], float(S), None, ALU.add).then_inc(tok_done, 1)

            pipeline(dve, step)

        @block.tensor
        def _(pe):
            pe.wait_ge(ident_ready, 1)
            for w in range(4):
                pe.wait_ge(w_loaded[w], 16)
                for c in range(DK):
                    for r in range(QC):
                        ins = nc.tensor.transpose(banks[4 + w][:, c * D + r * P:c * D + r * P + P],
                                                  w_raw[:, w, r, c * P:c * P + P], ident[:, :])
                ins.then_inc(wT_ready, 1)
            pe.wait_ge(b1_loaded, 16)
            nc.tensor.transpose(banks[0][:, 0:NE * FT], b1_raw[:, :], ident[0:NE * FT, 0:NE * FT]).then_inc(b1T_ready, 1)
            pe.wait_ge(wT_hi_done, 4)
            pe.wait_ge(wT_lo_done, 4)

            def product(out, pairs):
                for n, (l, r) in enumerate(pairs):
                    ins = nc.tensor.matmul(out, l, r, start=(n == 0), stop=(n == len(pairs) - 1))
                return ins

            def split_pairs(l_hi, l_lo, r_hi, r_lo):
                return [p for c in range(DK) for p in ((l_hi(c), r_hi(c)), (l_hi(c), r_lo(c)), (l_lo(c), r_hi(c)))]

            def pv(b, t):
                pe.wait_ge(exp_done, H * b.n + 4 * t + 4)
                if t == 0:
                    pe.wait_ge(v_done, b.n + 1)
                    if isinstance(b.n, int) and b.n < 2:
                        pe.wait_ge(v_ones, b.n + 1)
                if t % 2 == 0:
                    pe.wait_ge(u_done, 2 * b.n + t // 2)
                for c in range(QC):
                    for j in range(4):
                        u = 4 * t + j
                        out = banks[BU][32 * j:32 * j + 32, (t % 2) * S:(t % 2) * S + S]
                        ins = nc.tensor.matmul(out, v_aug[b.parity][:, c, u, :], probs[:, u % RING, c, :],
                                               start=(c == 0), stop=(c == QC - 1), tile_position=(0, 32 * j))
                ins.then_inc(pv_ready, 1)

            def mT(b, half):
                pe.wait_ge(max_done, H * b.n + HH * half + HH)
                for c in range(QC):
                    ins = nc.tensor.transpose(banks[(BA, BB)[half]][0:HH, c * P:c * P + P], negm[:, c, HH * half:HH * half + HH], ident[:, :])
                ins.then_inc(mT_ready[half], 1)

            def transpose4(bk, src):
                for c in range(DK):
                    for r in range(QC):
                        ins = nc.tensor.transpose(banks[bk][:, c * S + r * P:c * S + r * P + P], src[:, r, c * P:c * P + P], ident[:, :])
                return ins

            def project(w, a):
                hi, lo = xT_hi[a.parity], xT_lo[a.parity]
                for o in range(G):
                    ins = product(banks[BC][:, o * S:o * S + S], split_pairs(
                        lambda i: wT_hi[:, w, i, o * P:o * P + P], lambda i: wT_lo[:, w, i, o * P:o * P + P],
                        lambda i: hi[:, i, :], lambda i: lo[:, i, :]))
                ins.then_inc(qk_ready[w], 1)

            def by_row_tile(src_hi, src_lo, w):
                for c in range(QC):
                    ins = product(banks[BA][:, c * D:c * D + D], split_pairs(
                        lambda i: src_hi[:, i, c * P:c * P + P], lambda i: src_lo[:, i, c * P:c * P + P],
                        lambda i: wT_hi[:, w, i, :], lambda i: wT_lo[:, w, i, :]))
                return ins

            def step(s, num):
                a, b, d, e, f = (stage(s, num, lag) for lag in (-1, 0, 1, 2, 3))
                for k in range(H):
                    if k == 0 and a:
                        pe.wait_ge(x_loaded[a.parity], 16 * (a.half + 1))
                        pe.wait_ge(qk_lo_done[1], a.n)
                        if num is None or num >= 4:
                            pe.wait_ge(slotb_done, f.n)
                        transpose4(BC, x_sb[a.parity]).then_inc(xT_ready, 1)
                    if k == 1 and f:
                        pe.wait_ge(x1_done, f.n + 1)
                        transpose4(BA, x1).then_inc(x1T_ready, 1)
                    if k == 2 and e:
                        pv(e, QUADS - 1)
                    if k == 1 and d:
                        mT(d, 1)
                    if k == 3 and b:
                        pe.wait_ge(xT_lo_done, b.n + 1)
                        if f:
                            pe.wait_ge(x1T_copied, f.n + 1)
                        else:
                            pe.wait_ge(mT_lo_done[0], b.n)
                        by_row_tile(xT_hi[b.parity], xT_lo[b.parity], 2).then_inc(v_ready, 1)
                    if k == 5 and f:
                        pe.wait_ge(x1T_lo_done, f.n + 1)
                        if num == 3:
                            pe.wait_ge(gate_done, 2)
                        if a:
                            pe.wait_ge(xT_copied, a.n + 1)
                        else:
                            pe.wait_ge(slotb_done, f.n)
                        for c in range(QC):
                            ins = product(banks[BC][:, c * GW:c * GW + GW], split_pairs(
                                lambda i: x1T_hi[:, i, c * P:c * P + P], lambda i: x1T_lo[:, i, c * P:c * P + P],
                                lambda i: gate_hi[:, i, :, :].rearrange("p t e -> p (t e)"),
                                lambda i: gate_lo[:, i, :, :].rearrange("p t e -> p (t e)")))
                        ins.then_inc(lg_ready, 1)
                    if k == 5 and e:
                        pe.wait_ge(u_done, 2 * e.n + 2)
                        if b:
                            pe.wait_ge(v_done, b.n + 1)
                        else:
                            pe.wait_ge(x1T_copied, f.n + 1)
                        if d:
                            pe.wait_ge(mT_lo_done[1], d.n + 1)
                        for c in range(QC):
                            for t in range(QUADS):
                                ins = nc.tensor.transpose(banks[(BA, BB)[c]][:, t * P:t * P + P],
                                                          u_sb[:, t, c * P:c * P + P], ident[:, :])
                        ins.then_inc(uT_ready, 1)
                    if k == 6 and a:
                        pe.wait_ge(xT_lo_done, a.n + 1)
                        if f:
                            pe.wait_ge(lg_done, f.n + 1)
                        project(0, a)
                    if k == 8 and e:
                        pe.wait_ge(attn_done, e.n + 1)
                        transpose4(BB, attn).then_inc(aT_ready, 1)
                    if k == 9 and a:
                        pe.wait_ge(qk_lo_done[0], a.n + 1)
                        project(1, a)
                    if k == 9 and b:
                        if e:
                            pe.wait_ge(attn_done, e.n + 1)
                        else:
                            pe.wait_ge(v_done, b.n + 1)
                        mT(b, 0)
                    if k == 11 and e:
                        pe.wait_ge(aT_lo_done, e.n + 1)
                        if b:
                            pe.wait_ge(mT_lo_done[0], b.n + 1)
                        by_row_tile(aT_hi, aT_lo, 3).then_inc(o_ready, 1)
                    if k == 12 and d:
                        pv(d, 1)
                    if k == 13 and f:
                        pe.wait_ge(seen_done, f.n + 1)
                        if a:
                            pe.wait_ge(qk_lo_done[1], a.n + 1)
                        for c in range(QC):
                            out = banks[BC][:, c * NE:c * NE + NE]
                            nc.tensor.matmul(out, tri[:, :], mask[:, c, :], start=True, stop=False)
                            ins = nc.tensor.matmul(out, ones[:, :], (seen[f.parity], seen_t)[c][:, :], start=False, stop=True)
                        ins.then_inc(pos_ready, 1)
                    if b:
                        if k == 0 and num == 0:
                            pe.wait_ge(b1T_done, 1)
                        if k % HH == 0:
                            pe.wait_ge(stacked[k // HH], 64 * (b.n + 1))
                        if num is None or num >= 1 or k >= 2:
                            pe.wait_ge(max_done, H * b.n + k - 1)
                        for c in range(QC):
                            ins = nc.tensor.matmul(banks[BQ[k % 2]][:, c * S:c * S + S],
                                                   stack[b.parity][0:ROW_M, k, 0, c * P:c * P + P],
                                                   stack[b.parity][0:ROW_M, k, 1, :], start=True, stop=True)
                        ins.then_inc(s_ready, 1)
                    if d:
                        if k == 0 and num in (1, 2):
                            pe.wait_ge(keys_ready[d.parity], (1, 16)[d.parity])
                        if k % HH == 0:
                            pe.wait_ge(shift_in[k // HH], 32 * (d.n + 1))
                        if num is None or num >= 2 or k >= 2:
                            pe.wait_ge(exp_done, H * d.n + k - 1)
                        for c in range(QC):
                            ins = nc.tensor.matmul(banks[BD[k % 2]][:, c * S:c * S + S],
                                                   stack[d.parity][:, k, 1, c * P:c * P + P],
                                                   stack[d.parity][:, k, 0, :], start=True, stop=True)
                        ins.then_inc(st_ready, 1)
                        if k in (6, 14):
                            pv(d, k // 4 - 1)

            pipeline(pe, step)


def experts(nc, g):
    x1_d, acc_d, list_v, w1_d, w2_d, b2_d = g["x1_d"], g["acc_d"], g["list_v"], g["w1_d"], g["w2_d"], g["b2_d"]
    NE, FT, D, DK, FF, C, BLK, NC, QC = g["NE"], g["FT"], g["D"], g["DK"], g["FF"], g["C"], g["BLK"], g["NC"], g["QC"]
    banks, ident, b1T, w1_raw, w2_raw = g["banks"], g["ident"], g["b1T"], g["w1_raw"], g["w2_raw"]
    w1_loaded, w2_loaded = g["w1_loaded"], g["w2_loaded"]
    AHEAD = 3
    PARTS = 2
    PAIRS = FT // 2
    ctx = ExitStack()
    with ctx:
        def sem(name):
            return ctx.enter_context(nc.semaphore(name))

        def sb(name, shape, dt=F32):
            return ctx.enter_context(nc.sbuf_tensor(name, shape, dt))

        w1_hi, w1_lo = sb("w1_hi", [P, DK, FF], F32R), sb("w1_lo", [P, DK, FF], F32R)
        w2_hi, w2_lo = sb("w2_hi", [P, FT, D], F32R), sb("w2_lo", [P, FT, D], F32R)
        b2_all = sb("b2_all", [P, NE, D])
        lists = sb("lists", [P, NE, BLK, 2], I32)
        meta = [sb(f"meta{c}", [P, QC, 2], I32) for c in range(NC)]
        rows = [sb(f"rows{c}", [P, QC, D]) for c in range(NC)]
        g_hi = [sb(f"g_hi{i}", [P, DK, C], F32R) for i in range(3)]
        g_lo = [sb(f"g_lo{i}", [P, DK, C], F32R) for i in range(3)]
        h = [sb(f"h{i}", [P, 2, C]) for i in range(2)]
        h_hi = [sb(f"h_hi{i}", [P, FT, C], F32R) for i in range(3)]
        h_lo = [sb(f"h_lo{i}", [P, FT, C], F32R) for i in range(3)]
        o_b = [sb(f"o_b{i}", [P, QC, D]) for i in range(2)]
        o_w = [sb(f"o_w{c}", [P, QC, D]) for c in range(NC)]

        lists_loaded, b2_loaded = sem("lists_loaded"), g["b2_loaded"]
        w1_hi_done, w1_lo_done, w2_hi_done, w2_lo_done = sem("w1_hi_done"), sem("w1_lo_done"), sem("w2_hi_done"), sem("w2_lo_done")
        pool_passed, act_passed = sem("pool_passed2"), sem("act_passed")
        meta_done = sem("meta_done")
        gathered = [sem(f"gathered{c}") for c in range(NC)]
        gT_ready, g_hi_done, g_lo_done = sem("gT_ready"), sem("g_hi_done"), sem("g_lo_done")
        z_ready, h_done, h_hi_done, h_lo_done = sem("z_ready"), sem("h_done"), sem("h_hi_done"), sem("h_lo_done")
        eo_ready, ob_done, ow_done, added = sem("eo_ready"), sem("ob_done"), sem("ow_done"), sem("added")
        BZ, BO, BT = (0, 1, 2, 3), (4, 5), (6, 7)

        def bank(i, **kw):
            return banks[i][:, :].rearrange("p (a b) -> p a b", **kw)

        block = ctx.enter_context(nc.Block())

        @block.sync
        def _(sp):
            sp.dma_start(lists[:, :, :, :].rearrange("p e j w -> p e (j w)"), list_v).then_inc(lists_loaded, 16)
            sp.dma_start(b2_all[:, :, :].rearrange("p e d -> p (e d)"), b2_d.rearrange("e d -> (e d)").partition_broadcast(P)).then_inc(b2_loaded, 16)
            with sp.Fori(1, NE) as e:
                sp.wait_ge(w1_hi_done, PARTS * e)
                sp.wait_ge(w1_lo_done, PARTS * e)
                sp.dma_start(w1_raw[:, :, :], w1_d[e].rearrange("(c p) f -> p c f", p=P)).then_inc(w1_loaded, 16)
                sp.wait_ge(w2_hi_done, PARTS * e)
                sp.wait_ge(w2_lo_done, PARTS * e)
                sp.dma_start(w2_raw[:, :, :], w2_d[e].rearrange("(f p) d -> p f d", p=P)).then_inc(w2_loaded, 16)
            sp.wait_ge(added, 16 * NE * BLK)

        @block.gpsimd
        def _(pool):
            pool.wait_ge(lists_loaded, 16)

            def gather(e, c):
                n = NC * e + c
                if not (isinstance(e, int) and e == 0):
                    pool.wait_ge(added, 16 * QC * (n - NC + 1))
                nc.gpsimd.tensor_copy(meta[c][:, :, :], lists[:, e, QC * c:QC * c + QC, :]).then_inc(meta_done, 1)
                wait_apart(pool, pool_passed, (meta_done, n + 1))
                for r in range(QC):
                    nc.gpsimd.indirect_dma_start(
                        out=rows[c][:, r, :], out_offset=None, in_=x1_d,
                        in_offset=bass.IndirectOffsetOnAxis(ap=meta[c][:, r, 0:1], axis=0)).then_inc(gathered[c], 16)

            def add_back(e, c):
                n = NC * e + c
                pool.wait_ge(ow_done, QC * (n + 1))
                for r in range(QC):
                    wait_apart(pool, pool_passed, (added, 16 * (QC * n + r)))
                    nc.gpsimd.indirect_dma_start(
                        out=acc_d, out_offset=bass.IndirectOffsetOnAxis(ap=meta[c][:, r, 0:1], axis=0),
                        in_=o_w[c][:, r, :], in_offset=None, compute_op=ALU.add).then_inc(added, 16)

            def expert(e, last):
                for c in range(NC):
                    if c + AHEAD < NC:
                        gather(e, c + AHEAD)
                    elif not last:
                        gather(e + 1, c + AHEAD - NC)
                    add_back(e, c)

            for c in range(AHEAD):
                gather(0, c)
            expert(0, False)
            with pool.Fori(1, NE - 1) as e:
                expert(e, False)
            expert(NE - 1, True)

        @block.scalar
        def _(act):
            def split_w1(e):
                act.wait_ge(w1_loaded, 16 * (e + 1))
                act.wait_ge(z_ready, PAIRS * NC * e)
                for i in range(PARTS):
                    f = slice(i * (FF // PARTS), (i + 1) * (FF // PARTS))
                    nc.scalar.activation(w1_hi[:, :, f], w1_raw[:, :, f], ACT.Copy).then_inc(w1_hi_done, 1)

            def split_w2(e):
                act.wait_ge(w2_loaded, 16 * (e + 1))
                act.wait_ge(eo_ready, NC * e)
                for i in range(PARTS):
                    f = slice(i * (FT // PARTS), (i + 1) * (FT // PARTS))
                    nc.scalar.activation(w2_hi[:, f, :], w2_raw[:, f, :], ACT.Copy).then_inc(w2_hi_done, 1)

            def rows_hi(e, c):
                n = NC * e + c
                act.wait_ge(gT_ready, n + 1)
                if not (isinstance(n, int) and n < 3):
                    act.wait_ge(z_ready, PAIRS * (n - 1))
                nc.scalar.activation(g_hi[HBUF[c]][:, :, :], bank(BT[c % 2], a=DK), ACT.Copy).then_inc(g_hi_done, 1)

            def relu(e, c):
                for m in range(PAIRS):
                    n = PAIRS * (NC * e + c) + m
                    used = () if isinstance(n, int) and n < 2 else ((h_hi_done, n - 1), (h_lo_done, n - 1))
                    wait_apart(act, act_passed, (z_ready, n + 1), *used)
                    for i in range(2):
                        col = FT * e + 2 * m + i
                        ins = nc.scalar.activation(h[m % 2][:, i, :], bank(BZ[m], a=2)[:, i, :], ACT.Relu,
                                                   bias=b1T[:, col:col + 1] if isinstance(col, int) else b1T[:, bass.ds(col, 1)])
                    ins.then_inc(h_done, 1)

            def weigh(e, c):
                n = NC * e + c
                act.wait_ge(ob_done, n + 1)
                for r in range(QC):
                    nc.scalar.activation(o_w[c][:, r, :], o_b[c % 2][:, r, :], ACT.Copy,
                                         scale=meta[c][:, r, 1:2].bitcast(F32)).then_inc(ow_done, 1)

            expert_order(act, NE, NC, rows_hi, relu, weigh, split_w1, split_w2)

        @block.vector
        def _(dve):
            def split_w1(e):
                for i in range(PARTS):
                    f = slice(i * (FF // PARTS), (i + 1) * (FF // PARTS))
                    dve.wait_ge(w1_hi_done, PARTS * e + i + 1)
                    nc.vector.tensor_tensor(w1_lo[:, :, f], w1_raw[:, :, f], w1_hi[:, :, f].bitcast(F32),
                                            ALU.subtract).then_inc(w1_lo_done, 1)

            def split_w2(e):
                for i in range(PARTS):
                    f = slice(i * (FT // PARTS), (i + 1) * (FT // PARTS))
                    dve.wait_ge(w2_hi_done, PARTS * e + i + 1)
                    nc.vector.tensor_tensor(w2_lo[:, f, :], w2_raw[:, f, :], w2_hi[:, f, :].bitcast(F32),
                                            ALU.subtract).then_inc(w2_lo_done, 1)

            def rows_lo(e, c):
                dve.wait_ge(g_hi_done, NC * e + c + 1)
                nc.vector.tensor_tensor(g_lo[HBUF[c]][:, :, :], bank(BT[c % 2], a=DK), g_hi[HBUF[c]][:, :, :].bitcast(F32),
                                        ALU.subtract).then_inc(g_lo_done, 1)

            def halves(e, c):
                for m in range(PAIRS):
                    n = PAIRS * (NC * e + c) + m
                    dve.wait_ge(h_done, n + 1)
                    if m == 0 and not (isinstance(e, int) and e == 0 and c < 3):
                        dve.wait_ge(eo_ready, NC * e + c - 1)
                    t = slice(2 * m, 2 * m + 2)
                    nc.vector.tensor_copy(h_hi[HBUF[c]][:, t, :], h[m % 2][:, :, :]).then_inc(h_hi_done, 1)
                    dve.wait_ge(h_hi_done, n + 1)
                    nc.vector.tensor_tensor(h_lo[HBUF[c]][:, t, :], h[m % 2][:, :, :], h_hi[HBUF[c]][:, t, :].bitcast(F32),
                                            ALU.subtract).then_inc(h_lo_done, 1)

            def bias(e, c):
                n = NC * e + c
                dve.wait_ge(eo_ready, n + 1)
                if not (isinstance(n, int) and n < 3):
                    dve.wait_ge(ow_done, QC * (n - (1 if c != 0 else 0)))
                if isinstance(n, int) and n == 0:
                    dve.wait_ge(b2_loaded, 16)
                for r in range(QC):
                    ins = nc.vector.tensor_tensor(o_b[c % 2][:, r, :], bank(BO[c % 2], a=QC)[:, r, :], b2_all[:, e, :], ALU.add)
                ins.then_inc(ob_done, 1)

            expert_order(dve, NE, NC, rows_lo, halves, bias, split_w1, split_w2)

        @block.tensor
        def _(pe):
            def transposes(e, c):
                n = NC * e + c
                pe.wait_ge(gathered[c], 16 * QC * (e + 1))
                if not (isinstance(n, int) and n < 2):
                    pe.wait_ge(g_lo_done, n if c == 0 else n - 1)
                for i in range(DK):
                    for r in range(QC):
                        ins = nc.tensor.transpose(banks[BT[c % 2]][:, i * C + r * P:i * C + r * P + P],
                                                  rows[c][:, r, i * P:i * P + P], ident[:, :])
                ins.then_inc(gT_ready, 1)

            def layer1(e, c):
                n = NC * e + c
                pe.wait_ge(g_lo_done, n + 1)
                G_hi, G_lo = g_hi[HBUF[c]], g_lo[HBUF[c]]
                for m in range(PAIRS):
                    if c == 0 and m % (PAIRS // PARTS) == 0:
                        pe.wait_ge(w1_lo_done, PARTS * e + m // (PAIRS // PARTS) + 1)
                    if not (isinstance(n, int) and n == 0):
                        pe.wait_ge(h_done, PAIRS * (n - 1) + m + 1)
                    for i in range(2):
                        f = slice((2 * m + i) * P, (2 * m + i + 1) * P)
                        out = bank(BZ[m], a=2)[:, i, :]
                        for k in range(DK):
                            nc.tensor.matmul(out, w1_hi[:, k, f], G_hi[:, k, :], start=(k == 0), stop=False)
                            nc.tensor.matmul(out, w1_hi[:, k, f], G_lo[:, k, :], start=False, stop=False)
                            ins = nc.tensor.matmul(out, w1_lo[:, k, f], G_hi[:, k, :], start=False, stop=(k == DK - 1))
                    ins.then_inc(z_ready, 1)

            def layer2(e, c):
                n = NC * e + c
                if not (isinstance(n, int) and n < 2):
                    pe.wait_ge(ob_done, n if c == 0 else n - 1)
                H_hi, H_lo = h_hi[HBUF[c]], h_lo[HBUF[c]]
                for r in range(QC):
                    rs = slice(r * P, r * P + P)
                    out = bank(BO[c % 2], a=QC)[:, r, :]
                    for f in range(FT):
                        if r == 0 and c == 0 and f % (FT // PARTS) == 0:
                            pe.wait_ge(w2_lo_done, PARTS * e + f // (FT // PARTS) + 1)
                        if r == 0 and f % 2 == 0:
                            pe.wait_ge(h_lo_done, PAIRS * n + f // 2 + 1)
                        nc.tensor.matmul(out, H_hi[:, f, rs], w2_hi[:, f, :], start=(f == 0), stop=False)
                        nc.tensor.matmul(out, H_hi[:, f, rs], w2_lo[:, f, :], start=False, stop=False)
                        ins = nc.tensor.matmul(out, H_lo[:, f, rs], w2_hi[:, f, :], start=False, stop=(f == FT - 1))
                ins.then_inc(eo_ready, 1)

            expert_order(pe, NE, NC, transposes, layer1, layer2, None, None)


def expert_order(engine, NE, NC, take_in, layer1, layer2, split_w1, split_w2):
    def split(fn, e):
        if fn:
            fn(e)

    def body(e, last):
        for c in range(NC):
            if c + 2 < NC:
                take_in(e, c + 2)
            elif not last:
                take_in(e + 1, c + 2 - NC)
            if c + 1 < NC:
                layer1(e, c + 1)
            elif not last:
                layer1(e + 1, 0)
            if c + 1 == NC - 1 and not last:
                split(split_w1, e + 1)
            layer2(e, c)
        if not last:
            split(split_w2, e + 1)

    split(split_w1, 0)
    split(split_w2, 0)
    take_in(0, 0)
    take_in(0, 1)
    layer1(0, 0)
    body(0, False)
    with engine.Fori(1, NE - 1) as e:
        body(e, False)
    body(NE - 1, True)


def last_norm(nc, g):
    acc_d, out_d, T, D = g["acc_d"], g["out_d"], g["T"], g["D"]
    GROUP = 4
    NG = T // P // GROUP
    acc_v = acc_d[0:T, :].rearrange("(g t p) d -> g p t d", p=P, t=GROUP)
    out_v = out_d.rearrange("b s d -> (b s) d").rearrange("(g t p) d -> g p t d", p=P, t=GROUP)
    ctx = ExitStack()
    with ctx:
        def sem(name):
            return ctx.enter_context(nc.semaphore(name))

        def sb(name, shape, dt=F32):
            return ctx.enter_context(nc.sbuf_tensor(name, shape, dt))

        a = sb("acc_sb", [P, NG, GROUP, D])
        o = sb("out_sb", [P, NG, GROUP, D])
        stats = sb("stats2", [P, NG, GROUP, 6])
        mv = sb("mv2", [P, NG, GROUP, 2])
        minus_half = sb("minus_half", [P, GROUP])
        veps = sb("veps2", [P, NG, GROUP])
        nmean = sb("nmean2", [P, NG, GROUP])
        rstd = sb("rstd2", [P, NG, GROUP])
        shift = sb("shift2", [P, NG, GROUP])
        loaded = [sem(f"acc_loaded{i}") for i in range(NG)]
        stats_done, mv_done, veps_done, nmean_done, rstd_done, shift_done, o_done, stored = (sem(n) for n in (
            "stats2_done", "mv2_done", "veps2_done", "nmean2_done", "rstd2_done", "shift2_done", "out_done", "out_stored"))
        minus_half_ready = sem("minus_half_ready")
        block = ctx.enter_context(nc.Block())

        @block.sync
        def _(sp):
            for i in range(NG):
                sp.dma_start(a[:, i], acc_v[i]).then_inc(loaded[i], 16)
            for i in range(NG):
                sp.wait_ge(o_done, GROUP * (i + 1))
                sp.dma_start(out_v[i], o[:, i]).then_inc(stored, 16)
            sp.wait_ge(stored, 16 * NG)

        @block.vector
        def _(dve):
            for i in range(NG):
                dve.wait_ge(loaded[i], 16)
                for t in range(GROUP):
                    nc.vector.bn_stats(stats[:, i, t, :], a[:, i, t, :]).then_inc(stats_done, 1)
                for t in range(GROUP):
                    dve.wait_ge(stats_done, GROUP * i + t + 1)
                    ins = nc.vector.bn_aggr(mv[:, i, t, :], stats[:, i, t, :])
                ins.then_inc(mv_done, 1)

        @block.gpsimd
        def _(pool):
            nc.gpsimd.memset(minus_half[:, :], -0.5).then_inc(minus_half_ready, 1)
            pool.wait_ge(minus_half_ready, 1)
            for i in range(NG):
                pool.wait_ge(mv_done, i + 1)
                nc.gpsimd.tensor_scalar(veps[:, i, :], mv[:, i, :, 1], EPS, None, ALU.add).then_inc(veps_done, 1)
                nc.gpsimd.tensor_scalar(nmean[:, i, :], mv[:, i, :, 0], -1.0, None, ALU.mult).then_inc(nmean_done, 1)
                pool.wait_ge(veps_done, i + 1)
                nc.gpsimd.tensor_tensor(rstd[:, i, :], veps[:, i, :], minus_half[:, :], ALU.pow).then_inc(rstd_done, 1)
                pool.wait_ge(nmean_done, i + 1)
                pool.wait_ge(rstd_done, i + 1)
                nc.gpsimd.tensor_tensor(shift[:, i, :], nmean[:, i, :], rstd[:, i, :], ALU.mult).then_inc(shift_done, 1)

        @block.scalar
        def _(act):
            for i in range(NG):
                act.wait_ge(shift_done, i + 1)
                for t in range(GROUP):
                    nc.scalar.activation(o[:, i, t, :], a[:, i, t, :], ACT.Identity, bias=shift[:, i, t:t + 1],
                                         scale=rstd[:, i, t:t + 1]).then_inc(o_done, 1)


_INS = ['L0_attn_x', 'L0_attn_w_q', 'L0_attn_w_k', 'L0_attn_w_v', 'L0_attn_w_o', 'L0_ffn_gating_w',
        'L0_ffn_w1', 'L0_ffn_b1', 'L0_ffn_w2', 'L0_ffn_b2']


def kernel(**inputs):
    import numpy as _np
    import concourse.bacc as _bacc
    from concourse import mybir as _mybir
    from concourse.bass_utils import run_bass_kernel_spmd as _run

    nc = _bacc.Bacc("TRN2", target_bir_lowering=False, num_devices=1)
    arrays, args = {}, []
    for name in _INS:
        a = _np.ascontiguousarray(inputs[name])
        arrays[f"in_{name}"] = a
        args.append(nc.dram_tensor(f"in_{name}", a.shape, _mybir.dt.from_np(a.dtype), kind="ExternalInput").ap())
    shape = inputs['L0_attn_x'].shape
    args.append(nc.dram_tensor("out_0", shape, _mybir.dt.float32, kind="ExternalOutput").ap())
    build(nc, *args)
    r = _run(nc, [arrays], core_ids=[0])
    return r.results[0]["out_0"]
```
